# Optimizing a Trainium2 kernel written in Bass

```python
import numpy as np
import jax
import jax.numpy as jnp

def _softmax(x, axis=-1):
    return jax.nn.softmax(x, axis=axis)

def _gelu(x):
    return jax.nn.gelu(x, approximate=True)

def _silu(x):
    return jax.nn.silu(x)

def _sigmoid(x):
    return jax.nn.sigmoid(x)

def _layernorm(x, axis=-1, eps=1e-05):
    m = jnp.mean(x, axis=axis, keepdims=True)
    v = jnp.var(x, axis=axis, keepdims=True)
    return (x - m) / jnp.sqrt(v + eps)

def _scatter_add(tgt, idx, src, axis=0):
    return tgt.at[idx].add(src)

def _segment_sum(src, seg, n):
    return jax.ops.segment_sum(src, seg, n)
kernel_name = 'mk_xattn_ffn_d1_seqx_r4_f3a2e8'

def setup_inputs(seed: int=0):
    np.random.seed(seed)
    _w = jnp.asarray

    def _rec_inputs():
        import jax
        import jax.numpy as jnp
        _rk = jax.random.key(seed)
        x = 7.22e-05 + 1 * jax.random.normal(jax.random.fold_in(_rk, 1), (8, 256, 256), jnp.float32)
        _lenS = 256 - jax.random.randint(jax.random.fold_in(_rk, 7), (8,), 0, max(1, 256 // 4) + 1, jnp.int32)
        _lenS2 = 256 - jax.random.randint(jax.random.fold_in(_rk, 8), (8,), 0, max(1, 256 // 4) + 1, jnp.int32)
        _ctx_1024P = jax.random.normal(jax.random.fold_in(_rk, 11), (8, 16, 256), jnp.float32)
        _ctx_1024c = jax.random.dirichlet(jax.random.fold_in(_rk, 511), 0.3 * jnp.ones((16,), jnp.float32), (8, 256))
        _ctx_1024t = jnp.einsum('bsk,bkd->bsd', _ctx_1024c, _ctx_1024P)
        _ctx_1024t = _ctx_1024t * jax.lax.rsqrt(jnp.mean(jnp.square(_ctx_1024t)) + 1e-12) * 0.953939
        ctx_1024 = 4.13588e-05 + 0.999923 * (_ctx_1024t + 0.3 * jax.random.normal(jax.random.fold_in(_rk, 611), (8, 256, 256), jnp.float32))
        _validS = jnp.arange(256)[None, :] < _lenS[:, None]
        _validS2 = jnp.arange(256)[None, :] < _lenS2[:, None]
        _causal = jnp.tril(jnp.ones((256, 256), dtype=bool))
        mask_Bx1x1xS2_fk0 = jnp.where(jnp.broadcast_to(_validS2[:, None, None, :], (8, 1, 1, 256)), 0.0, 1.0).astype(jnp.float32)
        return (x, ctx_1024, mask_Bx1x1xS2_fk0)
    x, ctx_1024, mask_Bx1x1xS2_fk0 = _rec_inputs()

    def _L0_xattn_setup():
        import jax, jax.numpy as jnp
        import numpy as np
        NUM_HEADS = 16
        MODEL_DIM = 256
        DEPTH = MODEL_DIM // NUM_HEADS

        def _split_heads(x):
            B, S, _ = x.shape
            return x.reshape(B, S, NUM_HEADS, DEPTH).transpose(0, 2, 1, 3)
        key = jax.random.key(seed)
        ks = jax.random.split(key, 12)
        B, S, D = (4, 512, MODEL_DIM)
        scale = 1.0 / np.sqrt(D)
        inp = {'query': jax.random.normal(ks[0], (B, S, D), jnp.float32), 'key': jax.random.normal(ks[1], (B, S, D), jnp.float32), 'value': jax.random.normal(ks[2], (B, S, D), jnp.float32), 'mask': jax.random.randint(ks[3], (B, 1, 1, S), 0, 2).astype(jnp.float32), 'Wq': jax.random.normal(ks[4], (D, D), jnp.float32) * scale, 'bq': jnp.zeros((D,), jnp.float32), 'Wk': jax.random.normal(ks[5], (D, D), jnp.float32) * scale, 'bk': jnp.zeros((D,), jnp.float32), 'Wv': jax.random.normal(ks[6], (D, D), jnp.float32) * scale, 'bv': jnp.zeros((D,), jnp.float32), 'Wo': jax.random.normal(ks[7], (D, D), jnp.float32) * scale, 'bo': jnp.zeros((D,), jnp.float32)}
        return inp
    _L0_xattn_all = _L0_xattn_setup()
    _L0_xattn_in = {k: v for k, v in _L0_xattn_all.items() if k in ('Wq', 'bq', 'Wk', 'bk', 'Wv', 'bv', 'Wo', 'bo')}
    del _L0_xattn_all

    def _L0_ffn_setup():
        import jax, jax.numpy as jnp
        import numpy as np
        N_EMBD = 256
        N_EXP = 8
        TOP_K = 2
        CAPACITY = 1024
        D_FF = 3 * N_EMBD
        key = jax.random.key(seed)
        k1, k2, k3, k4 = jax.random.split(key, 4)
        x = jax.random.normal(k1, (8, 512, N_EMBD), dtype=jnp.float32)
        w_gate = jax.random.normal(k2, (N_EMBD, N_EXP), dtype=jnp.float32) * 0.02
        c_fc = jax.random.normal(k3, (N_EXP, N_EMBD, D_FF), dtype=jnp.float32) * 0.02
        c_proj = jax.random.normal(k4, (N_EXP, D_FF // 2, N_EMBD), dtype=jnp.float32) * 0.02
        return {'x': x, 'w_gate': w_gate, 'c_fc': c_fc, 'c_proj': c_proj}
    _L0_ffn_all = _L0_ffn_setup()
    _L0_ffn_in = {k: v for k, v in _L0_ffn_all.items() if k in ('w_gate', 'c_fc', 'c_proj')}
    del _L0_ffn_all
    return {'x': x, 'ctx_1024': ctx_1024, 'mask_Bx1x1xS2_fk0': mask_Bx1x1xS2_fk0, 'L0_xattn_Wq': _L0_xattn_in['Wq'], 'L0_xattn_bq': _L0_xattn_in['bq'], 'L0_xattn_Wk': _L0_xattn_in['Wk'], 'L0_xattn_bk': _L0_xattn_in['bk'], 'L0_xattn_Wv': _L0_xattn_in['Wv'], 'L0_xattn_bv': _L0_xattn_in['bv'], 'L0_xattn_Wo': _L0_xattn_in['Wo'], 'L0_xattn_bo': _L0_xattn_in['bo'], 'L0_ffn_w_gate': _L0_ffn_in['w_gate'], 'L0_ffn_c_fc': _L0_ffn_in['c_fc'], 'L0_ffn_c_proj': _L0_ffn_in['c_proj']}

def reference(x, ctx_1024, mask_Bx1x1xS2_fk0, L0_xattn_Wq, L0_xattn_bq, L0_xattn_Wk, L0_xattn_bk, L0_xattn_Wv, L0_xattn_bv, L0_xattn_Wo, L0_xattn_bo, L0_ffn_w_gate, L0_ffn_c_fc, L0_ffn_c_proj):
    import jax
    import jax.numpy as jnp

    def _L0_xattn_ref(query, key, value, mask, Wq, bq, Wk, bk, Wv, bv, Wo, bo):
        import jax, jax.numpy as jnp
        import numpy as np
        NUM_HEADS = 16
        MODEL_DIM = 256
        DEPTH = MODEL_DIM // NUM_HEADS

        def _split_heads(x):
            B, S, _ = x.shape
            return x.reshape(B, S, NUM_HEADS, DEPTH).transpose(0, 2, 1, 3)
        q = _split_heads(query @ Wq + bq)
        k = _split_heads(key @ Wk + bk)
        v = _split_heads(value @ Wv + bv)
        logits = jnp.einsum('bhqd,bhkd->bhqk', q, k) / jnp.sqrt(jnp.float32(DEPTH))
        logits = logits + mask * -1000000000.0
        attn = jax.nn.softmax(logits, axis=-1)
        ctx = jnp.einsum('bhqk,bhkd->bhqd', attn, v)
        B, H, Sq, d = ctx.shape
        concat = ctx.transpose(0, 2, 1, 3).reshape(B, Sq, H * d)
        return concat @ Wo + bo

    def _L0_ffn_ref(x, w_gate, c_fc, c_proj):
        import jax, jax.numpy as jnp
        import numpy as np
        N_EMBD = 256
        N_EXP = 8
        TOP_K = 2
        CAPACITY = 1024
        D_FF = 3 * N_EMBD
        B, T, d = x.shape
        N = B * T
        xf = x.reshape(N, d)
        scores = jax.nn.softmax(xf @ w_gate, axis=-1)
        weights, idx = jax.lax.top_k(scores, TOP_K)
        flat_e = idx.reshape(-1)
        tok = jnp.repeat(jnp.arange(N), TOP_K)
        oh = jax.nn.one_hot(flat_e, N_EXP, dtype=jnp.int32)
        pos = (jnp.cumsum(oh, axis=0) * oh).sum(-1) - 1
        valid = pos < CAPACITY
        pos_c = jnp.where(valid, pos, 0)
        vmask = valid.astype(x.dtype)[:, None]
        exp_x = jnp.zeros((N_EXP, CAPACITY, d), x.dtype)
        exp_x = exp_x.at[flat_e, pos_c].add(xf[tok] * vmask)
        h = jnp.einsum('ecd,edf->ecf', exp_x, c_fc)
        a, g = jnp.split(h, 2, axis=-1)
        h = jax.nn.silu(a) * g
        exp_out = jnp.einsum('ecf,efd->ecd', h, c_proj)
        gathered = exp_out[flat_e, pos_c]
        w = weights.reshape(-1)[:, None] * vmask
        out = (gathered * w).reshape(N, TOP_K, d).sum(axis=1)
        return out.reshape(B, T, d)
    x = x + _L0_xattn_ref(_layernorm(x, axis=-1), ctx_1024, ctx_1024, mask_Bx1x1xS2_fk0, L0_xattn_Wq, L0_xattn_bq, L0_xattn_Wk, L0_xattn_bk, L0_xattn_Wv, L0_xattn_bv, L0_xattn_Wo, L0_xattn_bo)
    x = x + _L0_ffn_ref(_layernorm(x, axis=-1), L0_ffn_w_gate, L0_ffn_c_fc, L0_ffn_c_proj)
    return x

_drawn_inputs = setup_inputs


def setup_inputs(seed=0):
    import zlib

    import numpy as np

    out = dict(_drawn_inputs(seed))
    spreads = {'L0_xattn_bq': (0.0, 0.386),
     'L0_xattn_bk': (0.0, 0.8),
     'L0_xattn_bv': (0.0, 0.1),
     'L0_xattn_bo': (0.0, 0.1)}
    factors = {'L0_ffn_w_gate': 8.0, 'L0_ffn_c_fc': 8.0, 'L0_ffn_c_proj': 8.0}
    for name, (base, spread) in spreads.items():
        noise = np.random.default_rng([zlib.crc32(name.encode()), seed]).standard_normal(out[name].shape)
        drawn = base * np.exp(spread * noise) if base else spread * noise
        out[name] = jnp.asarray(drawn.astype(out[name].dtype))
    for name, factor in factors.items():
        out[name] = (out[name] * factor).astype(out[name].dtype)
    return out
```

```python
from contextlib import ExitStack

import numpy as np

import concourse.bass as bass
from concourse import mybir

F32 = mybir.dt.float32
BF16 = mybir.dt.bfloat16
U32 = mybir.dt.uint32
I32 = mybir.dt.int32
ALU = mybir.AluOpType
ACT = mybir.ActivationFunctionType
AX = mybir.AxisListType

P = 128
B, S, D, H = 8, 256, 256, 16
DH = D // H
E, TOPK, CAP = 8, 2, 1024
FF = 384
NT = B * S // P
TB = S // P
KC = D // P
FC = FF // P
UNITS = 16
NPROB = 4
EPS = 1e-5
MASK_BIG = -1e9
RW = D + 2
PAD_TOK = B * S
XROWS = E * CAP + 3 * P
SLOT_LOST = 1 << 17
MAXPAIR = (B * S * TOPK // P + E - 1 + 1) // 2
MAXBLK = 2 * MAXPAIR + 2

LATE = 4
PADS = 15
COPY_ROWS_AT = 10
PEELED = 4

Q_PART = (0, 0, 1, 1, 0, 2)
K_PART = (0, 1, 0, 1, 2, 0)
R_MASK = 6 * DH
R_MAX = R_MASK + 3
R_END = R_MAX + 3


MISC_PLAN = (
    (1, "PF", -2), (2, "NM1", 0), (5, "WO", -1), (7, "V", 1),
    (9, "NM0", 1), (10, "X2", -1), (12, "LG", -1),
)
ITERATIONS = range(-2, B + 1)


PROJECTION = ((0, "CT"), (1, "XT"), (3, "K"), (4, "Q"))


def projected(it):
    if it == -2:
        return ((0, 0), (1, 7))
    return ((it + 2, 0),) if 0 <= it < B - 2 else ()


def projected_at(it, unit, after):
    return [n for n, start in projected(it) if unit == start + after]


def misc_at(it, unit):
    pieces = [(u, kind, it + rel) for u, kind, rel in MISC_PLAN if u == unit and 0 <= it + rel < B]
    pieces += [(start + u, kind, n) for n, start in projected(it) for u, kind in PROJECTION if start + u == unit]
    if it == B and unit == UNITS - 1:
        pieces += [(unit, "PF", B - 1)]
    return [(kind, n) for _, kind, n in sorted(pieces)]


MISC_ORDER = [piece for it in ITERATIONS for u in range(UNITS) for piece in misc_at(it, u)] + [("CNT", 0)]
MISC_NO = {piece: k for k, piece in enumerate(MISC_ORDER)}


def later(t, least):
    return not isinstance(t, int) or t >= least


def program(nc, x, ctx_in, mask, Wq, bq, Wk, bk, Wv, bv, Wo, bo, w_gate, c_fc, c_proj, out):
    x_t = x.rearrange("b (t p) d -> b p t d", p=P)
    c_t = ctx_in.rearrange("b (t p) d -> b p t d", p=P)
    out_rows = out.rearrange("b s d -> (b s) d")
    out_t = out.rearrange("b (t p) d -> b p t d", p=P)

    slots = nc.dram_tensor("slots", (XROWS, RW), F32, kind="Internal").ap()
    kparts_d = [nc.dram_tensor(f"kparts_d{i}", (3, KC, P, S), BF16, kind="Internal").ap() for i in range(2)]
    qparts_d = [nc.dram_tensor(f"qparts_d{i}", (3, KC, P, S), BF16, kind="Internal").ap() for i in range(2)]

    with ExitStack() as es:
        def sb(name, shape, dt=F32):
            return es.enter_context(nc.sbuf_tensor(name, shape, dt))

        def sem(name):
            return es.enter_context(nc.semaphore(name))

        bank = [es.enter_context(nc.psum_tensor(f"bank{i}", [P, 512], F32)) for i in range(8)]
        MXB, STB, AVB, MISC = bank[0:2], bank[2:4], bank[4:6], bank[6:8]

        X = sb("X", [P, NT, D])
        C = sb("C", [P, 3 * TB, D])
        wq = sb("wq", [P, KC, D]); wk = sb("wk", [P, KC, D]); wv = sb("wv", [P, KC, D])
        wo = sb("wo", [P, 2, D])
        wg = sb("wg", [P, KC, E])
        wf = sb("wf", [P, E * KC * 2 * FF])
        QS = wf[:, (E - LATE) * KC * 2 * FF:].bitcast(BF16).rearrange("p (r h s) -> p r h s", r=3, h=H)
        wp = sb("wp", [P, E * FC * D])
        bqc = sb("bqc", [P, KC]); bq4 = sb("bq4", [P, KC]); bkc = sb("bkc", [P, KC])
        bvb = sb("bvb", [P, D]); bob = sb("bob", [P, D])
        ident = sb("ident", [P, P]); identb = sb("identb", [P, P], BF16)
        before = sb("before", [P, P]); ones = sb("ones", [P, P])
        beforeb = sb("beforeb", [P, P], BF16); onesb = sb("onesb", [P, P], BF16)
        mhalf = sb("mhalf", [P, TB])
        iota_i = sb("iota_i", [P, 256], I32)
        expert_no = sb("expert_no", [P, E]); blk_lim = sb("blk_lim", [P, E, E]); tri = sb("tri", [P, E, E])
        blk_no = sb("blk_no", [P, MAXBLK]); pair_lim = sb("pair_lim", [P, MAXBLK // 2])
        tok_no = sb("tok_no", [P, NT], U32)
        pad_row = sb("pad_row", [P, RW])
        mparts = sb("mparts", [B, 3, S], BF16)
        bn1 = sb("bn1", [P, TB, 6]); mv1 = sb("mv1", [P, 2, TB, 2]); rs1 = sb("rs1", [P, 2, TB])
        bn2 = sb("bn2", [P, TB, 6]); mv2 = sb("mv2", [P, 2, TB, 2]); rs2 = sb("rs2", [P, 2, TB])
        XN = sb("XN", [P, 2, TB, D])
        CTt = sb("CTt", [P, 2, KC, S]); XTt = sb("XTt", [P, 2, KC, S])
        KF = sb("KF", [P, 2, KC * S]); QF = sb("QF", [P, 2, KC * S]); SPL = sb("SPL", [P, KC * S])
        KP = sb("KP", [P, 3, KC * S], BF16); QP = sb("QP", [P, 3, KC * S], BF16)
        KS = sb("KS", [P, 3, H, S], BF16)
        VA = sb("VA", [P, 2, TB, H, 32])
        PR = sb("PR", [P, NPROB, 512])
        NEG = sb("NEG", [P, 2, TB, H]); NR = sb("NR", [P, TB, 8]); NR2 = sb("NR2", [P, TB, 8])
        NMS = sb("NMS", [P, 2, TB, 3, 8], BF16); NMT = sb("NMT", [24, 2, S], BF16)
        AVT = sb("AVT", [P, 16, 32])
        RSUM = sb("RSUM", [P, 16]); AVN = sb("AVN", [P, 16, 2, DH])
        ON = sb("ON", [P, 512])
        R = sb("R", [P, 2, TB, TOPK, RW])
        X2T = sb("X2T", [P, KC, S])
        lg = sb("lg", [P, TB, E]); nmx = sb("nmx", [P, TB]); ls = sb("ls", [P, TB, E]); ex = sb("ex", [P, TB, E])
        sm = sb("sm", [P, TB]); rsm = sb("rsm", [P, TB]); sc = sb("sc", [P, TB, E])
        top = sb("top", [P, TB, 8]); topi = sb("topi", [P, TB, 8], U32); topf = sb("topf", [P, TB, TOPK])
        oh = sb("oh", [P, TB, TOPK, E]); sel = sb("sel", [P, 2, TB, E], BF16)
        chosen = sb("chosen", [P, B + 1, TB, E], BF16)
        ohp = sb("ohp", [P, TB, TOPK, E]); pos = sb("pos", [P, TB, TOPK])
        lost = sb("lost", [P, TB, TOPK]); slotf = sb("slotf", [P, TB, TOPK]); slotg = sb("slotg", [P, TB, TOPK])
        slot = sb("slot", [P, 2, TB, TOPK], U32)
        cnt = sb("cnt", [P, E]); cmp8 = sb("cmp8", [P, E, E]); nblk = sb("nblk", [P, E])
        cum8 = sb("cum8", [P, E, E]); incl = sb("incl", [P, E])
        bexp = sb("bexp", [P, MAXBLK]); bex = sb("bex", [P, MAXBLK]); bcl = sb("bcl", [P, MAXBLK])
        btmp = sb("btmp", [P, MAXBLK]); btmp2 = sb("btmp2", [P, MAXBLK])
        pcmp = sb("pcmp", [P, MAXBLK // 2]); pcnt = sb("pcnt", [P, 1])
        table = sb("table", [P, 3, MAXBLK], I32); npairs = sb("npairs", [P, 2], I32)
        GW = sb("GW", [P, 2, 1]); GI0 = sb("GI0", [P, 1], U32); GI1 = sb("GI1", [P, 1], U32)
        GI = (GI0, GI1)
        XG = sb("XG", [P, 2, RW])
        MASKBUF = PR[0:B, 0:3, 0:S]
        maskrow, mres, mres2 = MASKBUF[:, 0, :], MASKBUF[:, 1, :], MASKBUF[:, 2, :]
        le = PR[:, 0, 0:MAXBLK * E].rearrange("p (b e) -> p b e", e=E)
        leb = PR[:, 1, 0:MAXBLK * E].rearrange("p (b e) -> p b e", e=E)
        XTG = XN[:, :, 0, :].rearrange("p u (k t) -> p u k t", k=KC)
        SG, HM = KF[:, :, 0:FF], QF[:, :, 0:FF]
        HT = XTt[:].rearrange("p u c s -> p u (c s)")[:, :, 0:FF].rearrange("p u (c t) -> p u c t", c=FC)
        Y = CTt[:, :, 0, :]

        x_in = [sem(f"x_in{n}") for n in range(B)]
        c_in = [sem(f"c_in{n}") for n in range(B)]
        wkv_in = sem("wkv_in"); wq_in = sem("wq_in"); wrest_in = sem("wrest_in"); mask_in = sem("mask_in")
        slots_padded = sem("slots_padded")
        const_step = sem("const_step")
        dve_const = sem("dve_const")
        dve_step = sem("dve_step")
        qs_ones = sem("qs_ones"); ks_ones = sem("ks_ones"); va_ones = sem("va_ones")
        mask_split = sem("mask_split")
        stats1 = sem("stats1")
        var1_ready = sem("var1_ready"); xn_ready = sem("xn_ready"); xb_ready = sem("xb_ready")
        misc_ready = sem("misc_ready")
        ct_ready = sem("ct_ready"); xt_ready = sem("xt_ready")
        kf_ready = sem("kf_ready"); qf_ready = sem("qf_ready"); v_ready = sem("v_ready")
        kp0_ready = sem("kp0_ready"); qp0_ready = sem("qp0_ready"); krest_ready = sem("krest_ready"); qrest_ready = sem("qrest_ready"); kp_ready = sem("kp_ready"); qp_ready = sem("qp_ready")
        kd_out = [sem(f"kd_out{i}") for i in range(2)]
        qd_out = [sem(f"qd_out{i}") for i in range(2)]
        kq_in = [sem(f"kq_in{i}") for i in range(3)]
        mx_ready = sem("mx_ready"); mx_reduced = sem("mx_reduced")
        neg_split = [sem("neg_split0"), sem("neg_split1")]
        nmt_ready = [sem("nmt_ready0"), sem("nmt_ready1")]
        nm_in = [sem("nm_in0"), sem("nm_in1")]
        st_ready = sem("st_ready"); exp_done = sem("exp_done"); av_done = sem("av_done")
        av_taken = sem("av_taken"); norm_done = sem("norm_done")
        xmid_ready = sem("xmid_ready"); out_stored = sem("out_stored")
        stats2 = sem("stats2"); rs1_ready = sem("rs1_ready"); rs2_ready = sem("rs2_ready")
        var2_ready = sem("var2_ready"); rows_ready = sem("rows_ready"); rows_copied = sem("rows_copied")
        x2t_ready = sem("x2t_ready"); lg_ready = sem("lg_ready"); ls_ready = sem("ls_ready")
        ex_ready = sem("ex_ready"); sel_ready = sem("sel_ready"); chosen_ready = sem("chosen_ready"); gates_ready = sem("gates_ready")
        pos_read = sem("pos_read"); slot_ready = sem("slot_ready"); scattered = [sem("scattered0"), sem("scattered1")]
        we_in = sem("we_in")
        table_ready = sem("table_ready")
        xg_in = [sem("xg_in0"), sem("xg_in1")]
        tx_ready = sem("tx_ready"); txe_ready = sem("txe_ready"); gw_ready = sem("gw_ready"); gi_ready = sem("gi_ready")
        h_ready = sem("h_ready"); sg_ready = sem("sg_ready"); hm_ready = sem("hm_ready")
        ht_ready = sem("ht_ready"); hte_ready = sem("hte_ready")
        y_ready = sem("y_ready"); ys_ready = sem("ys_ready"); added = sem("added")

        EVACUATED = {"CT": ct_ready, "XT": xt_ready, "K": kf_ready, "Q": qf_ready, "V": v_ready,
                     "NM0": nmt_ready[0], "NM1": nmt_ready[1], "WO": xmid_ready, "X2": x2t_ready,
                     "LG": lg_ready, "PF": pos_read}

        def misc_bank(kind, n):
            return MISC[MISC_NO[kind, n] % 2]

        def wait_misc(eng, kind, n):
            eng.wait_ge(misc_ready, MISC_NO[kind, n] + 1)

        CONST_IDENT = 2
        CONST_ALL = 13
        DVE_CONSTS = 10
        block = es.enter_context(nc.Block())

        @block.sync
        def _(sp):
            def load_context(n):
                if n >= 3:
                    wait_misc(sp, "CT", n - 3)
                r = n % 3
                sp.dma_start(C[:, TB * r:TB * (r + 1), :], c_t[n]).then_inc(c_in[n], 16)

            load_context(0)
            sp.dma_start(wk[:], Wk.rearrange("(k p) n -> p k n", p=P)).then_inc(wkv_in, 16)
            sp.dma_start(X[:, 0:TB, :], x_t[0]).then_inc(x_in[0], 16)
            sp.dma_start(bkc[:], bk.rearrange("(c p) -> p c", p=P), allow_slow_non_contiguous=True).then_inc(wkv_in, 16)
            sp.dma_start(wq[:], Wq.rearrange("(k p) n -> p k n", p=P)).then_inc(wq_in, 16)
            sp.dma_start(bqc[:], bq.rearrange("(c p) -> p c", p=P), allow_slow_non_contiguous=True).then_inc(wq_in, 16)
            sp.dma_start(maskrow[:], mask.rearrange("b i j s -> b (i j s)")).then_inc(mask_in, 16)
            sp.dma_start(wv[:], Wv.rearrange("(k p) n -> p k n", p=P)).then_inc(wkv_in, 16)
            sp.dma_start(bvb[:], bv.partition_broadcast(P)).then_inc(wkv_in, 16)
            sp.dma_start(bob[:], bo.partition_broadcast(P)).then_inc(wq_in, 16)
            for n in range(1, B):
                sp.dma_start(X[:, TB * n:TB * (n + 1), :], x_t[n]).then_inc(x_in[n], 16)
                if n < 3:
                    load_context(n)
            for j in range(4):
                for i in range(2):
                    sp.dma_start(wo[32 * j + DH * i:32 * j + DH * (i + 1), :, :],
                                 Wo.rearrange("(i g j d) n -> j i d g n", i=2, g=2, d=DH)[j, i]).then_inc(wrest_in, 16)
            sp.dma_start(wg[:], w_gate.rearrange("(k p) e -> p k e", p=P), allow_slow_non_contiguous=True).then_inc(wrest_in, 16)

            def load_up(e):
                sp.dma_start(wf[:, e * KC * 2 * FF:(e + 1) * KC * 2 * FF].rearrange("p (k f) -> p k f", k=KC),
                             c_fc[e].rearrange("(k p) f -> p k f", p=P)).then_inc(we_in, 16)

            for it in ITERATIONS:
                if 3 <= it + 3 < B:
                    load_context(it + 3)
                for n, _ in projected(it):
                    if n >= 3:
                        sp.wait_ge(st_ready, UNITS * (n - 2))
                    if n < 3:
                        sp.wait_ge(mask_split, 1)
                        sp.wait_ge(qs_ones, n + 1)
                        sp.wait_ge(ks_ones, n + 1)
                    for j in range(3):
                        sp.dma_start(KS[R_MASK + j:R_MASK + j + 1, n % 3, :, :],
                                     mparts[n:n + 1, j, :].unsqueeze(1).broadcast_to([1, H, S])).then_inc(kq_in[n % 3], 16)
                    for parts, ready, back, dram in ((KP, kp_ready, kd_out, kparts_d), (QP, qp_ready, qd_out, qparts_d)):
                        sp.wait_ge(ready, n + 1)
                        if n >= 2:
                            sp.wait_ge(kq_in[(n - 2) % 3], 240 * ((n - 2) // 3 + 1))
                        sp.dma_start(dram[n % 2].rearrange("j c p t -> p (j c) t"), parts[:].rearrange("p j (c t) -> p (j c) t", c=KC)).then_inc(back[n % 2], 16)
                    for dst, part_of, back, dram in ((KS, K_PART, kd_out, kparts_d), (QS, Q_PART, qd_out, qparts_d)):
                        sp.wait_ge(back[n % 2], 16 * (n // 2 + 1))
                        for j in range(6):
                            sp.dma_start(dst[DH * j:DH * (j + 1), n % 3, :, :],
                                         dram[n % 2][part_of[j]].rearrange("c (h d) t -> d (c h) t", d=DH)).then_inc(kq_in[n % 3], 16)
                if 0 <= it - 1:
                    sp.wait_ge(xmid_ready, it)
                    sp.dma_start(out_t[it - 1], X[:, TB * (it - 1):TB * it, :]).then_inc(out_stored, 16)
                if 0 <= it < B:
                    if it < E - LATE:
                        load_up(it)
                    sp.dma_start(wp[:, it * FC * D:(it + 1) * FC * D].rearrange("p (k d) -> p k d", k=FC),
                                 c_proj[it].rearrange("(k p) d -> p k d", p=P)).then_inc(we_in, 16)
            sp.wait_ge(st_ready, UNITS * B)
            for e in range(E - LATE, E):
                load_up(e)

            sp.wait_ge(table_ready, 1)
            for i in range(2):
                sp.wait_ge(scattered[i], 16 * TB * TOPK * (B // 2))
            pairs = sp.value_load(npairs[0:1, 0:1], min_val=8, max_val=MAXPAIR)

            def load_block(t, u):
                if later(t, 2):
                    sp.wait_ge(tx_ready, t - 1)
                    sp.wait_ge(gi_ready, t - 1)
                row = sp.value_load(table[0:1, 0, bass.ds(t, 1)], min_val=0, max_val=XROWS - P)
                sp.dma_start(XG[:, u, :], slots[bass.ds(row, P), :]).then_inc(xg_in[u], 16)

            for t in range(PEELED + 1):
                load_block(t, t % 2)
            with sp.Fori(0, pairs - PEELED // 2) as i:
                for u in range(2):
                    load_block(2 * i + PEELED + 1 + u, 1 - u)
            sp.wait_ge(out_stored, 16 * B)

        @block.gpsimd
        def _(pool):
            def const(ins):
                ins.then_inc(const_step, 1)
                const.n += 1
                pool.wait_ge(const_step, const.n)
            const.n = 0
            const(pool.memset(ident[:], 0.0))
            const(pool.affine_select(out=ident[:], in_=ident[:], compare_op=ALU.not_equal, fill=1.0,
                                     base=0, pattern=[[-1, P]], channel_multiplier=1))
            const(pool.memset(ones[:], 1.0))
            const(pool.affine_select(out=before[:], in_=ones[:], compare_op=ALU.is_gt, fill=0.0,
                                     base=0, pattern=[[1, P]], channel_multiplier=-1))
            const(pool.memset(mhalf[:], -0.5))
            const(pool.iota(iota_i[:, 0:E], [[1, E]], base=0, channel_multiplier=0))
            const(pool.iota(iota_i[:, 8:72], [[0, E], [P, E]], base=0, channel_multiplier=0))
            const(pool.iota(iota_i[:, 72:136], [[1, E], [-1, E]], base=0, channel_multiplier=0))
            const(pool.iota(iota_i[:, 136:136 + MAXBLK], [[1, MAXBLK]], base=0, channel_multiplier=0))
            const(pool.iota(iota_i[:, 192:192 + MAXBLK // 2], [[2, MAXBLK // 2]], base=0, channel_multiplier=0))
            const(pool.iota(tok_no[:], [[P, NT]], base=0, channel_multiplier=1))
            const(pool.memset(pad_row[:, 0:D + 1], 0.0))
            const(pool.iota(pad_row[:, D + 1:D + 2].bitcast(U32), [[0, 1]], base=PAD_TOK, channel_multiplier=0))
            assert const.n == CONST_ALL

            def layernorm1(n):
                q = n % 2
                pool.wait_ge(stats1, TB * (n + 1))
                pool.tensor_scalar(rs1[:, q, :], mv1[:, q, :, 1], EPS, None, ALU.add).then_inc(var1_ready, 1)
                pool.wait_ge(var1_ready, n + 1)
                pool.tensor_tensor(rs1[:, q, :], rs1[:, q, :], mhalf[:], ALU.pow).then_inc(rs1_ready, 1)

            def add_output_bias(n):
                if n == 0:
                    pool.wait_ge(wq_in, 48)
                pool.wait_ge(xn_ready, TB * (n + 1))
                xs = X[:, TB * n:TB * (n + 1), :]
                pool.tensor_tensor(xs, xs, bob[:].unsqueeze(1).broadcast_to([P, TB, D]), ALU.add).then_inc(xb_ready, 1)

            def last_part(n, parts, rest_done, done):
                pool.wait_ge(rest_done, n + 1)
                pool.tensor_tensor(parts[:, 2, :], SPL[:], parts[:, 1, :], ALU.subtract).then_inc(done, 1)

            def layernorm2(n):
                q = n % 2
                pool.wait_ge(stats2, TB * (n + 1))
                pool.tensor_scalar(rs2[:, q, :], mv2[:, q, :, 1], EPS, None, ALU.add).then_inc(var2_ready, 1)
                pool.wait_ge(var2_ready, n + 1)
                pool.tensor_tensor(rs2[:, q, :], rs2[:, q, :], mhalf[:], ALU.pow).then_inc(rs2_ready, 1)

            def scatter(n):
                q = n % 2
                if n == 0:
                    pool.wait_ge(slots_padded, 16 * PADS)
                pool.wait_ge(rows_copied, n + 1)
                pool.wait_ge(slot_ready, n + 1)
                for t in range(TB):
                    for k in range(TOPK):
                        pool.indirect_dma_start(
                            slots, bass.IndirectOffsetOnAxis(ap=slot[:, q, t, k:k + 1], axis=0),
                            R[:, q, t, k, :], None, bounds_check=E * CAP - 1, oob_is_err=False).then_inc(scattered[q], 16)

            def ones_rows(slot_no):
                two = float(np.array([0x3F803F80], np.uint32).view(np.float32)[0])
                if slot_no:
                    pool.wait_ge(qp_ready, slot_no)
                else:
                    pool.wait_ge(rs1_ready, 1)
                for dst, done in ((KS, ks_ones), (QS, qs_ones)):
                    pool.memset(dst[R_MASK:P, slot_no].rearrange("p h s -> p (h s)").bitcast(F32), two).then_inc(done, 1)
                    pool.wait_ge(done, slot_no + 1)

            layernorm1(0)
            ones_rows(0)
            add_output_bias(0)
            for it in ITERATIONS:
                if it - 2 >= 0:
                    scatter(it - 2)
                if it + 3 < B:
                    layernorm1(it + 3)
                for n, _ in projected(it):
                    last_part(n, KP, krest_ready, kp_ready)
                    last_part(n, QP, qrest_ready, qp_ready)
                    if n < 2:
                        ones_rows(n + 1)
                if 0 <= it - 1:
                    layernorm2(it - 1)
                if it + 3 < B:
                    add_output_bias(it + 3)
            scatter(B - 1)

            pool.wait_ge(out_stored, 16 * B)
            pool.wait_ge(table_ready, 1)
            pairs = pool.value_load(npairs[0:1, 0:1], min_val=8, max_val=MAXPAIR)

            no_row, last_row = pool.alloc_register("no_row"), pool.alloc_register("last_row")
            pool.reg_mov(no_row, 0)

            def add_block(t, u):
                if later(t, 1):
                    pool.wait_ge(added, t * 16)
                pool.wait_ge(ys_ready, t + 1)
                pool.reg_add(last_row, no_row, B * S - 1)
                pool.indirect_dma_start(out_rows, bass.IndirectOffsetOnAxis(ap=GI[u][:], axis=0), Y[:, u, :], None,
                                        bounds_check=last_row, oob_is_err=False,
                                        compute_op=ALU.add).then_inc(added, 16)

            add_block(0, 0)
            add_block(1, 1)
            with pool.Fori(0, pairs - 1) as i:
                for u in range(2):
                    add_block(2 * i + 2 + u, u)
            pool.wait_ge(added, pairs * 32)

        @block.scalar
        def _(act):
            act.wait_ge(const_step, CONST_ALL)
            def evacuate(kind, n):
                wait_misc(act, kind, n)
                src = misc_bank(kind, n)
                q = n % 2
                if kind in ("CT", "XT"):
                    dst, ready = (CTt, ct_ready) if kind == "CT" else (XTt, xt_ready)
                    if n >= 2:
                        wait_misc(act, "V" if kind == "CT" else "Q", n - 2)
                    act.activation(dst[:, q].rearrange("p c s -> p (c s)"), src[:], ACT.Copy).then_inc(ready, 1)
                elif kind in ("K", "Q"):
                    dst, bias, scale, done, ready = ((KF, bkc, 1.0, kp_ready, kf_ready) if kind == "K" else
                                                     (QF, bq4, 0.25, qp_ready, qf_ready))
                    if n >= 2:
                        act.wait_ge(done, n - 1)
                    if n == 0 and kind == "K":
                        act.wait_ge(wkv_in, 64)
                    if n == 0 and kind == "Q":
                        act.wait_ge(dve_const, DVE_CONSTS)
                    for c in range(KC):
                        ins = act.activation(dst[:, q, c * S:(c + 1) * S], src[:, c * S:(c + 1) * S], ACT.Identity,
                                             bias=bias[:, c:c + 1], scale=scale)
                    ins.then_inc(ready, 1)
                    parts, copied, first_ready = (KP, kd_out, kp0_ready) if kind == "K" else (QP, qd_out, qp0_ready)
                    act.wait_ge(ready, n + 1)
                    if n >= 1:
                        act.wait_ge(copied[1 - q], 16 * ((n + 1) // 2))
                    act.activation(parts[:, 0, :], dst[:, q, :], ACT.Copy).then_inc(first_ready, 1)
                elif kind in ("NM0", "NM1"):
                    half = int(kind[2])
                    if n >= 1:
                        act.wait_ge(nm_in[half], 48 * n)
                    act.activation(NMT[:, half, :], src[0:24, 0:S // 2].bitcast(BF16), ACT.Copy).then_inc(nmt_ready[half], 1)
                elif kind == "X2":
                    if n >= 1:
                        wait_misc(act, "LG", n - 1)
                    act.activation(X2T[:].rearrange("p c s -> p (c s)"), src[:], ACT.Copy).then_inc(x2t_ready, 1)

            def max_rows(n, half):
                act.wait_ge(nmt_ready[half], n + 1)
                if n >= 3:
                    act.wait_ge(st_ready, UNITS * (n - 2))
                if n < 3:
                    act.wait_ge(qs_ones, n + 1)
                for j in range(3):
                    act.dma_start(QS[R_MAX + j:R_MAX + j + 1, n % 3, 8 * half:8 * half + 8, :],
                                  NMT[8 * j:8 * j + 8, half, :]).then_inc(nm_in[half], 16)

            def copy_rows(n):
                q = n % 2
                act.wait_ge(rows_ready, TB * (n + 1))
                if n >= 2:
                    act.wait_ge(scattered[q], 16 * TB * TOPK * (n // 2))
                act.activation(R[:, q, :, 1, 0:D], R[:, q, :, 0, 0:D], ACT.Copy).then_inc(rows_copied, 1)

            pad_rows = slots.rearrange("(n p) f -> p n f", p=P)

            def pad_slots(k):
                a, b = XROWS // P * k // PADS, XROWS // P * (k + 1) // PADS
                act.dma_start(pad_rows[:, a:b], pad_row[:].unsqueeze(1).broadcast_to([P, b - a, RW])).then_inc(slots_padded, 16)

            def exponentials(n, u):
                s = UNITS * n + u
                act.wait_ge(st_ready, s + 1)
                if s >= NPROB:
                    act.wait_ge(av_done, s - NPROB + 1)
                act.activation(PR[:, s % NPROB, :], STB[s % 2][:], ACT.Exp).then_inc(exp_done, 1)

            for it in ITERATIONS:
                for u in range(UNITS):
                    if 0 <= it < B:
                        exponentials(it, u)
                    for kind, n in misc_at(it, u):
                        if kind in ("CT", "XT", "K", "Q", "NM0", "NM1", "X2"):
                            evacuate(kind, n)
                    if u == COPY_ROWS_AT and 0 <= it - 1:
                        copy_rows(it - 1)
                    if u == 3 and 0 <= it < B:
                        max_rows(it, 1)
                    if -1 <= it < 2 and u % 3 == 2:
                        pad_slots(5 * (it + 1) + u // 3)
                    if u == 11 and 0 <= it + 1 < B:
                        max_rows(it + 1, 0)
                    if u == 12 and 0 <= it - 1:
                        act.wait_ge(ls_ready, it)
                        act.activation(ex[:], ls[:], ACT.Exp).then_inc(ex_ready, 1)

            act.wait_ge(table_ready, 1)
            pairs = act.value_load(npairs[0:1, 0:1], min_val=8, max_val=MAXPAIR)
            last = act.value_load(npairs[0:1, 1:2], min_val=14, max_val=2 * MAXPAIR - 2) + 1

            def silu(t, u):
                act.wait_ge(h_ready, t + 1)
                if later(t, 2):
                    act.wait_ge(hm_ready, t - 1)
                act.activation(SG[:, u, :], bank[2 + 2 * u][:, 0:FF], ACT.Silu).then_inc(sg_ready, 1)

            def hidden_copy(t, u):
                act.wait_ge(ht_ready, t + 1)
                if later(t, 2):
                    act.wait_ge(y_ready, t - 1)
                act.activation(HT[:, u].rearrange("p c t -> p (c t)"), bank[1][:, 0:FF], ACT.Copy).then_inc(hte_ready, 1)

            def step(t, u):
                hidden_copy(t - 1, 1 - u)
                silu(t, u)

            silu(0, 0)
            for t in range(1, PEELED):
                step(t, t % 2)
            with act.Fori(0, pairs - PEELED // 2) as i:
                for u in range(2):
                    step(2 * i + PEELED + u, u)
            hidden_copy(last, 1)

        @block.tensor
        def _(pe):
            def take_bank(kind, n):
                k = MISC_NO[kind, n]
                if k >= 2:
                    before_kind, m = MISC_ORDER[k - 2]
                    pe.wait_ge(EVACUATED[before_kind], m + 1)
                return MISC[k % 2]

            def transposes(src, kind, n):
                dst = take_bank(kind, n)
                for k in range(KC):
                    for t in range(TB):
                        ins = pe.transpose(dst[:, k * S + t * P:k * S + (t + 1) * P], src(t, k), ident[:])
                ins.then_inc(misc_ready, 1)

            def misc(kind, n):
                q = n % 2
                if kind == "CT":
                    pe.wait_ge(c_in[n], 16)
                    transposes(lambda t, k: C[:, TB * (n % 3) + t, k * P:(k + 1) * P], kind, n)
                elif kind == "XT":
                    pe.wait_ge(xn_ready, TB * (n + 1))
                    transposes(lambda t, k: XN[:, q, t, k * P:(k + 1) * P], kind, n)
                elif kind in ("K", "Q"):
                    w, src, ready = (wk, CTt, ct_ready) if kind == "K" else (wq, XTt, xt_ready)
                    pe.wait_ge(ready, n + 1)
                    if n == 0 and kind == "K":
                        pe.wait_ge(wkv_in, 64)
                    if n == 0 and kind == "Q":
                        pe.wait_ge(wq_in, 48)
                    dst = take_bank(kind, n)
                    for c in range(KC):
                        for k in range(KC):
                            ins = pe.matmul(dst[:, c * S:(c + 1) * S], w[:, k, c * P:(c + 1) * P], src[:, q, k, :],
                                            start=k == 0, stop=k == KC - 1)
                    ins.then_inc(misc_ready, 1)
                elif kind == "V":
                    dst = take_bank(kind, n)
                    for t in range(TB):
                        for k in range(KC):
                            ins = pe.matmul(dst[:, t * D:(t + 1) * D], CTt[:, q, k, t * P:(t + 1) * P], wv[:, k, :],
                                            start=k == 0, stop=k == KC - 1)
                    ins.then_inc(misc_ready, 1)
                elif kind in ("NM0", "NM1"):
                    half = int(kind[2])
                    pe.wait_ge(neg_split[half], n + 1)
                    if n == 0:
                        pe.wait_ge(dve_const, DVE_CONSTS)
                    dst = take_bank(kind, n)
                    for t in range(TB):
                        ins = pe.transpose(dst[0:24, t * P // 2:(t + 1) * P // 2].bitcast(BF16),
                                           NMS[:, half, t].rearrange("p j h -> p (j h)"), identb[:])
                    ins.then_inc(misc_ready, 1)
                elif kind == "WO":
                    pe.wait_ge(norm_done, n + 1)
                    if n == 0:
                        pe.wait_ge(wrest_in, 144)
                    dst = take_bank(kind, n)
                    for t in range(TB):
                        for g in range(2):
                            ins = pe.matmul(dst[:, t * D:(t + 1) * D], ON[:, g * S + t * P:g * S + (t + 1) * P], wo[:, g, :],
                                            start=g == 0, stop=g == 1)
                    ins.then_inc(misc_ready, 1)
                elif kind == "X2":
                    pe.wait_ge(rows_ready, TB * (n + 1))
                    transposes(lambda t, k: R[:, q, t, 0, k * P:(k + 1) * P], kind, n)
                elif kind == "LG":
                    pe.wait_ge(x2t_ready, n + 1)
                    dst = take_bank(kind, n)
                    for t in range(TB):
                        for k in range(KC):
                            ins = pe.matmul(dst[:, t * E:(t + 1) * E], X2T[:, k, t * P:(t + 1) * P], wg[:, k, :],
                                            start=k == 0, stop=k == KC - 1)
                    ins.then_inc(misc_ready, 1)
                elif kind == "PF":
                    pe.wait_ge(chosen_ready, 2 * n + 1)
                    dst = take_bank(kind, n)
                    pe.matmul(dst[:, 0:TB * E], beforeb[:], sel[:, q].rearrange("p t e -> p (t e)"), start=True, stop=False)
                    pe.matmul(dst[:, 0:TB * E], onesb[:], chosen[:, n].rearrange("p t e -> p (t e)"),
                              start=False, stop=True).then_inc(misc_ready, 1)

            def row_max_logits(n, u):
                m = UNITS * n + u
                hp, t = u // 2, u % 2
                if u == 0:
                    pe.wait_ge(kq_in[n % 3], 240 * (n // 3 + 1))
                if m >= 2:
                    pe.wait_ge(mx_reduced, m - 1)
                for i in range(2):
                    h = 2 * hp + i
                    ins = pe.matmul(MXB[m % 2][:, i * S:(i + 1) * S], QS[0:R_MAX, n % 3, h, t * P:(t + 1) * P],
                                    KS[0:R_MAX, n % 3, h, :], start=True, stop=True)
                ins.then_inc(mx_ready, 1)

            def logits(n, u):
                s = UNITS * n + u
                hp, c = u // 2, u % 2
                if u % 8 == 0:
                    pe.wait_ge(nm_in[u // 8], 48 * (n + 1))
                if s >= 2:
                    pe.wait_ge(exp_done, s - 1)
                for i in range(2):
                    h = 2 * hp + i
                    ins = pe.matmul(STB[s % 2][:, i * S:(i + 1) * S], KS[0:R_END, n % 3, h, c * P:(c + 1) * P],
                                    QS[0:R_END, n % 3, h, :], start=True, stop=True)
                ins.then_inc(st_ready, 1)

            def values(n, u):
                s = UNITS * n + u
                hp, c = u // 2, u % 2
                pe.wait_ge(exp_done, s + 1)
                if u == 0:
                    pe.wait_ge(v_ready, n + 1)
                    pe.wait_ge(va_ones, 1)
                if u % 8 == 0 and n >= 1:
                    pe.wait_ge(av_taken, 2 * (n - 1) + u // 8 + 1)
                for i in range(2):
                    h = 2 * hp + i
                    g, j = h // 4, h % 4
                    ins = pe.matmul(AVB[g // 2][32 * j:32 * j + 32, (g % 2) * S:(g % 2 + 1) * S],
                                    VA[:, n % 2, c, h, :], PR[:, s % NPROB, i * S:(i + 1) * S],
                                    start=c == 0, stop=c == 1)
                ins.then_inc(av_done, 1)

            pe.wait_ge(const_step, CONST_IDENT)
            for it in ITERATIONS:
                for u in range(UNITS):
                    if 0 <= it + 1 < B:
                        row_max_logits(it + 1, u)
                    if 0 <= it < B:
                        logits(it, u)
                    if u >= 2 and 0 <= it < B:
                        values(it, u - 2)
                    if u < 2 and 0 <= it - 1:
                        values(it - 1, UNITS - 2 + u)
                    for kind, n in misc_at(it, u):
                        misc(kind, n)

            pe.wait_ge(chosen_ready, 2 * B)
            cnt_bank = take_bank("CNT", 0)
            pe.matmul(cnt_bank[:, 0:E], onesb[:], chosen[:, B, 0, :], start=True, stop=True).then_inc(misc_ready, 1)

            pe.wait_ge(mx_reduced, UNITS * B)
            pe.wait_ge(exp_done, UNITS * B)
            pe.wait_ge(av_taken, 2 * B)
            pe.wait_ge(pos_read, B)
            pe.wait_ge(table_ready, 1)
            pe.wait_ge(we_in, 32 * E)
            pairs = pe.value_load(npairs[0:1, 0:1], min_val=8, max_val=MAXPAIR)
            last = pe.value_load(npairs[0:1, 1:2], min_val=14, max_val=2 * MAXPAIR - 2) + 1

            def turn_rows(t, u):
                pe.wait_ge(xg_in[u], (t - u) * 8 + 16)
                if later(t, 1):
                    pe.wait_ge(txe_ready, t)
                for k in range(KC):
                    ins = pe.transpose(bank[0][:, k * P:(k + 1) * P], XG[:, u, k * P:(k + 1) * P], ident[:])
                ins.then_inc(tx_ready, 1)

            def up_weights(t):
                return pe.value_load(table[0:1, 1, bass.ds(t, 1)], min_val=0, max_val=(E - 1) * KC * 2 * FF)

            def down_weights(t):
                return pe.value_load(table[0:1, 2, bass.ds(t, 1)], min_val=0, max_val=(E - 1) * FC * D)

            def hidden(t, u, off):
                pe.wait_ge(txe_ready, t + 1)
                if later(t, 2):
                    pe.wait_ge(hm_ready, t - 1)
                for g in range(2):
                    for k in range(KC):
                        ins = pe.matmul(bank[2 + 2 * u + g][:, 0:FF], XTG[:, u, k, :],
                                        wf[:, bass.ds(off + (k * 2 + g) * FF, FF)],
                                        start=k == 0, stop=k == KC - 1)
                ins.then_inc(h_ready, 1)

            def turn_hidden(t, u):
                pe.wait_ge(hm_ready, t + 1)
                if later(t, 1):
                    pe.wait_ge(hte_ready, t)
                for c in range(FC):
                    ins = pe.transpose(bank[1][:, c * P:(c + 1) * P], HM[:, u, c * P:(c + 1) * P], ident[:])
                ins.then_inc(ht_ready, 1)

            def down(t, u, off):
                pe.wait_ge(hte_ready, t + 1)
                if later(t, 2):
                    pe.wait_ge(ys_ready, t - 1)
                for c in range(FC):
                    ins = pe.matmul(bank[6 + u][:, 0:D], HT[:, u, c, :], wp[:, bass.ds(off + c * D, D)],
                                    start=c == 0, stop=c == FC - 1)
                ins.then_inc(y_ready, 1)

            def step(t, u):
                up, dn = up_weights(t), down_weights(t - 1)
                turn_hidden(t - 1, 1 - u)
                hidden(t, u, up)
                turn_rows(t + 1, 1 - u)
                down(t - 1, 1 - u, dn)

            turn_rows(0, 0)
            hidden(0, 0, up_weights(0))
            turn_rows(1, 1)
            for t in range(1, PEELED):
                step(t, t % 2)
            with pe.Fori(0, pairs - PEELED // 2) as i:
                for u in range(2):
                    step(2 * i + PEELED + u, u)
            dn = down_weights(last)
            turn_hidden(last, 1)
            down(last, 1, dn)

        @block.vector
        def _(dve):
            def link(ins):
                link.n += 1
                ins.then_inc(dve_step, 1)
                dve.wait_ge(dve_step, link.n)
            link.n = 0

            def stats(n, src, bn, mv, out_sem, read_sem):
                q = n % 2
                if n >= 2:
                    dve.wait_ge(read_sem, TB * (n - 1))
                if n >= 1:
                    dve.wait_ge(out_sem, TB * n)
                for t in range(TB):
                    link(dve.bn_stats(bn[:, t, :], src[:, TB * n + t, :]))
                for t in range(TB):
                    dve.bn_aggr(mv[:, q, t, :], bn[:, t, :]).then_inc(out_sem, 1)

            def stats1_of(n):
                dve.wait_ge(x_in[n], 16)
                stats(n, X, bn1, mv1, stats1, xn_ready)

            def normalize1(n):
                q = n % 2
                dve.wait_ge(rs1_ready, n + 1)
                if n >= 2:
                    wait_misc(dve, "XT", n - 2)
                for t in range(TB):
                    dve.tensor_scalar(XN[:, q, t, :], X[:, TB * n + t, :], mv1[:, q, t, 0:1], rs1[:, q, t:t + 1],
                                      ALU.subtract, ALU.mult).then_inc(xn_ready, 1)

            stats1_of(0)
            dve.memset(VA[:, :, :, :, DH:32], 1.0).then_inc(va_ones, 1)
            dve.memset(chosen[:, 0, 0, :], 0.0).then_inc(dve_const, 1)
            normalize1(0)
            dve.wait_ge(mask_in, 16)
            link(dve.tensor_scalar(mres[:], maskrow[:], MASK_BIG, None, ALU.mult))
            link(dve.tensor_copy(mparts[:, 0, :], mres[:]))
            link(dve.tensor_tensor(mres2[:], mres[:], mparts[:, 0, :], ALU.subtract))
            link(dve.tensor_copy(mparts[:, 1, :], mres2[:]))
            dve.tensor_tensor(mparts[:, 2, :], mres2[:], mparts[:, 1, :], ALU.subtract).then_inc(mask_split, 1)
            dve.wait_ge(wq_in, 48)
            dve.tensor_scalar(bq4[:], bqc[:], 0.25, None, ALU.mult).then_inc(dve_const, 1)
            dve.wait_ge(const_step, CONST_ALL)
            dve.tensor_copy(identb[:], ident[:]).then_inc(dve_const, 1)
            dve.tensor_copy(beforeb[:], before[:]).then_inc(dve_const, 1)
            dve.tensor_copy(onesb[:], ones[:]).then_inc(dve_const, 1)
            dve.tensor_copy(expert_no[:], iota_i[:, 0:E]).then_inc(dve_const, 1)
            dve.tensor_copy(blk_lim[:].rearrange("p a b -> p (a b)"), iota_i[:, 8:72]).then_inc(dve_const, 1)
            dve.tensor_scalar(tri[:].rearrange("p a b -> p (a b)"), iota_i[:, 72:136], 0.0, None, ALU.is_ge).then_inc(dve_const, 1)
            dve.tensor_copy(blk_no[:], iota_i[:, 136:136 + MAXBLK]).then_inc(dve_const, 1)
            dve.tensor_copy(pair_lim[:], iota_i[:, 192:192 + MAXBLK // 2]).then_inc(dve_const, 1)
            dve.wait_ge(dve_const, DVE_CONSTS)
            dve.wait_ge(mask_split, 1)

            def reduce_max(n, u):
                m = UNITS * n + u
                hp, t = u // 2, u % 2
                dve.wait_ge(mx_ready, m + 1)
                dve.tensor_reduce(NEG[:, n % 2, t, 2 * hp:2 * hp + 2],
                                  MXB[m % 2][:].rearrange("p (i s) -> p i s", i=2), AX.X, ALU.max,
                                  negate=True).then_inc(mx_reduced, 1)

            def split_max(n, half):
                neg = NEG[:, n % 2, :, 8 * half:8 * half + 8]
                dve.wait_ge(mx_reduced, UNITS * n + 8 * (half + 1))
                if n >= 1:
                    wait_misc(dve, f"NM{half}", n - 1)
                if n >= 1 or half == 1:
                    dve.wait_ge(neg_split[1 - half], n + half)
                link(dve.tensor_copy(NMS[:, half, :, 0, :], neg))
                link(dve.tensor_tensor(NR[:], neg, NMS[:, half, :, 0, :], ALU.subtract))
                link(dve.tensor_copy(NMS[:, half, :, 1, :], NR[:]))
                dve.tensor_tensor(NMS[:, half, :, 2, :], NR[:], NMS[:, half, :, 1, :], ALU.subtract).then_inc(neg_split[half], 1)

            def normalize_product(n, i):
                dve.wait_ge(av_done, UNITS * n + 8 * (i + 1))
                ins = dve.transpose(AVT[:].rearrange("p b c -> p (b c)"), AVB[i][:])
                ins.then_inc(av_taken, 1)
                dve.wait_ge(av_taken, 2 * n + i + 1)
                link(dve.reciprocal(RSUM[:], AVT[:, :, DH]))
                link(dve.tensor_tensor(AVN[:, :, i, :], AVT[:, :, 0:DH],
                                       RSUM[:].unsqueeze(2).broadcast_to([P, 16, DH]), ALU.mult))
                if i == 1:
                    if n >= 1:
                        wait_misc(dve, "WO", n - 1)
                    dve.transpose(ON[:], AVN[:].rearrange("p b i d -> p (b i d)")).then_inc(norm_done, 1)
                    dve.wait_ge(norm_done, n + 1)

            def second_part(n, full, parts, first_ready, copied, rest_ready, spl_used, spl_count):
                q = n % 2
                dve.wait_ge(first_ready, n + 1)
                if n >= 1:
                    dve.wait_ge(copied[1 - q], 16 * ((n + 1) // 2))
                if spl_count > 0:
                    dve.wait_ge(spl_used, spl_count)
                link(dve.tensor_tensor(SPL[:], full[:, q, :], parts[:, 0, :], ALU.subtract))
                dve.tensor_copy(parts[:, 1, :], SPL[:]).then_inc(rest_ready, 1)

            def normalize2(n):
                q = n % 2
                dve.wait_ge(rs2_ready, n + 1)
                if n >= 2:
                    dve.wait_ge(scattered[q], 16 * TB * TOPK * (n // 2))
                for t in range(TB):
                    dve.tensor_scalar(R[:, q, t, 0, 0:D], X[:, TB * n + t, :], mv2[:, q, t, 0:1], rs2[:, q, t:t + 1],
                                      ALU.subtract, ALU.mult).then_inc(rows_ready, 1)

            def take_values(n):
                wait_misc(dve, "V", n)
                if n == 0:
                    dve.wait_ge(wkv_in, 64)
                if n >= 2:
                    dve.wait_ge(av_done, UNITS * (n - 1))
                dve.tensor_tensor(VA[:, n % 2, :, :, 0:DH],
                                  misc_bank("V", n)[:].rearrange("p (t h d) -> p t h d", t=TB, d=DH),
                                  bvb[:].rearrange("p (h d) -> p h d", d=DH).unsqueeze(1).broadcast_to([P, TB, H, DH]),
                                  ALU.add).then_inc(v_ready, 1)

            def residual(n):
                wait_misc(dve, "WO", n)
                dve.wait_ge(xb_ready, n + 1)
                xs = X[:, TB * n:TB * (n + 1), :].rearrange("p t d -> p (t d)")
                dve.tensor_tensor(xs, misc_bank("WO", n)[:], xs, ALU.add).then_inc(xmid_ready, 1)
                dve.wait_ge(xmid_ready, n + 1)
                stats(n, X, bn2, mv2, stats2, rows_ready)

            def route_scores(n):
                wait_misc(dve, "LG", n)
                if n >= 1:
                    dve.wait_ge(ls_ready, n)
                dve.tensor_copy(lg[:].rearrange("p t e -> p (t e)"), misc_bank("LG", n)[:, 0:TB * E]).then_inc(lg_ready, 1)
                dve.wait_ge(lg_ready, n + 1)
                link(dve.tensor_reduce(nmx[:], lg[:], AX.X, ALU.max, negate=True))
                if n >= 1:
                    dve.wait_ge(ex_ready, n)
                dve.tensor_tensor(ls[:], lg[:], nmx[:].unsqueeze(2).broadcast_to([P, TB, E]), ALU.add).then_inc(ls_ready, 1)

            def route_choice(n):
                q = n % 2
                dve.wait_ge(ex_ready, n + 1)
                if n >= 1:
                    dve.wait_ge(gates_ready, 2 * n)
                    dve.wait_ge(chosen_ready, 2 * n)
                    dve.wait_ge(pos_read, n)
                    dve.wait_ge(slot_ready, n)
                link(dve.tensor_reduce(sm[:], ex[:], AX.X, ALU.add))
                link(dve.reciprocal(rsm[:], sm[:]))
                link(dve.tensor_tensor(sc[:], ex[:], rsm[:].unsqueeze(2).broadcast_to([P, TB, E]), ALU.mult))
                for t in range(TB):
                    link(dve.max(top[:, t, :], sc[:, t, :]))
                for t in range(TB):
                    link(dve.max_index(topi[:, t, :], top[:, t, :], sc[:, t, :]))
                link(dve.tensor_copy(topf[:], topi[:, :, 0:TOPK]))
                link(dve.tensor_tensor(oh[:], topf[:].unsqueeze(3).broadcast_to([P, TB, TOPK, E]),
                                       expert_no[:].unsqueeze(1).unsqueeze(1).broadcast_to([P, TB, TOPK, E]), ALU.is_equal))
                if n >= 2:
                    wait_misc(dve, "PF", n - 2)
                dve.tensor_tensor(sel[:, q], oh[:, :, 0, :], oh[:, :, 1, :], ALU.add).then_inc(sel_ready, 1)
                dve.wait_ge(sel_ready, n + 1)
                dve.tensor_tensor(chosen[:, n, 1, :], chosen[:, n, 0, :], sel[:, q, 0, :], ALU.add).then_inc(chosen_ready, 1)
                dve.wait_ge(chosen_ready, 2 * n + 1)
                dve.tensor_tensor(chosen[:, n + 1, 0, :], chosen[:, n, 1, :], sel[:, q, 1, :], ALU.add).then_inc(chosen_ready, 1)
                if n >= 2:
                    dve.wait_ge(scattered[q], 16 * TB * TOPK * (n // 2))
                dve.tensor_copy(R[:, q, :, :, D], top[:, :, 0:TOPK]).then_inc(gates_ready, 1)
                dve.tensor_copy(R[:].bitcast(U32)[:, q, :, :, D + 1],
                                tok_no[:, TB * n:TB * (n + 1)].unsqueeze(2).broadcast_to([P, TB, TOPK])).then_inc(gates_ready, 1)

            def route_slots(n):
                q = n % 2
                wait_misc(dve, "PF", n)
                earlier = misc_bank("PF", n)[:, 0:TB * E].rearrange("p (t e) -> p t e", e=E)
                dve.tensor_tensor(ohp[:], earlier.unsqueeze(2).broadcast_to([P, TB, TOPK, E]), oh[:], ALU.mult).then_inc(pos_read, 1)
                dve.wait_ge(pos_read, n + 1)
                link(dve.tensor_reduce(pos[:], ohp[:], AX.X, ALU.add))
                link(dve.tensor_scalar(lost[:], pos[:], float(CAP), float(SLOT_LOST), ALU.is_ge, ALU.mult))
                link(dve.scalar_tensor_tensor(out=slotf[:], in0=topf[:], scalar=float(CAP), in1=pos[:],
                                              op0=ALU.mult, op1=ALU.add))
                dve.tensor_tensor(slot[:, q], slotf[:], lost[:], ALU.add).then_inc(slot_ready, 1)

            for it in ITERATIONS:
                for u in range(UNITS):
                    if 0 <= it + 1 < B:
                        reduce_max(it + 1, u)
                    if u == 0 and 0 <= it < B:
                        split_max(it, 1)
                    if u == 1 and 0 <= it - 2:
                        route_slots(it - 2)
                    if u == 1 and 1 <= it + 3 < B:
                        stats1_of(it + 3)
                    if u == 2 and 0 <= it - 1:
                        normalize_product(it - 1, 1)
                    for n in projected_at(it, u, 3):
                        second_part(n, KF, KP, kp0_ready, kd_out, krest_ready, qp_ready, n)
                    if u == 4 and it + 3 < B:
                        normalize1(it + 3)
                    for n in projected_at(it, u, 4):
                        second_part(n, QF, QP, qp0_ready, qd_out, qrest_ready, kp_ready, n + 1)
                    if u == 8 and 0 <= it - 1:
                        normalize2(it - 1)
                    if u == 6 and 0 <= it - 1:
                        residual(it - 1)
                    if u == 7 and 0 <= it + 1 < B:
                        take_values(it + 1)
                    if u == 8 and 0 <= it + 1 < B:
                        split_max(it + 1, 0)
                    if u == 10 and 0 <= it < B:
                        normalize_product(it, 0)
                    if u == 12 and 0 <= it - 1:
                        route_scores(it - 1)
                    if u == 13 and 0 <= it - 1:
                        route_choice(it - 1)
                    if u == 15 and it == B:
                        route_slots(it - 1)

            wait_misc(dve, "CNT", 0)
            link(dve.tensor_scalar(cnt[:], misc_bank("CNT", 0)[:, 0:E], float(CAP), None, ALU.min))
            link(dve.tensor_tensor(cmp8[:], cnt[:].unsqueeze(2).broadcast_to([P, E, E]), blk_lim[:], ALU.is_gt))
            link(dve.tensor_reduce(nblk[:], cmp8[:], AX.X, ALU.add))
            link(dve.tensor_tensor(cum8[:], tri[:], nblk[:].unsqueeze(1).broadcast_to([P, E, E]), ALU.mult))
            link(dve.tensor_reduce(incl[:], cum8[:], AX.X, ALU.add))
            link(dve.tensor_tensor(le[:], incl[:].unsqueeze(1).broadcast_to([P, MAXBLK, E]),
                                   blk_no[:].unsqueeze(2).broadcast_to([P, MAXBLK, E]), ALU.is_le))
            link(dve.tensor_reduce(bexp[:], le[:], AX.X, ALU.add))
            link(dve.tensor_tensor(leb[:], le[:], nblk[:].unsqueeze(1).broadcast_to([P, MAXBLK, E]), ALU.mult))
            link(dve.tensor_reduce(bex[:], leb[:], AX.X, ALU.add))
            link(dve.scalar_tensor_tensor(out=btmp[:], in0=bexp[:], scalar=float(CAP // P), in1=blk_no[:],
                                          op0=ALU.mult, op1=ALU.add))
            link(dve.tensor_tensor(btmp2[:], btmp[:], bex[:], ALU.subtract))
            link(dve.tensor_scalar(table[:, 0, :], btmp2[:], float(P), None, ALU.mult))
            link(dve.tensor_scalar(bcl[:], bexp[:], float(E - 1), None, ALU.min))
            link(dve.tensor_scalar(table[:, 1, :], bcl[:], float(KC * 2 * FF), None, ALU.mult))
            link(dve.tensor_scalar(table[:, 2, :], bcl[:], float(FC * D), None, ALU.mult))
            link(dve.tensor_scalar(pcmp[:], pair_lim[:], incl[:, E - 1:E], None, ALU.is_lt))
            link(dve.tensor_reduce(pcnt[:], pcmp[:], AX.X, ALU.add))
            link(dve.tensor_copy(npairs[:, 0:1], pcnt[:]))
            dve.tensor_scalar(npairs[:, 1:2], pcnt[:], 2.0, -2.0, ALU.mult, ALU.add).then_inc(table_ready, 1)

            dve.wait_ge(table_ready, 1)
            pairs = dve.value_load(npairs[0:1, 0:1], min_val=8, max_val=MAXPAIR)
            last = dve.value_load(npairs[0:1, 1:2], min_val=14, max_val=2 * MAXPAIR - 2) + 1

            def rows_copy(t, u):
                dve.wait_ge(tx_ready, t + 1)
                if later(t, 2):
                    dve.wait_ge(h_ready, t - 1)
                dve.tensor_copy(XTG[:, u].rearrange("p k t -> p (k t)"), bank[0][:, 0:D]).then_inc(txe_ready, 1)

            def gates_copy(t, u):
                dve.wait_ge(xg_in[u], (t - u) * 8 + 16)
                if later(t, 2):
                    dve.wait_ge(added, (t - 1) * 16)
                dve.tensor_copy(GW[:, u, :], XG[:, u, D:D + 1]).then_inc(gw_ready, 1)
                dve.tensor_copy(GI[u][:], XG[:, u, D + 1:D + 2].bitcast(U32)).then_inc(gi_ready, 1)

            def gated(t, u):
                dve.wait_ge(sg_ready, t + 1)
                if later(t, 2):
                    dve.wait_ge(ht_ready, t - 1)
                dve.tensor_tensor(HM[:, u, :], bank[3 + 2 * u][:, 0:FF], SG[:, u, :], ALU.mult).then_inc(hm_ready, 1)

            def weigh(t, u):
                dve.wait_ge(y_ready, t + 1)
                dve.wait_ge(gw_ready, t + 1)
                if later(t, 2):
                    dve.wait_ge(added, (t - 1) * 16)
                dve.tensor_scalar(Y[:, u, :], bank[6 + u][:, 0:D], GW[:, u, 0:1], None, ALU.mult).then_inc(ys_ready, 1)

            def step(t, u):
                gates_copy(t, u)
                rows_copy(t + 1, 1 - u)
                gated(t, u)
                weigh(t - 1, 1 - u)

            rows_copy(0, 0)
            gates_copy(0, 0)
            rows_copy(1, 1)
            gated(0, 0)
            for t in range(1, PEELED):
                step(t, t % 2)
            with dve.Fori(0, pairs - PEELED // 2) as i:
                for u in range(2):
                    step(2 * i + PEELED + u, u)
            weigh(last, 1)


INPUTS = ["x", "ctx_1024", "mask_Bx1x1xS2_fk0", "L0_xattn_Wq", "L0_xattn_bq", "L0_xattn_Wk", "L0_xattn_bk",
          "L0_xattn_Wv", "L0_xattn_bv", "L0_xattn_Wo", "L0_xattn_bo", "L0_ffn_w_gate", "L0_ffn_c_fc", "L0_ffn_c_proj"]


def kernel(**inputs):
    import concourse.bacc as bacc
    from concourse.bass_utils import run_bass_kernel_spmd

    nc = bacc.Bacc("TRN2", target_bir_lowering=False, num_devices=1)
    arrays, args = {}, []
    for name in INPUTS:
        a = np.ascontiguousarray(inputs[name])
        arrays[f"in_{name}"] = a
        args.append(nc.dram_tensor(f"in_{name}", a.shape, mybir.dt.from_np(a.dtype), kind="ExternalInput").ap())
    out = nc.dram_tensor("out_0", (B, S, D), F32, kind="ExternalOutput").ap()
    program(nc, *args, out)
    r = run_bass_kernel_spmd(nc, [arrays], core_ids=[0])
    return r.results[0]["out_0"]
```

```python
from contextlib import ExitStack

import numpy as np

import concourse.bass as bass
from concourse import mybir

F32 = mybir.dt.float32
BF16 = mybir.dt.bfloat16
U32 = mybir.dt.uint32
I32 = mybir.dt.int32
ALU = mybir.AluOpType
ACT = mybir.ActivationFunctionType
AX = mybir.AxisListType

P = 128
B, S, D, H = 8, 256, 256, 16
DH = D // H
E, TOPK, CAP = 8, 2, 1024
FF = 384
NT = B * S // P
TB = S // P
KC = D // P
FC = FF // P
UNITS = 16
NPROB = 4
EPS = 1e-5
MASK_BIG = -1e9
RW = D + 2
PAD_TOK = B * S
XROWS = E * CAP + 3 * P
SLOT_LOST = 1 << 17
MAXPAIR = (B * S * TOPK // P + E - 1 + 1) // 2
MAXBLK = 2 * MAXPAIR + 2

LATE = 4
PADS = 15
PEELED = 4

MATCH_K = (0, 1, 0)
MATCH_Q = (1, 0, 0)
ROWS3 = 3 * DH
KQ_LOADS = 9
R_MASK = 6 * DH
R_MAX = R_MASK + 3
R_END = R_MAX + 3


MISC_PLAN = (
    (1, "PF", -2), (3, "NM1", 0), (5, "WO", -1), (7, "V", 1),
    (10, "NM0", 1), (10, "X2", -1), (12, "LG", -1),
)
ITERATIONS = range(-2, B + 1)


COPY_ROWS_AT = 10
SECOND_K, SECOND_Q = 5, 6
GATES_AT = 14
BIAS_AT = 3
PROJECTION = ((0, "CT"), (1, "XT"), (3, "K"), (4, "Q"))


def projected(it):
    if it == -2:
        return ((0, 0), (1, 7))
    return ((it + 2, 0),) if 0 <= it < B - 2 else ()


def projected_at(it, unit, after):
    return [n for n, start in projected(it) if unit == start + after]


def misc_at(it, unit):
    pieces = [(u, kind, it + rel) for u, kind, rel in MISC_PLAN if u == unit and 0 <= it + rel < B]
    pieces += [(start + u, kind, n) for n, start in projected(it) for u, kind in PROJECTION if start + u == unit]
    if it == -1 and unit == BIAS_AT:
        pieces += [(unit, "BO", 0)]
    if it == B and unit == UNITS - 1:
        pieces += [(unit, "PF", B - 1)]
    return [(kind, n) for _, kind, n in sorted(pieces)]


MISC_ORDER = [piece for it in ITERATIONS for u in range(UNITS) for piece in misc_at(it, u)] + [("CNT", 0)]
MISC_NO = {piece: k for k, piece in enumerate(MISC_ORDER)}


def by_chunk(ap):
    return ap.rearrange("p (c t) -> p c t", c=KC)


def later(t, least):
    return not isinstance(t, int) or t >= least


def program(nc, x, ctx_in, mask, Wq, bq, Wk, bk, Wv, bv, Wo, bo, w_gate, c_fc, c_proj, out):
    x_t = x.rearrange("b (t p) d -> b p t d", p=P)
    c_t = ctx_in.rearrange("b (t p) d -> b p t d", p=P)
    out_rows = out.rearrange("b s d -> (b s) d")
    out_t = out.rearrange("b (t p) d -> b p t d", p=P)

    slots = nc.dram_tensor("slots", (XROWS, RW), F32, kind="Internal").ap()
    mparts_d = nc.dram_tensor("mparts_d", (B, 3, S), BF16, kind="Internal").ap()
    kparts_d = [nc.dram_tensor(f"kparts_d{i}", (KC, P, 3, S), BF16, kind="Internal").ap() for i in range(2)]
    qparts_d = [nc.dram_tensor(f"qparts_d{i}", (KC, P, 3, S), BF16, kind="Internal").ap() for i in range(2)]

    with ExitStack() as es:
        def sb(name, shape, dt=F32):
            return es.enter_context(nc.sbuf_tensor(name, shape, dt))

        def sem(name):
            return es.enter_context(nc.semaphore(name))

        bank = [es.enter_context(nc.psum_tensor(f"bank{i}", [P, 512], F32)) for i in range(8)]
        MXB, STB, AVB, MISC = bank[0:2], bank[2:4], bank[4:6], bank[6:8]

        X = sb("X", [P, NT, D])
        C = sb("C", [P, 3 * TB, D])
        wq = sb("wq", [P, KC, D]); wk = sb("wk", [P, KC, D]); wv = sb("wv", [P, KC, D])
        wo = sb("wo", [P, 2, D])
        wg = sb("wg", [P, KC, E])
        wf = sb("wf", [P, E * KC * 2 * FF])
        QS = wf[:, (E - LATE) * KC * 2 * FF:].bitcast(BF16).rearrange("p (r h s) -> p r h s", r=3, h=H)
        wp = sb("wp", [P, E * FC * D])
        bvc = sb("bvc", [P, 2]); bvm = sb("bvm", [P, 2, P])
        bqc = sb("bqc", [P, KC]); bq4 = sb("bq4", [P, KC]); bkc = sb("bkc", [P, KC])
        bob = sb("bob", [P, D])
        ident = sb("ident", [P, P]); identb = sb("identb", [P, P], BF16)
        before = sb("before", [P, P]); ones = sb("ones", [P, P])
        beforeb = sb("beforeb", [P, P], BF16); onesb = sb("onesb", [P, P], BF16)
        mhalf = sb("mhalf", [P, TB])
        iota_i = sb("iota_i", [P, 256], I32)
        expert_no = sb("expert_no", [P, E]); blk_lim = sb("blk_lim", [P, E, E]); tri = sb("tri", [P, E, E])
        blk_no = sb("blk_no", [P, MAXBLK]); pair_lim = sb("pair_lim", [P, MAXBLK // 2])
        tok_no = sb("tok_no", [P, NT], U32)
        pad_row = sb("pad_row", [P, RW])
        mparts = sb("mparts", [B, 3, S], BF16)
        bn1 = sb("bn1", [P, TB, 6]); mv1 = sb("mv1", [P, 2, TB, 2]); rs1 = sb("rs1", [P, 2, TB])
        bn2 = sb("bn2", [P, TB, 6]); mv2 = sb("mv2", [P, 2, TB, 2]); rs2 = sb("rs2", [P, 2, TB])
        XN = sb("XN", [P, 2, TB, D])
        CTt = sb("CTt", [P, 2, KC, S]); XTt = sb("XTt", [P, 2, KC, S])
        KF = sb("KF", [P, 2, KC * S]); QF = sb("QF", [P, 2, KC * S]); KREST = sb("KREST", [P, KC * S]); QREST = sb("QREST", [P, KC * S])
        KP = sb("KP", [P, KC, 3, S], BF16); QP = sb("QP", [P, KC, 3, S], BF16)
        KS = sb("KS", [P, 3, H, S], BF16)
        VA = sb("VA", [P, 2, TB, H, 32])
        PR = sb("PR", [P, NPROB, 512])
        NEG = sb("NEG", [P, 2, TB, H]); NR = sb("NR", [P, TB, 8]); NR2 = sb("NR2", [P, TB, 8])
        NMS = sb("NMS", [P, 2, TB, 3, 8], BF16); NMT = sb("NMT", [24, 2, S], BF16)
        AVT = sb("AVT", [P, 16, 32])
        RSUM = sb("RSUM", [P, 16]); AVN = sb("AVN", [P, 16, 2, DH])
        ON = sb("ON", [P, 512])
        R = sb("R", [P, 2, TB, TOPK, RW])
        X2T = sb("X2T", [P, KC, S])
        ls = sb("ls", [P, TB, E]); ex = sb("ex", [P, TB, E])
        sm = sb("sm", [P, TB]); rsm = sb("rsm", [P, TB]); 
        top = sb("top", [P, TB, 8]); topi = sb("topi", [P, TB, 8], U32); topf = sb("topf", [P, TB, TOPK])
        oh = sb("oh", [P, TB, TOPK, E]); sel = sb("sel", [P, 2, TB, E], BF16)
        chosen = sb("chosen", [P, B + 1, TB, E], BF16)
        ohp = sb("ohp", [P, TB, TOPK, E]); pos = sb("pos", [P, TB, TOPK])
        lost = sb("lost", [P, TB, TOPK]); slotf = sb("slotf", [P, TB, TOPK]); slotg = sb("slotg", [P, TB, TOPK])
        slot = sb("slot", [P, 2, TB, TOPK], U32)
        cnt = sb("cnt", [P, E]); cmp8 = sb("cmp8", [P, E, E]); nblk = sb("nblk", [P, E])
        cum8 = sb("cum8", [P, E, E]); incl = sb("incl", [P, E])
        bexp = sb("bexp", [P, MAXBLK]); bex = sb("bex", [P, MAXBLK]); bcl = sb("bcl", [P, MAXBLK])
        btmp = sb("btmp", [P, MAXBLK]); btmp2 = sb("btmp2", [P, MAXBLK])
        pcmp = sb("pcmp", [P, MAXBLK // 2]); pcnt = sb("pcnt", [P, 1])
        table = sb("table", [P, 3, MAXBLK], I32); npairs = sb("npairs", [P, 2], I32)
        GW = sb("GW", [P, 2, 1]); GI0 = sb("GI0", [P, 1], U32); GI1 = sb("GI1", [P, 1], U32)
        GI = (GI0, GI1)
        XG = sb("XG", [P, 2, RW])
        MASKBUF = PR[0:B, 0:3, 0:S]
        maskrow, mres, mres2 = MASKBUF[:, 0, :], MASKBUF[:, 1, :], MASKBUF[:, 2, :]
        le = PR[:, 0, 0:MAXBLK * E].rearrange("p (b e) -> p b e", e=E)
        leb = PR[:, 1, 0:MAXBLK * E].rearrange("p (b e) -> p b e", e=E)
        XTG = XN[:, :, 0, :].rearrange("p u (k t) -> p u k t", k=KC)
        SG, HM = KF[:, :, 0:FF], QF[:, :, 0:FF]
        HT = XTt[:].rearrange("p u c s -> p u (c s)")[:, :, 0:FF].rearrange("p u (c t) -> p u c t", c=FC)
        Y = CTt[:, :, 0, :]

        x_in = [sem(f"x_in{n}") for n in range(B)]
        c_in = [sem(f"c_in{n}") for n in range(B)]
        wkv_in = sem("wkv_in"); wq_in = sem("wq_in"); wrest_in = sem("wrest_in"); mask_in = sem("mask_in")
        slots_padded = sem("slots_padded")
        const_step = sem("const_step")
        dve_const = sem("dve_const")
        dve_step = sem("dve_step")
        qs_ones = sem("qs_ones"); ks_ones = sem("ks_ones"); va_ones = sem("va_ones")
        mask_split = sem("mask_split"); mask_out = sem("mask_out")
        stats1 = sem("stats1")
        var1_ready = sem("var1_ready"); xn_ready = sem("xn_ready"); xb_ready = sem("xb_ready")
        misc_ready = sem("misc_ready")
        ct_ready = sem("ct_ready"); xt_ready = sem("xt_ready")
        kf_ready = sem("kf_ready"); qf_ready = sem("qf_ready"); v_ready = sem("v_ready")
        bvm_ready = sem("bvm_ready"); bias_ready = sem("bias_ready")
        kp0_ready = sem("kp0_ready"); qp0_ready = sem("qp0_ready"); kp1_ready = sem("kp1_ready"); qp1_ready = sem("qp1_ready"); krest_ready = sem("krest_ready"); qrest_ready = sem("qrest_ready"); kp_ready = sem("kp_ready"); qp_ready = sem("qp_ready")
        kd_out = [sem(f"kd_out{i}") for i in range(2)]
        qd_out = [sem(f"qd_out{i}") for i in range(2)]
        kq_in = [sem(f"kq_in{i}") for i in range(3)]
        mx_ready = sem("mx_ready"); mx_reduced = sem("mx_reduced")
        neg_split = [sem("neg_split0"), sem("neg_split1")]
        nmt_ready = [sem("nmt_ready0"), sem("nmt_ready1")]
        nm_in = [sem("nm_in0"), sem("nm_in1")]
        st_ready = sem("st_ready"); exp_done = sem("exp_done"); av_done = sem("av_done")
        av_taken = sem("av_taken"); norm_done = sem("norm_done")
        xmid_ready = sem("xmid_ready"); out_stored = sem("out_stored")
        stats2 = sem("stats2"); rs1_ready = sem("rs1_ready"); rs2_ready = sem("rs2_ready")
        var2_ready = sem("var2_ready"); rows_ready = sem("rows_ready"); rows_copied = sem("rows_copied")
        x2t_ready = sem("x2t_ready"); lg_ready = sem("lg_ready"); ls_ready = sem("ls_ready")
        ex_ready = sem("ex_ready"); sel_ready = sem("sel_ready"); chosen_ready = sem("chosen_ready"); gates_ready = sem("gates_ready")
        pos_read = sem("pos_read"); slot_ready = sem("slot_ready"); scattered = [sem("scattered0"), sem("scattered1")]
        we_in = sem("we_in"); numbers_ready = sem("numbers_ready")
        table_ready = sem("table_ready")
        xg_in = [sem("xg_in0"), sem("xg_in1")]
        tx_ready = sem("tx_ready"); txe_ready = sem("txe_ready"); gw_ready = sem("gw_ready"); gi_ready = sem("gi_ready")
        h_ready = sem("h_ready"); sg_ready = sem("sg_ready"); hm_ready = sem("hm_ready")
        ht_ready = sem("ht_ready"); hte_ready = sem("hte_ready")
        y_ready = sem("y_ready"); ys_ready = sem("ys_ready"); added = sem("added")

        EVACUATED = {"CT": ct_ready, "XT": xt_ready, "K": kf_ready, "Q": qf_ready, "V": v_ready,
                     "NM0": nmt_ready[0], "NM1": nmt_ready[1], "WO": xmid_ready, "X2": x2t_ready,
                     "LG": lg_ready, "BO": bias_ready, "PF": pos_read}

        def misc_bank(kind, n):
            return MISC[MISC_NO[kind, n] % 2]

        def wait_misc(eng, kind, n):
            eng.wait_ge(misc_ready, MISC_NO[kind, n] + 1)

        CONST_IDENT = 2
        CONST_ALL = 13
        DVE_CONSTS = 10
        block = es.enter_context(nc.Block())

        @block.sync
        def _(sp):
            def load_context(n):
                if n >= 3:
                    wait_misc(sp, "CT", n - 3)
                r = n % 3
                sp.dma_start(C[:, TB * r:TB * (r + 1), :], c_t[n]).then_inc(c_in[n], 16)

            load_context(0)
            sp.dma_start(wk[:], Wk.rearrange("(k p) n -> p k n", p=P)).then_inc(wkv_in, 16)
            sp.dma_start(X[:, 0:TB, :], x_t[0]).then_inc(x_in[0], 16)
            sp.dma_start(bkc[:], bk.rearrange("(c p) -> p c", p=P), allow_slow_non_contiguous=True).then_inc(wkv_in, 16)
            sp.dma_start(wq[:], Wq.rearrange("(k p) n -> p k n", p=P)).then_inc(wq_in, 16)
            sp.dma_start(bqc[:], bq.rearrange("(c p) -> p c", p=P), allow_slow_non_contiguous=True).then_inc(wq_in, 16)
            sp.dma_start(maskrow[:], mask.rearrange("b i j s -> b (i j s)")).then_inc(mask_in, 16)
            sp.dma_start(wv[:], Wv.rearrange("(k p) n -> p k n", p=P)).then_inc(wkv_in, 16)
            sp.dma_start(bob[:], bo.partition_broadcast(P)).then_inc(wq_in, 16)
            for n in range(1, B):
                sp.dma_start(X[:, TB * n:TB * (n + 1), :], x_t[n]).then_inc(x_in[n], 16)
                if n < 3:
                    load_context(n)
            for j in range(4):
                for i in range(2):
                    sp.dma_start(wo[32 * j + DH * i:32 * j + DH * (i + 1), :, :],
                                 Wo.rearrange("(i g j d) n -> j i d g n", i=2, g=2, d=DH)[j, i]).then_inc(wrest_in, 16)
                    sp.dma_start(bvc[32 * j + DH * i:32 * j + DH * (i + 1), :],
                                 bv.rearrange("(i g j d) -> j i d g", i=2, g=2, d=DH)[j, i],
                                 allow_slow_non_contiguous=True).then_inc(wrest_in, 16)
            sp.dma_start(wg[:], w_gate.rearrange("(k p) e -> p k e", p=P), allow_slow_non_contiguous=True).then_inc(wrest_in, 16)

            def load_up(e):
                sp.dma_start(wf[:, e * KC * 2 * FF:(e + 1) * KC * 2 * FF].rearrange("p (k f) -> p k f", k=KC),
                             c_fc[e].rearrange("(k p) f -> p k f", p=P)).then_inc(we_in, 16)

            for it in ITERATIONS:
                if 3 <= it + 3 < B:
                    load_context(it + 3)
                for n, _ in projected(it):
                    if n >= 3:
                        sp.wait_ge(st_ready, UNITS * (n - 2))
                    if n < 3:
                        sp.wait_ge(qs_ones, n + 1)
                        sp.wait_ge(ks_ones, n + 1)
                    if n == 0:
                        sp.wait_ge(mask_split, 1)
                        sp.dma_start(mparts_d, mparts[:]).then_inc(mask_out, 16)
                        sp.wait_ge(mask_out, 16)
                    sp.dma_start(KS[R_MASK:R_MAX, n % 3, :, :],
                                 mparts_d[n].unsqueeze(1).broadcast_to([3, H, S])).then_inc(kq_in[n % 3], 16)
                    for parts, ready, back, dram in ((KP, kp_ready, kd_out, kparts_d), (QP, qp_ready, qd_out, qparts_d)):
                        sp.wait_ge(ready, n + 1)
                        if n >= 2:
                            sp.wait_ge(kq_in[(n - 2) % 3], KQ_LOADS * 16 * ((n - 2) // 3 + 1))
                        sp.dma_start(dram[n % 2].rearrange("c p j t -> p c (j t)"),
                                     parts[:].rearrange("p c j t -> p c (j t)")).then_inc(back[n % 2], 16)
                    for dst, own, other, match, back, dram in ((KS, ROWS3, 0, MATCH_K, kd_out, kparts_d),
                                                               (QS, 0, ROWS3, MATCH_Q, qd_out, qparts_d)):
                        sp.wait_ge(back[n % 2], 16 * (n // 2 + 1))
                        sp.dma_start(dst[own:own + ROWS3, n % 3, :, :],
                                     dram[n % 2].rearrange("c (h d) j t -> (d j) (c h) t", d=DH)).then_inc(kq_in[n % 3], 16)
                        for j in range(3):
                            sp.dma_start(dst[other + j:other + ROWS3:3, n % 3, :, :],
                                         dram[n % 2][:, :, match[j]].rearrange("c (h d) t -> d (c h) t", d=DH)).then_inc(kq_in[n % 3], 16)
                if 0 <= it - 1:
                    sp.wait_ge(xmid_ready, it)
                    sp.dma_start(out_t[it - 1], X[:, TB * (it - 1):TB * it, :]).then_inc(out_stored, 16)
                if 0 <= it < B:
                    if it < E - LATE:
                        load_up(it)
                    sp.dma_start(wp[:, it * FC * D:(it + 1) * FC * D].rearrange("p (k d) -> p k d", k=FC),
                                 c_proj[it].rearrange("(k p) d -> p k d", p=P)).then_inc(we_in, 16)
            sp.wait_ge(st_ready, UNITS * B)
            for e in range(E - LATE, E):
                load_up(e)

            sp.wait_ge(table_ready, 1)
            for i in range(2):
                sp.wait_ge(scattered[i], 16 * TB * TOPK * (B // 2))
            pairs = sp.value_load(npairs[0:1, 0:1], min_val=8, max_val=MAXPAIR)

            def load_block(t, u):
                if later(t, 2):
                    sp.wait_ge(tx_ready, t - 1)
                    sp.wait_ge(gi_ready, t - 1)
                row = sp.value_load(table[0:1, 0, bass.ds(t, 1)], min_val=0, max_val=XROWS - P)
                sp.dma_start(XG[:, u, :], slots[bass.ds(row, P), :]).then_inc(xg_in[u], 16)

            for t in range(PEELED + 1):
                load_block(t, t % 2)
            with sp.Fori(0, pairs - PEELED // 2) as i:
                for u in range(2):
                    load_block(2 * i + PEELED + 1 + u, 1 - u)
            sp.wait_ge(out_stored, 16 * B)

        @block.gpsimd
        def _(pool):
            def const(ins):
                ins.then_inc(const_step, 1)
                const.n += 1
                pool.wait_ge(const_step, const.n)
            const.n = 0
            const(pool.memset(ident[:], 0.0))
            const(pool.affine_select(out=ident[:], in_=ident[:], compare_op=ALU.not_equal, fill=1.0,
                                     base=0, pattern=[[-1, P]], channel_multiplier=1))
            const(pool.memset(ones[:], 1.0))
            const(pool.affine_select(out=before[:], in_=ones[:], compare_op=ALU.is_gt, fill=0.0,
                                     base=0, pattern=[[1, P]], channel_multiplier=-1))
            const(pool.memset(mhalf[:], -0.5))
            const(pool.iota(iota_i[:, 0:E], [[1, E]], base=0, channel_multiplier=0))
            const(pool.iota(iota_i[:, 8:72], [[0, E], [P, E]], base=0, channel_multiplier=0))
            const(pool.iota(iota_i[:, 72:136], [[1, E], [-1, E]], base=0, channel_multiplier=0))
            const(pool.iota(iota_i[:, 136:136 + MAXBLK], [[1, MAXBLK]], base=0, channel_multiplier=0))
            const(pool.iota(iota_i[:, 192:192 + MAXBLK // 2], [[2, MAXBLK // 2]], base=0, channel_multiplier=0))
            const(pool.iota(tok_no[:], [[P, NT]], base=0, channel_multiplier=1))
            const(pool.memset(pad_row[:, 0:D + 1], 0.0))
            const(pool.iota(pad_row[:, D + 1:D + 2].bitcast(U32), [[0, 1]], base=PAD_TOK, channel_multiplier=0))
            assert const.n == CONST_ALL

            def layernorm1(n):
                q = n % 2
                pool.wait_ge(stats1, TB * (n + 1))
                pool.tensor_scalar(rs1[:, q, :], mv1[:, q, :, 1], EPS, None, ALU.add).then_inc(var1_ready, 1)
                pool.wait_ge(var1_ready, n + 1)
                pool.tensor_tensor(rs1[:, q, :], rs1[:, q, :], mhalf[:], ALU.pow).then_inc(rs1_ready, 1)

            def normalize1(n):
                q = n % 2
                pool.wait_ge(rs1_ready, n + 1)
                if n >= 2:
                    wait_misc(pool, "XT", n - 2)
                for t in range(TB):
                    pool.tensor_scalar(XN[:, q, t, :], X[:, TB * n + t, :], mv1[:, q, t, 0:1], rs1[:, q, t:t + 1],
                                      ALU.subtract, ALU.mult).then_inc(xn_ready, 1)

            def add_output_bias(n):
                pool.wait_ge(bias_ready, 1)
                pool.wait_ge(xn_ready, TB * (n + 1))
                xs = X[:, TB * n:TB * (n + 1), :]
                pool.tensor_tensor(xs, xs, bob[:].unsqueeze(1).broadcast_to([P, TB, D]), ALU.add).then_inc(xb_ready, 1)

            def first_rest(n, full, parts, rest, first_ready, rest_ready, done):
                q = n % 2
                pool.wait_ge(first_ready, n + 1)
                if n >= 1:
                    pool.wait_ge(done, n)
                pool.tensor_tensor(by_chunk(rest[:]), by_chunk(full[:, q, :]), parts[:, :, 0, :], ALU.subtract).then_inc(rest_ready, 1)

            def last_part(n, parts, rest, second_ready, done):
                pool.wait_ge(second_ready, n + 1)
                pool.tensor_tensor(parts[:, :, 2, :], by_chunk(rest[:]), parts[:, :, 1, :], ALU.subtract).then_inc(done, 1)

            def layernorm2(n):
                q = n % 2
                pool.wait_ge(stats2, TB * (n + 1))
                pool.tensor_scalar(rs2[:, q, :], mv2[:, q, :, 1], EPS, None, ALU.add).then_inc(var2_ready, 1)
                pool.wait_ge(var2_ready, n + 1)
                pool.tensor_tensor(rs2[:, q, :], rs2[:, q, :], mhalf[:], ALU.pow).then_inc(rs2_ready, 1)

            def scatter(n):
                q = n % 2
                if n == 0:
                    pool.wait_ge(slots_padded, 16 * PADS)
                if n >= 2:
                    pool.wait_ge(scattered[q], 16 * TB * TOPK * (n // 2))
                pool.tensor_copy(R[:].bitcast(U32)[:, q, :, :, D + 1],
                                 tok_no[:, TB * n:TB * (n + 1)].unsqueeze(2).broadcast_to([P, TB, TOPK])).then_inc(numbers_ready, 1)
                pool.wait_ge(numbers_ready, n + 1)
                pool.wait_ge(gates_ready, n + 1)
                pool.wait_ge(rows_copied, n + 1)
                pool.wait_ge(slot_ready, n + 1)
                for t in range(TB):
                    for k in range(TOPK):
                        pool.indirect_dma_start(
                            slots, bass.IndirectOffsetOnAxis(ap=slot[:, q, t, k:k + 1], axis=0),
                            R[:, q, t, k, :], None, bounds_check=E * CAP - 1, oob_is_err=False).then_inc(scattered[q], 16)

            def ones_rows(slot_no):
                two = float(np.array([0x3F803F80], np.uint32).view(np.float32)[0])
                if slot_no:
                    pool.wait_ge(qp_ready, slot_no)
                else:
                    pool.wait_ge(xn_ready, TB)
                for dst, done in ((KS, ks_ones), (QS, qs_ones)):
                    pool.memset(dst[R_MASK:P, slot_no].rearrange("p h s -> p (h s)").bitcast(F32), two).then_inc(done, 1)
                    pool.wait_ge(done, slot_no + 1)

            layernorm1(0)
            normalize1(0)
            ones_rows(0)
            for it in ITERATIONS:
                if it == -2:
                    layernorm1(1)
                    normalize1(1)
                for n, _ in projected(it):
                    first_rest(n, KF, KP, KREST, kp0_ready, krest_ready, kp_ready)
                    first_rest(n, QF, QP, QREST, qp0_ready, qrest_ready, qp_ready)
                    last_part(n, KP, KREST, kp1_ready, kp_ready)
                    last_part(n, QP, QREST, qp1_ready, qp_ready)
                    if n < 2:
                        ones_rows(n + 1)
                if 0 <= it - 1:
                    layernorm2(it - 1)
                if it - 2 >= 0:
                    scatter(it - 2)
                if 2 <= it + 3 < B:
                    layernorm1(it + 3)
                    normalize1(it + 3)
                if 0 <= it < B:
                    add_output_bias(it)
            scatter(B - 1)

            pool.wait_ge(out_stored, 16 * B)
            pool.wait_ge(table_ready, 1)
            pairs = pool.value_load(npairs[0:1, 0:1], min_val=8, max_val=MAXPAIR)

            no_row, last_row = pool.alloc_register("no_row"), pool.alloc_register("last_row")
            pool.reg_mov(no_row, 0)

            def add_block(t, u):
                if later(t, 1):
                    pool.wait_ge(added, t * 16)
                pool.wait_ge(ys_ready, t + 1)
                pool.reg_add(last_row, no_row, B * S - 1)
                pool.indirect_dma_start(out_rows, bass.IndirectOffsetOnAxis(ap=GI[u][:], axis=0), Y[:, u, :], None,
                                        bounds_check=last_row, oob_is_err=False,
                                        compute_op=ALU.add).then_inc(added, 16)

            add_block(0, 0)
            add_block(1, 1)
            with pool.Fori(0, pairs - 1) as i:
                for u in range(2):
                    add_block(2 * i + 2 + u, u)
            pool.wait_ge(added, pairs * 32)

        @block.scalar
        def _(act):
            act.wait_ge(const_step, CONST_ALL)
            def evacuate(kind, n):
                wait_misc(act, kind, n)
                src = misc_bank(kind, n)
                q = n % 2
                if kind in ("CT", "XT"):
                    dst, ready = (CTt, ct_ready) if kind == "CT" else (XTt, xt_ready)
                    if n >= 2:
                        wait_misc(act, "V" if kind == "CT" else "Q", n - 2)
                    act.activation(dst[:, q].rearrange("p c s -> p (c s)"), src[:], ACT.Copy).then_inc(ready, 1)
                elif kind in ("K", "Q"):
                    dst, bias, scale, done, ready = ((KF, bkc, 1.0, kp_ready, kf_ready) if kind == "K" else
                                                     (QF, bq4, 0.25, qp_ready, qf_ready))
                    if n >= 2:
                        act.wait_ge(done, n - 1)
                    if n == 0 and kind == "K":
                        act.wait_ge(wkv_in, 48)
                    if n == 0 and kind == "Q":
                        act.wait_ge(dve_const, DVE_CONSTS)
                    for c in range(KC):
                        ins = act.activation(dst[:, q, c * S:(c + 1) * S], src[:, c * S:(c + 1) * S], ACT.Identity,
                                             bias=bias[:, c:c + 1], scale=scale)
                    ins.then_inc(ready, 1)
                    parts, copied, first_ready = (KP, kd_out, kp0_ready) if kind == "K" else (QP, qd_out, qp0_ready)
                    act.wait_ge(ready, n + 1)
                    if n >= 1:
                        act.wait_ge(copied[1 - q], 16 * ((n + 1) // 2))
                    act.activation(parts[:, :, 0, :], by_chunk(dst[:, q, :]), ACT.Copy).then_inc(first_ready, 1)
                elif kind in ("NM0", "NM1"):
                    half = int(kind[2])
                    if n >= 1:
                        act.wait_ge(nm_in[half], 48 * n)
                    act.activation(NMT[:, half, :], src[0:24, 0:S // 2].bitcast(BF16), ACT.Copy).then_inc(nmt_ready[half], 1)
                elif kind == "V":
                    if n >= 2:
                        act.wait_ge(av_done, UNITS * (n - 1))
                    act.activation(VA[:, n % 2, :, :, 0:DH], src[:].rearrange("p (t h d) -> p t h d", t=TB, d=DH),
                                   ACT.Copy).then_inc(v_ready, 1)
                elif kind == "X2":
                    if n >= 1:
                        wait_misc(act, "LG", n - 1)
                    act.activation(X2T[:].rearrange("p c s -> p (c s)"), src[:], ACT.Copy).then_inc(x2t_ready, 1)

            def max_rows(n, half):
                act.wait_ge(nmt_ready[half], n + 1)
                if n >= 3:
                    act.wait_ge(st_ready, UNITS * (n - 2))
                if n < 3:
                    act.wait_ge(qs_ones, n + 1)
                for j in range(3):
                    act.dma_start(QS[R_MAX + j:R_MAX + j + 1, n % 3, 8 * half:8 * half + 8, :],
                                  NMT[8 * j:8 * j + 8, half, :]).then_inc(nm_in[half], 16)

            def second_part(n, parts, rest, rest_ready, copied, done):
                act.wait_ge(rest_ready, n + 1)
                if n >= 1:
                    act.wait_ge(copied[(n - 1) % 2], 16 * ((n + 1) // 2))
                act.activation(parts[:, :, 1, :], by_chunk(rest[:]), ACT.Copy).then_inc(done, 1)

            def copy_rows(n):
                q = n % 2
                act.wait_ge(rows_ready, TB * (n + 1))
                if n >= 2:
                    act.wait_ge(scattered[q], 16 * TB * TOPK * (n // 2))
                act.activation(R[:, q, :, 1, 0:D], R[:, q, :, 0, 0:D], ACT.Copy).then_inc(rows_copied, 1)

            pad_rows = slots.rearrange("(n p) f -> p n f", p=P)

            def pad_slots(k):
                a, b = XROWS // P * k // PADS, XROWS // P * (k + 1) // PADS
                act.dma_start(pad_rows[:, a:b], pad_row[:].unsqueeze(1).broadcast_to([P, b - a, RW])).then_inc(slots_padded, 16)

            def exponentials(n, u):
                s = UNITS * n + u
                act.wait_ge(st_ready, s + 1)
                if s >= NPROB:
                    act.wait_ge(av_done, s - NPROB + 1)
                act.activation(PR[:, s % NPROB, :], STB[s % 2][:], ACT.Exp).then_inc(exp_done, 1)

            for it in ITERATIONS:
                for u in range(UNITS):
                    for n in projected_at(it, u, SECOND_Q):
                        second_part(n, QP, QREST, qrest_ready, qd_out, qp1_ready)
                    if 0 <= it < B:
                        exponentials(it, u)
                    for n in projected_at(it, u, SECOND_K):
                        second_part(n, KP, KREST, krest_ready, kd_out, kp1_ready)
                    for kind, n in misc_at(it, u):
                        if kind in ("CT", "XT", "K", "Q", "V", "NM0", "NM1", "X2"):
                            evacuate(kind, n)
                    if u == COPY_ROWS_AT and 0 <= it - 1:
                        copy_rows(it - 1)
                    if u == 4 and 0 <= it < B:
                        max_rows(it, 1)
                    if -1 <= it < 2 and u % 3 == 2:
                        pad_slots(5 * (it + 1) + u // 3)
                    if u == 11 and 0 <= it + 1 < B:
                        max_rows(it + 1, 0)
                    if u == GATES_AT - 1 and 0 <= it - 1:
                        act.wait_ge(ls_ready, it)
                        if it >= 2:
                            act.wait_ge(gates_ready, it - 1)
                        act.activation(ex[:], ls[:], ACT.Exp).then_inc(ex_ready, 1)

            act.wait_ge(table_ready, 1)
            pairs = act.value_load(npairs[0:1, 0:1], min_val=8, max_val=MAXPAIR)
            last = act.value_load(npairs[0:1, 1:2], min_val=14, max_val=2 * MAXPAIR - 2) + 1

            def silu(t, u):
                act.wait_ge(h_ready, t + 1)
                if later(t, 2):
                    act.wait_ge(hm_ready, t - 1)
                act.activation(SG[:, u, :], bank[2 + 2 * u][:, 0:FF], ACT.Silu).then_inc(sg_ready, 1)

            def hidden_copy(t, u):
                act.wait_ge(ht_ready, t + 1)
                if later(t, 2):
                    act.wait_ge(y_ready, t - 1)
                act.activation(HT[:, u].rearrange("p c t -> p (c t)"), bank[1][:, 0:FF], ACT.Copy).then_inc(hte_ready, 1)

            def step(t, u):
                hidden_copy(t - 1, 1 - u)
                silu(t, u)

            silu(0, 0)
            for t in range(1, PEELED):
                step(t, t % 2)
            with act.Fori(0, pairs - PEELED // 2) as i:
                for u in range(2):
                    step(2 * i + PEELED + u, u)
            hidden_copy(last, 1)

        @block.tensor
        def _(pe):
            def take_bank(kind, n):
                k = MISC_NO[kind, n]
                if k >= 2:
                    before_kind, m = MISC_ORDER[k - 2]
                    pe.wait_ge(EVACUATED[before_kind], (m + 1) * (TB if before_kind == "LG" else 1))
                return MISC[k % 2]

            def transposes(src, kind, n):
                dst = take_bank(kind, n)
                for k in range(KC):
                    for t in range(TB):
                        ins = pe.transpose(dst[:, k * S + t * P:k * S + (t + 1) * P], src(t, k), ident[:])
                ins.then_inc(misc_ready, 1)

            def misc(kind, n):
                q = n % 2
                if kind == "CT":
                    pe.wait_ge(c_in[n], 16)
                    transposes(lambda t, k: C[:, TB * (n % 3) + t, k * P:(k + 1) * P], kind, n)
                elif kind == "XT":
                    pe.wait_ge(xn_ready, TB * (n + 1))
                    transposes(lambda t, k: XN[:, q, t, k * P:(k + 1) * P], kind, n)
                elif kind in ("K", "Q"):
                    w, src, ready = (wk, CTt, ct_ready) if kind == "K" else (wq, XTt, xt_ready)
                    pe.wait_ge(ready, n + 1)
                    if n == 0 and kind == "K":
                        pe.wait_ge(wkv_in, 48)
                    if n == 0 and kind == "Q":
                        pe.wait_ge(wq_in, 48)
                    dst = take_bank(kind, n)
                    for c in range(KC):
                        for k in range(KC):
                            ins = pe.matmul(dst[:, c * S:(c + 1) * S], w[:, k, c * P:(c + 1) * P], src[:, q, k, :],
                                            start=k == 0, stop=k == KC - 1)
                    ins.then_inc(misc_ready, 1)
                elif kind == "V":
                    dst = take_bank(kind, n)
                    for t in range(TB):
                        for k in range(KC):
                            ins = pe.matmul(dst[:, t * D:(t + 1) * D], CTt[:, q, k, t * P:(t + 1) * P], wv[:, k, :],
                                            start=k == 0, stop=k == KC - 1)
                    ins.then_inc(misc_ready, 1)
                elif kind in ("NM0", "NM1"):
                    half = int(kind[2])
                    pe.wait_ge(neg_split[half], n + 1)
                    if n == 0:
                        pe.wait_ge(dve_const, DVE_CONSTS)
                    dst = take_bank(kind, n)
                    for t in range(TB):
                        ins = pe.transpose(dst[0:24, t * P // 2:(t + 1) * P // 2].bitcast(BF16),
                                           NMS[:, half, t].rearrange("p j h -> p (j h)"), identb[:])
                    ins.then_inc(misc_ready, 1)
                elif kind == "BO":
                    pe.wait_ge(bvm_ready, 2)
                    pe.wait_ge(wrest_in, 272)
                    dst = take_bank(kind, n)
                    for g in range(2):
                        ins = pe.matmul(dst[:, 0:D], bvm[:, g, :], wo[:, g, :], start=g == 0, stop=g == 1)
                    ins.then_inc(misc_ready, 1)
                elif kind == "WO":
                    pe.wait_ge(norm_done, n + 1)
                    if n == 0:
                        pe.wait_ge(wrest_in, 272)
                    dst = take_bank(kind, n)
                    for t in range(TB):
                        for g in range(2):
                            ins = pe.matmul(dst[:, t * D:(t + 1) * D], ON[:, g * S + t * P:g * S + (t + 1) * P], wo[:, g, :],
                                            start=g == 0, stop=g == 1)
                    ins.then_inc(misc_ready, 1)
                elif kind == "X2":
                    pe.wait_ge(rows_ready, TB * (n + 1))
                    transposes(lambda t, k: R[:, q, t, 0, k * P:(k + 1) * P], kind, n)
                elif kind == "LG":
                    pe.wait_ge(x2t_ready, n + 1)
                    dst = take_bank(kind, n)
                    for t in range(TB):
                        for k in range(KC):
                            ins = pe.matmul(dst[:, t * E:(t + 1) * E], X2T[:, k, t * P:(t + 1) * P], wg[:, k, :],
                                            start=k == 0, stop=k == KC - 1)
                    ins.then_inc(misc_ready, 1)
                elif kind == "PF":
                    pe.wait_ge(chosen_ready, 2 * n + 1)
                    dst = take_bank(kind, n)
                    pe.matmul(dst[:, 0:TB * E], beforeb[:], sel[:, q].rearrange("p t e -> p (t e)"), start=True, stop=False)
                    pe.matmul(dst[:, 0:TB * E], onesb[:], chosen[:, n].rearrange("p t e -> p (t e)"),
                              start=False, stop=True).then_inc(misc_ready, 1)

            def row_max_logits(n, u):
                m = UNITS * n + u
                hp, t = u // 2, u % 2
                if u == 0:
                    pe.wait_ge(kq_in[n % 3], KQ_LOADS * 16 * (n // 3 + 1))
                if m >= 2:
                    pe.wait_ge(mx_reduced, m - 1)
                for i in range(2):
                    h = 2 * hp + i
                    ins = pe.matmul(MXB[m % 2][:, i * S:(i + 1) * S], QS[0:R_MAX, n % 3, h, t * P:(t + 1) * P],
                                    KS[0:R_MAX, n % 3, h, :], start=True, stop=True)
                ins.then_inc(mx_ready, 1)

            def logits(n, u):
                s = UNITS * n + u
                hp, c = u // 2, u % 2
                if u % 8 == 0:
                    pe.wait_ge(nm_in[u // 8], 48 * (n + 1))
                if s >= 2:
                    pe.wait_ge(exp_done, s - 1)
                for i in range(2):
                    h = 2 * hp + i
                    ins = pe.matmul(STB[s % 2][:, i * S:(i + 1) * S], KS[0:R_END, n % 3, h, c * P:(c + 1) * P],
                                    QS[0:R_END, n % 3, h, :], start=True, stop=True)
                ins.then_inc(st_ready, 1)

            def values(n, u):
                s = UNITS * n + u
                hp, c = u // 2, u % 2
                pe.wait_ge(exp_done, s + 1)
                if u == 0:
                    pe.wait_ge(v_ready, n + 1)
                    pe.wait_ge(va_ones, 1)
                if u % 8 == 0 and n >= 1:
                    pe.wait_ge(av_taken, 2 * (n - 1) + u // 8 + 1)
                for i in range(2):
                    h = 2 * hp + i
                    g, j = h // 4, h % 4
                    ins = pe.matmul(AVB[g // 2][32 * j:32 * j + 32, (g % 2) * S:(g % 2 + 1) * S],
                                    VA[:, n % 2, c, h, :], PR[:, s % NPROB, i * S:(i + 1) * S],
                                    start=c == 0, stop=c == 1)
                ins.then_inc(av_done, 1)

            pe.wait_ge(const_step, CONST_IDENT)
            for it in ITERATIONS:
                for u in range(UNITS):
                    if 0 <= it + 1 < B:
                        row_max_logits(it + 1, u)
                    if 0 <= it < B:
                        logits(it, u)
                    if u >= 2 and 0 <= it < B:
                        values(it, u - 2)
                    if u < 2 and 0 <= it - 1:
                        values(it - 1, UNITS - 2 + u)
                    for kind, n in misc_at(it, u):
                        misc(kind, n)

            pe.wait_ge(chosen_ready, 2 * B)
            cnt_bank = take_bank("CNT", 0)
            pe.matmul(cnt_bank[:, 0:E], onesb[:], chosen[:, B, 0, :], start=True, stop=True).then_inc(misc_ready, 1)

            pe.wait_ge(mx_reduced, UNITS * B)
            pe.wait_ge(exp_done, UNITS * B)
            pe.wait_ge(av_taken, 2 * B)
            pe.wait_ge(pos_read, B)
            pe.wait_ge(table_ready, 1)
            pe.wait_ge(we_in, 32 * E)
            pairs = pe.value_load(npairs[0:1, 0:1], min_val=8, max_val=MAXPAIR)
            last = pe.value_load(npairs[0:1, 1:2], min_val=14, max_val=2 * MAXPAIR - 2) + 1

            def turn_rows(t, u):
                pe.wait_ge(xg_in[u], (t - u) * 8 + 16)
                if later(t, 1):
                    pe.wait_ge(txe_ready, t)
                for k in range(KC):
                    ins = pe.transpose(bank[0][:, k * P:(k + 1) * P], XG[:, u, k * P:(k + 1) * P], ident[:])
                ins.then_inc(tx_ready, 1)

            def up_weights(t):
                return pe.value_load(table[0:1, 1, bass.ds(t, 1)], min_val=0, max_val=(E - 1) * KC * 2 * FF)

            def down_weights(t):
                return pe.value_load(table[0:1, 2, bass.ds(t, 1)], min_val=0, max_val=(E - 1) * FC * D)

            def hidden(t, u, off):
                pe.wait_ge(txe_ready, t + 1)
                if later(t, 2):
                    pe.wait_ge(hm_ready, t - 1)
                for g in range(2):
                    for k in range(KC):
                        ins = pe.matmul(bank[2 + 2 * u + g][:, 0:FF], XTG[:, u, k, :],
                                        wf[:, bass.ds(off + (k * 2 + g) * FF, FF)],
                                        start=k == 0, stop=k == KC - 1)
                ins.then_inc(h_ready, 1)

            def turn_hidden(t, u):
                pe.wait_ge(hm_ready, t + 1)
                if later(t, 1):
                    pe.wait_ge(hte_ready, t)
                for c in range(FC):
                    ins = pe.transpose(bank[1][:, c * P:(c + 1) * P], HM[:, u, c * P:(c + 1) * P], ident[:])
                ins.then_inc(ht_ready, 1)

            def down(t, u, off):
                pe.wait_ge(hte_ready, t + 1)
                if later(t, 2):
                    pe.wait_ge(ys_ready, t - 1)
                for c in range(FC):
                    ins = pe.matmul(bank[6 + u][:, 0:D], HT[:, u, c, :], wp[:, bass.ds(off + c * D, D)],
                                    start=c == 0, stop=c == FC - 1)
                ins.then_inc(y_ready, 1)

            def step(t, u):
                up, dn = up_weights(t), down_weights(t - 1)
                turn_hidden(t - 1, 1 - u)
                hidden(t, u, up)
                turn_rows(t + 1, 1 - u)
                down(t - 1, 1 - u, dn)

            turn_rows(0, 0)
            hidden(0, 0, up_weights(0))
            turn_rows(1, 1)
            for t in range(1, PEELED):
                step(t, t % 2)
            with pe.Fori(0, pairs - PEELED // 2) as i:
                for u in range(2):
                    step(2 * i + PEELED + u, u)
            dn = down_weights(last)
            turn_hidden(last, 1)
            down(last, 1, dn)

        @block.vector
        def _(dve):
            def link(ins):
                link.n += 1
                ins.then_inc(dve_step, 1)
                dve.wait_ge(dve_step, link.n)
            link.n = 0

            def stats(n, src, bn, mv, out_sem, read_sem):
                q = n % 2
                if n >= 2:
                    dve.wait_ge(read_sem, TB * (n - 1))
                if n >= 1:
                    dve.wait_ge(out_sem, TB * n)
                for t in range(TB):
                    link(dve.bn_stats(bn[:, t, :], src[:, TB * n + t, :]))
                for t in range(TB):
                    dve.bn_aggr(mv[:, q, t, :], bn[:, t, :]).then_inc(out_sem, 1)

            def stats1_of(n):
                dve.wait_ge(x_in[n], 16)
                stats(n, X, bn1, mv1, stats1, xn_ready)

            def bias_columns():
                dve.wait_ge(wrest_in, 272)
                for g in range(2):
                    dve.tensor_scalar(bvm[:, g, :], ones[:], bvc[:, g:g + 1], None, ALU.mult).then_inc(bvm_ready, 1)

            stats1_of(0)
            dve.memset(VA[:, :, :, :, DH:32], 1.0).then_inc(va_ones, 1)
            dve.memset(chosen[:, 0, 0, :], 0.0).then_inc(dve_const, 1)
            dve.wait_ge(mask_in, 16)
            link(dve.tensor_scalar(mres[:], maskrow[:], MASK_BIG, None, ALU.mult))
            link(dve.tensor_copy(mparts[:, 0, :], mres[:]))
            link(dve.tensor_tensor(mres2[:], mres[:], mparts[:, 0, :], ALU.subtract))
            link(dve.tensor_copy(mparts[:, 1, :], mres2[:]))
            dve.tensor_tensor(mparts[:, 2, :], mres2[:], mparts[:, 1, :], ALU.subtract).then_inc(mask_split, 1)
            dve.wait_ge(wq_in, 48)
            dve.tensor_scalar(bq4[:], bqc[:], 0.25, None, ALU.mult).then_inc(dve_const, 1)
            dve.wait_ge(const_step, CONST_ALL)
            dve.tensor_copy(identb[:], ident[:]).then_inc(dve_const, 1)
            dve.tensor_copy(beforeb[:], before[:]).then_inc(dve_const, 1)
            dve.tensor_copy(onesb[:], ones[:]).then_inc(dve_const, 1)
            dve.tensor_copy(expert_no[:], iota_i[:, 0:E]).then_inc(dve_const, 1)
            dve.tensor_copy(blk_lim[:].rearrange("p a b -> p (a b)"), iota_i[:, 8:72]).then_inc(dve_const, 1)
            dve.tensor_scalar(tri[:].rearrange("p a b -> p (a b)"), iota_i[:, 72:136], 0.0, None, ALU.is_ge).then_inc(dve_const, 1)
            dve.tensor_copy(blk_no[:], iota_i[:, 136:136 + MAXBLK]).then_inc(dve_const, 1)
            dve.tensor_copy(pair_lim[:], iota_i[:, 192:192 + MAXBLK // 2]).then_inc(dve_const, 1)
            dve.wait_ge(dve_const, DVE_CONSTS)
            dve.wait_ge(mask_split, 1)

            def reduce_max(n, u):
                m = UNITS * n + u
                hp, t = u // 2, u % 2
                dve.wait_ge(mx_ready, m + 1)
                dve.tensor_reduce(NEG[:, n % 2, t, 2 * hp:2 * hp + 2],
                                  MXB[m % 2][:].rearrange("p (i s) -> p i s", i=2), AX.X, ALU.max,
                                  negate=True).then_inc(mx_reduced, 1)

            def split_max(n, half):
                neg = NEG[:, n % 2, :, 8 * half:8 * half + 8]
                dve.wait_ge(mx_reduced, UNITS * n + 8 * (half + 1))
                if n >= 1:
                    wait_misc(dve, f"NM{half}", n - 1)
                if n >= 1 or half == 1:
                    dve.wait_ge(neg_split[1 - half], n + half)
                link(dve.tensor_copy(NMS[:, half, :, 0, :], neg))
                link(dve.tensor_tensor(NR[:], neg, NMS[:, half, :, 0, :], ALU.subtract))
                link(dve.tensor_copy(NMS[:, half, :, 1, :], NR[:]))
                dve.tensor_tensor(NMS[:, half, :, 2, :], NR[:], NMS[:, half, :, 1, :], ALU.subtract).then_inc(neg_split[half], 1)

            def normalize_product(n, i):
                dve.wait_ge(av_done, UNITS * n + 8 * (i + 1))
                ins = dve.transpose(AVT[:].rearrange("p b c -> p (b c)"), AVB[i][:])
                ins.then_inc(av_taken, 1)
                dve.wait_ge(av_taken, 2 * n + i + 1)
                link(dve.reciprocal(RSUM[:], AVT[:, :, DH]))
                link(dve.tensor_tensor(AVN[:, :, i, :], AVT[:, :, 0:DH],
                                       RSUM[:].unsqueeze(2).broadcast_to([P, 16, DH]), ALU.mult))
                if i == 1:
                    if n >= 1:
                        wait_misc(dve, "WO", n - 1)
                    dve.transpose(ON[:], AVN[:].rearrange("p b i d -> p (b i d)")).then_inc(norm_done, 1)
                    dve.wait_ge(norm_done, n + 1)

            def normalize_product(n, i):
                dve.wait_ge(av_done, UNITS * n + 8 * (i + 1))
                ins = dve.transpose(AVT[:].rearrange("p b c -> p (b c)"), AVB[i][:])
                ins.then_inc(av_taken, 1)
                dve.wait_ge(av_taken, 2 * n + i + 1)
                link(dve.reciprocal(RSUM[:], AVT[:, :, DH]))
                link(dve.tensor_tensor(AVN[:, :, i, :], AVT[:, :, 0:DH],
                                       RSUM[:].unsqueeze(2).broadcast_to([P, 16, DH]), ALU.mult))
                if i == 1:
                    if n >= 1:
                        wait_misc(dve, "WO", n - 1)
                    dve.transpose(ON[:], AVN[:].rearrange("p b i d -> p (b i d)")).then_inc(norm_done, 1)
                    dve.wait_ge(norm_done, n + 1)

            def normalize2(n):
                q = n % 2
                dve.wait_ge(rs2_ready, n + 1)
                if n >= 2:
                    dve.wait_ge(scattered[q], 16 * TB * TOPK * (n // 2))
                for t in range(TB):
                    dve.tensor_scalar(R[:, q, t, 0, 0:D], X[:, TB * n + t, :], mv2[:, q, t, 0:1], rs2[:, q, t:t + 1],
                                      ALU.subtract, ALU.mult).then_inc(rows_ready, 1)

            def total_bias():
                wait_misc(dve, "BO", 0)
                dve.wait_ge(wq_in, 48)
                dve.tensor_tensor(bob[:], misc_bank("BO", 0)[:, 0:D], bob[:], ALU.add).then_inc(bias_ready, 1)

            def residual(n):
                wait_misc(dve, "WO", n)
                dve.wait_ge(xb_ready, n + 1)
                xs = X[:, TB * n:TB * (n + 1), :].rearrange("p t d -> p (t d)")
                dve.tensor_tensor(xs, misc_bank("WO", n)[:], xs, ALU.add).then_inc(xmid_ready, 1)
                dve.wait_ge(xmid_ready, n + 1)
                stats(n, X, bn2, mv2, stats2, rows_ready)

            def route_choice(n):
                q = n % 2
                wait_misc(dve, "LG", n)
                if n >= 1:
                    dve.wait_ge(ex_ready, n)
                    dve.wait_ge(pos_read, n)
                    dve.wait_ge(slot_ready, n)
                scores = misc_bank("LG", n)[:, 0:TB * E].rearrange("p (t e) -> p t e", e=E)
                for t in range(TB):
                    link(dve.max(top[:, t, :], scores[:, t, :]))
                dve.tensor_tensor(ls[:], top[:], top[:, :, 0:1].broadcast_to([P, TB, E]), ALU.subtract).then_inc(ls_ready, 1)
                for t in range(TB):
                    ins = dve.max_index(topi[:, t, :], top[:, t, :], scores[:, t, :])
                    ins.then_inc(lg_ready, 1)
                dve.wait_ge(lg_ready, TB * (n + 1))
                link(dve.tensor_copy(topf[:], topi[:, :, 0:TOPK]))
                link(dve.tensor_tensor(oh[:], topf[:].unsqueeze(3).broadcast_to([P, TB, TOPK, E]),
                                       expert_no[:].unsqueeze(1).unsqueeze(1).broadcast_to([P, TB, TOPK, E]), ALU.is_equal))
                if n >= 2:
                    wait_misc(dve, "PF", n - 2)
                dve.tensor_tensor(sel[:, q], oh[:, :, 0, :], oh[:, :, 1, :], ALU.add).then_inc(sel_ready, 1)
                dve.wait_ge(sel_ready, n + 1)
                dve.tensor_tensor(chosen[:, n, 1, :], chosen[:, n, 0, :], sel[:, q, 0, :], ALU.add).then_inc(chosen_ready, 1)
                dve.wait_ge(chosen_ready, 2 * n + 1)
                dve.tensor_tensor(chosen[:, n + 1, 0, :], chosen[:, n, 1, :], sel[:, q, 1, :], ALU.add).then_inc(chosen_ready, 1)

            def route_gates(n):
                q = n % 2
                dve.wait_ge(ex_ready, n + 1)
                if n >= 1:
                    dve.wait_ge(gates_ready, n)
                link(dve.tensor_reduce(sm[:], ex[:], AX.X, ALU.add))
                link(dve.reciprocal(rsm[:], sm[:]))
                if n >= 2:
                    dve.wait_ge(scattered[q], 16 * TB * TOPK * (n // 2))
                dve.tensor_tensor(R[:, q, :, :, D], ex[:, :, 0:TOPK], rsm[:].unsqueeze(2).broadcast_to([P, TB, TOPK]),
                                  ALU.mult).then_inc(gates_ready, 1)

            def route_slots(n):
                q = n % 2
                wait_misc(dve, "PF", n)
                earlier = misc_bank("PF", n)[:, 0:TB * E].rearrange("p (t e) -> p t e", e=E)
                dve.tensor_tensor(ohp[:], earlier.unsqueeze(2).broadcast_to([P, TB, TOPK, E]), oh[:], ALU.mult).then_inc(pos_read, 1)
                dve.wait_ge(pos_read, n + 1)
                link(dve.tensor_reduce(pos[:], ohp[:], AX.X, ALU.add))
                link(dve.tensor_scalar(lost[:], pos[:], float(CAP), float(SLOT_LOST), ALU.is_ge, ALU.mult))
                link(dve.scalar_tensor_tensor(out=slotf[:], in0=topf[:], scalar=float(CAP), in1=pos[:],
                                              op0=ALU.mult, op1=ALU.add))
                dve.tensor_tensor(slot[:, q], slotf[:], lost[:], ALU.add).then_inc(slot_ready, 1)

            for it in ITERATIONS:
                for u in range(UNITS):
                    if 0 <= it + 1 < B:
                        reduce_max(it + 1, u)
                    if u == 0 and 0 <= it < B:
                        split_max(it, 1)
                    if u == 1 and 0 <= it - 2:
                        route_slots(it - 2)
                    if u == 1 and 1 <= it + 3 < B:
                        stats1_of(it + 3)
                    if u == 2 and 0 <= it - 1:
                        normalize_product(it - 1, 1)
                    if u == 8 and 0 <= it - 1:
                        normalize2(it - 1)
                    if u == 6 and 0 <= it - 1:
                        residual(it - 1)
                    if u == 0 and it == -1:
                        bias_columns()
                    if u == BIAS_AT and it == -1:
                        total_bias()
                    if u == 8 and 0 <= it + 1 < B:
                        split_max(it + 1, 0)
                    if u == 10 and 0 <= it < B:
                        normalize_product(it, 0)
                    if u == 12 and 0 <= it - 1:
                        route_choice(it - 1)
                    if u == GATES_AT and 0 <= it - 1:
                        route_gates(it - 1)
                    if u == 15 and it == B:
                        route_slots(it - 1)

            wait_misc(dve, "CNT", 0)
            link(dve.tensor_scalar(cnt[:], misc_bank("CNT", 0)[:, 0:E], float(CAP), None, ALU.min))
            link(dve.tensor_tensor(cmp8[:], cnt[:].unsqueeze(2).broadcast_to([P, E, E]), blk_lim[:], ALU.is_gt))
            link(dve.tensor_reduce(nblk[:], cmp8[:], AX.X, ALU.add))
            link(dve.tensor_tensor(cum8[:], tri[:], nblk[:].unsqueeze(1).broadcast_to([P, E, E]), ALU.mult))
            link(dve.tensor_reduce(incl[:], cum8[:], AX.X, ALU.add))
            link(dve.tensor_tensor(le[:], incl[:].unsqueeze(1).broadcast_to([P, MAXBLK, E]),
                                   blk_no[:].unsqueeze(2).broadcast_to([P, MAXBLK, E]), ALU.is_le))
            link(dve.tensor_reduce(bexp[:], le[:], AX.X, ALU.add))
            link(dve.tensor_tensor(leb[:], le[:], nblk[:].unsqueeze(1).broadcast_to([P, MAXBLK, E]), ALU.mult))
            link(dve.tensor_reduce(bex[:], leb[:], AX.X, ALU.add))
            link(dve.scalar_tensor_tensor(out=btmp[:], in0=bexp[:], scalar=float(CAP // P), in1=blk_no[:],
                                          op0=ALU.mult, op1=ALU.add))
            link(dve.tensor_tensor(btmp2[:], btmp[:], bex[:], ALU.subtract))
            link(dve.tensor_scalar(table[:, 0, :], btmp2[:], float(P), None, ALU.mult))
            link(dve.tensor_scalar(bcl[:], bexp[:], float(E - 1), None, ALU.min))
            link(dve.tensor_scalar(table[:, 1, :], bcl[:], float(KC * 2 * FF), None, ALU.mult))
            link(dve.tensor_scalar(table[:, 2, :], bcl[:], float(FC * D), None, ALU.mult))
            link(dve.tensor_scalar(pcmp[:], pair_lim[:], incl[:, E - 1:E], None, ALU.is_lt))
            link(dve.tensor_reduce(pcnt[:], pcmp[:], AX.X, ALU.add))
            link(dve.tensor_copy(npairs[:, 0:1], pcnt[:]))
            dve.tensor_scalar(npairs[:, 1:2], pcnt[:], 2.0, -2.0, ALU.mult, ALU.add).then_inc(table_ready, 1)

            dve.wait_ge(table_ready, 1)
            pairs = dve.value_load(npairs[0:1, 0:1], min_val=8, max_val=MAXPAIR)
            last = dve.value_load(npairs[0:1, 1:2], min_val=14, max_val=2 * MAXPAIR - 2) + 1

            def rows_copy(t, u):
                dve.wait_ge(tx_ready, t + 1)
                if later(t, 2):
                    dve.wait_ge(h_ready, t - 1)
                dve.tensor_copy(XTG[:, u].rearrange("p k t -> p (k t)"), bank[0][:, 0:D]).then_inc(txe_ready, 1)

            def gates_copy(t, u):
                dve.wait_ge(xg_in[u], (t - u) * 8 + 16)
                if later(t, 2):
                    dve.wait_ge(added, (t - 1) * 16)
                dve.tensor_copy(GW[:, u, :], XG[:, u, D:D + 1]).then_inc(gw_ready, 1)
                dve.tensor_copy(GI[u][:], XG[:, u, D + 1:D + 2].bitcast(U32)).then_inc(gi_ready, 1)

            def gated(t, u):
                dve.wait_ge(sg_ready, t + 1)
                if later(t, 2):
                    dve.wait_ge(ht_ready, t - 1)
                dve.tensor_tensor(HM[:, u, :], bank[3 + 2 * u][:, 0:FF], SG[:, u, :], ALU.mult).then_inc(hm_ready, 1)

            def weigh(t, u):
                dve.wait_ge(y_ready, t + 1)
                dve.wait_ge(gw_ready, t + 1)
                if later(t, 2):
                    dve.wait_ge(added, (t - 1) * 16)
                dve.tensor_scalar(Y[:, u, :], bank[6 + u][:, 0:D], GW[:, u, 0:1], None, ALU.mult).then_inc(ys_ready, 1)

            def step(t, u):
                gates_copy(t, u)
                rows_copy(t + 1, 1 - u)
                gated(t, u)
                weigh(t - 1, 1 - u)

            rows_copy(0, 0)
            gates_copy(0, 0)
            rows_copy(1, 1)
            gated(0, 0)
            for t in range(1, PEELED):
                step(t, t % 2)
            with dve.Fori(0, pairs - PEELED // 2) as i:
                for u in range(2):
                    step(2 * i + PEELED + u, u)
            weigh(last, 1)


INPUTS = ["x", "ctx_1024", "mask_Bx1x1xS2_fk0", "L0_xattn_Wq", "L0_xattn_bq", "L0_xattn_Wk", "L0_xattn_bk",
          "L0_xattn_Wv", "L0_xattn_bv", "L0_xattn_Wo", "L0_xattn_bo", "L0_ffn_w_gate", "L0_ffn_c_fc", "L0_ffn_c_proj"]


def kernel(**inputs):
    import concourse.bacc as bacc
    from concourse.bass_utils import run_bass_kernel_spmd

    nc = bacc.Bacc("TRN2", target_bir_lowering=False, num_devices=1)
    arrays, args = {}, []
    for name in INPUTS:
        a = np.ascontiguousarray(inputs[name])
        arrays[f"in_{name}"] = a
        args.append(nc.dram_tensor(f"in_{name}", a.shape, mybir.dt.from_np(a.dtype), kind="ExternalInput").ap())
    out = nc.dram_tensor("out_0", (B, S, D), F32, kind="ExternalOutput").ap()
    program(nc, *args, out)
    r = run_bass_kernel_spmd(nc, [arrays], core_ids=[0])
    return r.results[0]["out_0"]
```

```python
from contextlib import ExitStack

import numpy as np

import concourse.bass as bass
from concourse import mybir

F32 = mybir.dt.float32
BF16 = mybir.dt.bfloat16
U32 = mybir.dt.uint32
I32 = mybir.dt.int32
ALU = mybir.AluOpType
ACT = mybir.ActivationFunctionType
AX = mybir.AxisListType

P = 128
B, S, D, H = 8, 256, 256, 16
DH = D // H
E, TOPK, CAP = 8, 2, 1024
FF = 384
NT = B * S // P
TB = S // P
KC = D // P
FC = FF // P
UNITS = 16
NPROB = 4
EPS = 1e-5
MASK_BIG = -1e9
RW = D + 2
PAD_TOK = B * S
XROWS = E * CAP + 3 * P
SLOT_LOST = 1 << 17
MAXPAIR = (B * S * TOPK // P + E - 1 + 1) // 2
MAXBLK = 2 * MAXPAIR + 2

LATE = 4
PADS = 15
AHEAD = 8
KNOWN = B - 2
PEELED = AHEAD
RESTBLK = MAXBLK - AHEAD

MATCH_K = (0, 1, 0)
MATCH_Q = (1, 0, 0)
ROWS3 = 3 * DH
KQ_LOADS = 9
R_MASK = 6 * DH
R_MAX = R_MASK + 3
R_END = R_MAX + 3


AT = {
    "PF": 2, "NM1": 1, "WO": 4, "V": 7, "NM0": 11, "X2": 11, "LG": 12,
    "X2 of the last": 10, "LG of the last": 11, "CNT": 1, "BO": 5,
    "CT": 0, "XT": 1, "K": 3, "Q": 4,
    "second K": 5, "second Q": 6,
    "copy rows": 10, "max rows 0": 11, "max rows 1": 4, "gate exps": 13,
    "split 0": 7, "split 1": 0, "slots": 2, "stats1": 1, "product 0": 10, "product 1": 2,
    "residual": 6, "normalize2": 8, "choice": 12, "gates": 15, "table": 2,
    "start of 1": 7,
    "values": 2,
}
MISC_PLAN = (("PF", -2), ("NM1", 0), ("WO", -1), ("V", 1), ("NM0", 1), ("X2", -1), ("LG", -1))
PROJECTION = ("CT", "XT", "K", "Q")
ITERATIONS = range(-2, B + 1)


def projected(it):
    if it == -2:
        return ((0, 0), (1, AT["start of 1"]))
    return ((it + 2, 0),) if 0 <= it < B - 2 else ()


def projected_at(it, unit, after):
    return [n for n, start in projected(it) if unit == start + after]


def misc_at(it, unit):
    def at(kind):
        return AT[kind + " of the last"] if it == B - 1 and kind in ("X2", "LG") else AT[kind]

    pieces = [(kind, n) for n, start in projected(it) for kind in PROJECTION if start + AT[kind] == unit]
    if it == 0 and unit == AT["BO"]:
        pieces.append(("BO", 0))
    pieces += [(kind, it + rel) for kind, rel in MISC_PLAN if unit == at(kind) and 0 <= it + rel < B]
    if it == B - 1 and unit == AT["CNT"]:
        pieces.append(("CNT", KNOWN))
    if it == B and unit == UNITS - 1:
        pieces.append(("PF", B - 1))
    return pieces


MISC_ORDER = [piece for it in ITERATIONS for u in range(UNITS) for piece in misc_at(it, u)] + [("CNT", B)]
MISC_NO = {piece: k for k, piece in enumerate(MISC_ORDER)}


def by_chunk(ap):
    return ap.rearrange("p (c t) -> p c t", c=KC)


def later(t, least):
    return not isinstance(t, int) or t >= least


def program(nc, x, ctx_in, mask, Wq, bq, Wk, bk, Wv, bv, Wo, bo, w_gate, c_fc, c_proj, out):
    x_t = x.rearrange("b (t p) d -> b p t d", p=P)
    c_t = ctx_in.rearrange("b (t p) d -> b p t d", p=P)
    out_rows = out.rearrange("b s d -> (b s) d")
    out_t = out.rearrange("b (t p) d -> b p t d", p=P)

    slots = nc.dram_tensor("slots", (XROWS, RW), F32, kind="Internal").ap()
    mparts_d = nc.dram_tensor("mparts_d", (B, 3, S), BF16, kind="Internal").ap()
    kparts_d = [nc.dram_tensor(f"kparts_d{i}", (KC, P, 3, S), BF16, kind="Internal").ap() for i in range(2)]
    qparts_d = [nc.dram_tensor(f"qparts_d{i}", (KC, P, 3, S), BF16, kind="Internal").ap() for i in range(2)]

    with ExitStack() as es:
        def sb(name, shape, dt=F32):
            return es.enter_context(nc.sbuf_tensor(name, shape, dt))

        def sem(name):
            return es.enter_context(nc.semaphore(name))

        bank = [es.enter_context(nc.psum_tensor(f"bank{i}", [P, 512], F32)) for i in range(8)]
        MXB, STB, AVB, MISC = bank[0:2], bank[2:4], bank[4:6], bank[6:8]

        X = sb("X", [P, NT, D])
        C = sb("C", [P, 3 * TB, D])
        wq = sb("wq", [P, KC, D]); wk = sb("wk", [P, KC, D]); wv = sb("wv", [P, KC, D])
        wo = sb("wo", [P, 2, D])
        wg = sb("wg", [P, KC, E])
        wf = sb("wf", [P, E * KC * 2 * FF])
        QS = wf[:, (E - LATE) * KC * 2 * FF:].bitcast(BF16).rearrange("p (r h s) -> p r h s", r=3, h=H)
        wp = sb("wp", [P, E * FC * D])
        bvc = sb("bvc", [P, 2]); bvm = sb("bvm", [P, 2, P])
        bqc = sb("bqc", [P, KC]); bq4 = sb("bq4", [P, KC]); bkc = sb("bkc", [P, KC])
        bob = sb("bob", [P, D])
        ident = sb("ident", [P, P]); identb = sb("identb", [P, P], BF16)
        before = sb("before", [P, P]); ones = sb("ones", [P, P])
        beforeb = sb("beforeb", [P, P], BF16); onesb = sb("onesb", [P, P], BF16)
        mhalf = sb("mhalf", [P, TB])
        iota_i = sb("iota_i", [P, 256], I32)
        expert_no = sb("expert_no", [P, E]); blk_lim = sb("blk_lim", [P, E, E]); tri = sb("tri", [P, E, E])
        blk_no = sb("blk_no", [P, RESTBLK]); pair_lim = sb("pair_lim", [P, RESTBLK // 2])
        tok_no = sb("tok_no", [P, NT], U32)
        pad_row = sb("pad_row", [P, RW])
        mparts = sb("mparts", [B, 3, S], BF16)
        bn1 = sb("bn1", [P, TB, 6]); mv1 = sb("mv1", [P, 2, TB, 2]); rs1 = sb("rs1", [P, 2, TB])
        bn2 = sb("bn2", [P, TB, 6]); mv2 = sb("mv2", [P, 2, TB, 2]); rs2 = sb("rs2", [P, 2, TB])
        XN = sb("XN", [P, 2, TB, D])
        CTt = sb("CTt", [P, 2, KC, S]); XTt = sb("XTt", [P, 2, KC, S])
        KF = sb("KF", [P, 2, KC * S]); QF = sb("QF", [P, 2, KC * S])
        KREST = sb("KREST", [P, KC * S]); QREST = sb("QREST", [P, KC * S])
        KP = sb("KP", [P, KC, 3, S], BF16); QP = sb("QP", [P, KC, 3, S], BF16)
        KS = sb("KS", [P, 3, H, S], BF16)
        VA = sb("VA", [P, 2, TB, H, 32])
        PR = sb("PR", [P, NPROB, 512])
        NEG = sb("NEG", [P, 2, TB, H]); NR = sb("NR", [P, TB, 8])
        NMS = sb("NMS", [P, 2, TB, 3, 8], BF16); NMT = sb("NMT", [24, 2, S], BF16)
        AVT = sb("AVT", [P, 16, 32])
        RSUM = sb("RSUM", [P, 16]); AVN = sb("AVN", [P, 16, 2, DH])
        ON = sb("ON", [P, 512])
        R = sb("R", [P, 2, TB, TOPK, RW])
        X2T = sb("X2T", [P, KC, S])
        ls = sb("ls", [P, TB, E]); ex = sb("ex", [P, TB, E])
        sm = sb("sm", [P, TB]); rsm = sb("rsm", [P, TB])
        top = sb("top", [P, TB, 8]); topi = sb("topi", [P, TB, 8], U32); topf = sb("topf", [P, TB, TOPK])
        oh = sb("oh", [P, TB, TOPK, E]); sel = sb("sel", [P, 2, TB, E], BF16)
        chosen = sb("chosen", [P, B + 1, TB, E], BF16)
        ohp = sb("ohp", [P, TB, TOPK, E]); pos = sb("pos", [P, TB, TOPK])
        lost = sb("lost", [P, TB, TOPK]); slotf = sb("slotf", [P, TB, TOPK])
        slot = sb("slot", [P, 2, TB, TOPK], U32)
        cnt = sb("cnt", [P, E]); cmp8 = sb("cmp8", [P, E, E]); nblk = sb("nblk", [P, E])
        cum8 = sb("cum8", [P, E, E]); incl = sb("incl", [P, E])
        full = sb("full", [P, E]); before8 = sb("before8", [P, E]); taken = sb("taken", [P, E + 1])
        taken_incl = sb("taken_incl", [P, E]); taken_excl = sb("taken_excl", [P, E]); more = sb("more", [P, E]); weight8 = sb("weight8", [P, E])
        bexp = sb("bexp", [P, RESTBLK]); bex = sb("bex", [P, RESTBLK]); bcl = sb("bcl", [P, RESTBLK])
        btmp = sb("btmp", [P, RESTBLK]); btmp2 = sb("btmp2", [P, RESTBLK])
        pcmp = sb("pcmp", [P, RESTBLK // 2]); pcnt = sb("pcnt", [P, 1])
        table = sb("table", [P, 3, MAXBLK], I32); npairs = sb("npairs", [P, 2], I32)
        GW = sb("GW", [P, 2, 1]); GI0 = sb("GI0", [P, 1], U32); GI1 = sb("GI1", [P, 1], U32)
        GI = (GI0, GI1)
        XG = sb("XG", [P, 2, RW])
        LE = sb("LE", [P, RESTBLK * E]); LEB = sb("LEB", [P, RESTBLK * E])
        MASKBUF = PR[0:B, 0:3, 0:S]
        maskrow, mres, mres2 = MASKBUF[:, 0, :], MASKBUF[:, 1, :], MASKBUF[:, 2, :]
        le = LE[:].rearrange("p (b e) -> p b e", e=E)
        leb = LEB[:].rearrange("p (b e) -> p b e", e=E)
        XTG = XN[:, :, 0, :].rearrange("p u (k t) -> p u k t", k=KC)
        SG, HM = KF[:, :, 0:FF], QF[:, :, 0:FF]
        HT = XTt[:].rearrange("p u c s -> p u (c s)")[:, :, 0:FF].rearrange("p u (c t) -> p u c t", c=FC)
        Y = CTt[:, :, 0, :]

        x_in = [sem(f"x_in{n}") for n in range(B)]
        c_in = [sem(f"c_in{n}") for n in range(B)]
        wkv_in = sem("wkv_in"); wq_in = sem("wq_in"); wrest_in = sem("wrest_in"); mask_in = sem("mask_in")
        slots_padded = sem("slots_padded")
        const_step = sem("const_step")
        dve_const = sem("dve_const")
        dve_step = sem("dve_step")
        qs_ones = sem("qs_ones"); ks_ones = sem("ks_ones"); va_ones = sem("va_ones")
        mask_split = sem("mask_split"); mask_out = sem("mask_out")
        stats1 = sem("stats1")
        var1_ready = sem("var1_ready"); xn_ready = sem("xn_ready"); xb_ready = sem("xb_ready")
        misc_ready = sem("misc_ready")
        ct_ready = sem("ct_ready"); xt_ready = sem("xt_ready")
        kf_ready = sem("kf_ready"); qf_ready = sem("qf_ready"); v_ready = sem("v_ready")
        bvm_ready = sem("bvm_ready"); bias_ready = sem("bias_ready")
        kp0_ready = sem("kp0_ready"); qp0_ready = sem("qp0_ready")
        krest_ready = sem("krest_ready"); qrest_ready = sem("qrest_ready")
        kp1_ready = sem("kp1_ready"); qp1_ready = sem("qp1_ready")
        kp_ready = sem("kp_ready"); qp_ready = sem("qp_ready")
        kd_out = [sem(f"kd_out{i}") for i in range(2)]
        qd_out = [sem(f"qd_out{i}") for i in range(2)]
        kq_in = [sem(f"kq_in{i}") for i in range(3)]
        mx_ready = sem("mx_ready"); mx_reduced = sem("mx_reduced")
        neg_split = [sem("neg_split0"), sem("neg_split1")]
        nmt_ready = [sem("nmt_ready0"), sem("nmt_ready1")]
        nm_in = [sem("nm_in0"), sem("nm_in1")]
        st_ready = sem("st_ready"); exp_done = sem("exp_done"); av_done = sem("av_done")
        av_taken = sem("av_taken"); norm_done = sem("norm_done")
        xmid_ready = sem("xmid_ready"); out_stored = [sem("known_out_stored"), sem("rest_out_stored")]
        stats2 = sem("stats2"); rs1_ready = sem("rs1_ready"); rs2_ready = sem("rs2_ready")
        var2_ready = sem("var2_ready"); rows_ready = sem("rows_ready"); rows_copied = sem("rows_copied")
        x2t_ready = sem("x2t_ready"); lg_ready = sem("lg_ready"); ls_ready = sem("ls_ready")
        ex_ready = sem("ex_ready"); sel_ready = sem("sel_ready"); chosen_ready = sem("chosen_ready"); gates_ready = sem("gates_ready")
        pos_read = sem("pos_read"); slot_ready = sem("slot_ready"); scattered = [sem("scattered0"), sem("scattered1")]
        we_in = sem("we_in"); numbers_ready = sem("numbers_ready")
        table_ready = sem("table_ready"); ahead_ready = sem("ahead_ready"); rest_ready = sem("rest_ready"); cnt_read = sem("cnt_read")
        xg_in = [sem("xg_in0"), sem("xg_in1")]
        tx_ready = sem("tx_ready"); txe_ready = sem("txe_ready"); gw_ready = sem("gw_ready"); gi_ready = sem("gi_ready")
        h_ready = sem("h_ready"); sg_ready = sem("sg_ready"); hm_ready = sem("hm_ready")
        ht_ready = sem("ht_ready"); hte_ready = sem("hte_ready")
        y_ready = sem("y_ready"); ys_ready = sem("ys_ready"); added = sem("added")

        EVACUATED = {"CT": ct_ready, "XT": xt_ready, "K": kf_ready, "Q": qf_ready, "V": v_ready,
                     "NM0": nmt_ready[0], "NM1": nmt_ready[1], "WO": xmid_ready, "X2": x2t_ready,
                     "LG": lg_ready, "BO": bias_ready, "CNT": cnt_read, "PF": pos_read}

        def misc_bank(kind, n):
            return MISC[MISC_NO[kind, n] % 2]

        def wait_misc(eng, kind, n):
            eng.wait_ge(misc_ready, MISC_NO[kind, n] + 1)

        CONST_IDENT = 2
        CONST_ALL = 13
        DVE_CONSTS = 10

        def normalize1(eng, n):
            q = n % 2
            eng.wait_ge(rs1_ready, n + 1)
            if n >= 1:
                eng.wait_ge(xn_ready, TB * n)
            if n >= 2:
                wait_misc(eng, "XT", n - 2)
            for t in range(TB):
                eng.tensor_scalar(XN[:, q, t, :], X[:, TB * n + t, :], mv1[:, q, t, 0:1], rs1[:, q, t:t + 1],
                                  ALU.subtract, ALU.mult).then_inc(xn_ready, 1)

        def first_rest(eng, n, full, parts, rest, first_ready, rest_ready, done):
            q = n % 2
            eng.wait_ge(first_ready, n + 1)
            if n >= 1:
                eng.wait_ge(done, n)
            eng.tensor_tensor(by_chunk(rest[:]), by_chunk(full[:, q, :]), parts[:, :, 0, :], ALU.subtract).then_inc(rest_ready, 1)

        def last_part(eng, n, parts, rest, second_ready, done):
            eng.wait_ge(second_ready, n + 1)
            eng.tensor_tensor(parts[:, :, 2, :], by_chunk(rest[:]), parts[:, :, 1, :], ALU.subtract).then_inc(done, 1)

        def split(eng, n):
            first_rest(eng, n, KF, KP, KREST, kp0_ready, krest_ready, kp_ready)
            first_rest(eng, n, QF, QP, QREST, qp0_ready, qrest_ready, qp_ready)
            last_part(eng, n, KP, KREST, kp1_ready, kp_ready)
            last_part(eng, n, QP, QREST, qp1_ready, qp_ready)

        block = es.enter_context(nc.Block())

        @block.sync
        def _(sp):
            def load_context(n):
                if n >= 3:
                    wait_misc(sp, "CT", n - 3)
                r = n % 3
                sp.dma_start(C[:, TB * r:TB * (r + 1), :], c_t[n]).then_inc(c_in[n], 16)

            load_context(0)
            sp.dma_start(wk[:], Wk.rearrange("(k p) n -> p k n", p=P)).then_inc(wkv_in, 16)
            sp.dma_start(X[:, 0:TB, :], x_t[0]).then_inc(x_in[0], 16)
            sp.dma_start(bkc[:], bk.rearrange("(c p) -> p c", p=P), allow_slow_non_contiguous=True).then_inc(wkv_in, 16)
            sp.dma_start(wq[:], Wq.rearrange("(k p) n -> p k n", p=P)).then_inc(wq_in, 16)
            sp.dma_start(bqc[:], bq.rearrange("(c p) -> p c", p=P), allow_slow_non_contiguous=True).then_inc(wq_in, 16)
            sp.dma_start(maskrow[:], mask.rearrange("b i j s -> b (i j s)")).then_inc(mask_in, 16)
            sp.dma_start(wv[:], Wv.rearrange("(k p) n -> p k n", p=P)).then_inc(wkv_in, 16)
            sp.dma_start(bob[:], bo.partition_broadcast(P)).then_inc(wq_in, 16)
            for n in range(1, B):
                sp.dma_start(X[:, TB * n:TB * (n + 1), :], x_t[n]).then_inc(x_in[n], 16)
                if n < 3:
                    load_context(n)
            sp.wait_ge(mask_split, 1)
            sp.dma_start(mparts_d, mparts[:]).then_inc(mask_out, 16)

            def load_rest():
                for j in range(4):
                    for i in range(2):
                        sp.dma_start(wo[32 * j + DH * i:32 * j + DH * (i + 1), :, :],
                                     Wo.rearrange("(i g j d) n -> j i d g n", i=2, g=2, d=DH)[j, i]).then_inc(wrest_in, 16)
                        sp.dma_start(bvc[32 * j + DH * i:32 * j + DH * (i + 1), :],
                                     bv.rearrange("(i g j d) -> j i d g", i=2, g=2, d=DH)[j, i],
                                     allow_slow_non_contiguous=True).then_inc(wrest_in, 16)
                sp.dma_start(wg[:], w_gate.rearrange("(k p) e -> p k e", p=P), allow_slow_non_contiguous=True).then_inc(wrest_in, 16)

            def load_up(e):
                sp.dma_start(wf[:, e * KC * 2 * FF:(e + 1) * KC * 2 * FF].rearrange("p (k f) -> p k f", k=KC),
                             c_fc[e].rearrange("(k p) f -> p k f", p=P)).then_inc(we_in, 16)

            late_after = {}
            for e in range(E - LATE, E):
                start, size = (e - (E - LATE)) * KC * 2 * FF * 4, H * S * 2
                places = range(start // size, (start + KC * 2 * FF * 4 - 1) // size + 1)
                late_after[e] = max(n for n in range(B) if n % 3 in places)

            for it in ITERATIONS[:-1]:
                if it == -1:
                    load_rest()
                if 3 <= it + 3 < B:
                    load_context(it + 3)
                for n, _ in projected(it):
                    if n >= 3:
                        sp.wait_ge(st_ready, UNITS * (n - 2))
                    if n < 3:
                        sp.wait_ge(qs_ones, n + 1)
                        sp.wait_ge(ks_ones, n + 1)
                    if n == 0:
                        sp.wait_ge(mask_out, 16)
                    sp.dma_start(KS[R_MASK:R_MAX, n % 3, :, :],
                                 mparts_d[n].unsqueeze(1).broadcast_to([3, H, S])).then_inc(kq_in[n % 3], 16)
                    for parts, ready, back, dram in ((KP, kp_ready, kd_out, kparts_d), (QP, qp_ready, qd_out, qparts_d)):
                        sp.wait_ge(ready, n + 1)
                        if n >= 2:
                            sp.wait_ge(kq_in[(n - 2) % 3], KQ_LOADS * 16 * ((n - 2) // 3 + 1))
                        sp.dma_start(dram[n % 2].rearrange("c p j t -> p c (j t)"),
                                     parts[:].rearrange("p c j t -> p c (j t)")).then_inc(back[n % 2], 16)
                    for dst, own, other, match, back, dram in ((KS, ROWS3, 0, MATCH_K, kd_out, kparts_d),
                                                               (QS, 0, ROWS3, MATCH_Q, qd_out, qparts_d)):
                        sp.wait_ge(back[n % 2], 16 * (n // 2 + 1))
                        sp.dma_start(dst[own:own + ROWS3, n % 3, :, :],
                                     dram[n % 2].rearrange("c (h d) j t -> (d j) (c h) t", d=DH)).then_inc(kq_in[n % 3], 16)
                        for j in range(3):
                            sp.dma_start(dst[other + j:other + ROWS3:3, n % 3, :, :],
                                         dram[n % 2][:, :, match[j]].rearrange("c (h d) t -> d (c h) t", d=DH)).then_inc(kq_in[n % 3], 16)
                if 0 <= it - 1:
                    sp.wait_ge(xmid_ready, it)
                    sp.dma_start(out_t[it - 1], X[:, TB * (it - 1):TB * it, :]).then_inc(out_stored[it - 1 >= KNOWN], 16)
                if 0 <= it < B:
                    if it < E - LATE:
                        load_up(it)
                    for e in range(E - LATE, E):
                        if late_after[e] == it - 1:
                            sp.wait_ge(st_ready, UNITS * it)
                            load_up(e)
                    sp.dma_start(wp[:, it * FC * D:(it + 1) * FC * D].rearrange("p (k d) -> p k d", k=FC),
                                 c_proj[it].rearrange("(k p) d -> p k d", p=P)).then_inc(we_in, 16)
            def load_block(t, u):
                if later(t, 2):
                    sp.wait_ge(tx_ready, t - 1)
                    sp.wait_ge(gi_ready, t - 1)
                row = sp.value_load(table[0:1, 0, bass.ds(t, 1)], min_val=0, max_val=XROWS - P)
                sp.dma_start(XG[:, u, :], slots[bass.ds(row, P), :]).then_inc(xg_in[u], 16)

            sp.wait_ge(ahead_ready, 1)
            for i in range(2):
                sp.wait_ge(scattered[i], 16 * TB * TOPK * (KNOWN // 2))
            load_block(0, 0)
            load_block(1, 1)
            sp.wait_ge(st_ready, UNITS * B)
            for e in range(E - LATE, E):
                if late_after[e] == B - 1:
                    load_up(e)
            sp.wait_ge(xmid_ready, B)
            sp.dma_start(out_t[B - 1], X[:, TB * (B - 1):TB * B, :]).then_inc(out_stored[1], 16)
            for t in range(2, AHEAD):
                load_block(t, t % 2)
            sp.wait_ge(table_ready, 1)
            for i in range(2):
                sp.wait_ge(scattered[i], 16 * TB * TOPK * (B // 2))
            pairs = sp.value_load(npairs[0:1, 0:1], min_val=8, max_val=MAXPAIR)
            load_block(PEELED, 0)
            with sp.Fori(0, pairs - PEELED // 2) as i:
                for u in range(2):
                    load_block(2 * i + PEELED + 1 + u, 1 - u)
            sp.wait_ge(out_stored[0], 16 * KNOWN)
            sp.wait_ge(out_stored[1], 16 * (B - KNOWN))

        @block.gpsimd
        def _(pool):
            def const(ins):
                ins.then_inc(const_step, 1)
                const.n += 1
                pool.wait_ge(const_step, const.n)
            const.n = 0
            const(pool.memset(ident[:], 0.0))
            const(pool.affine_select(out=ident[:], in_=ident[:], compare_op=ALU.not_equal, fill=1.0,
                                     base=0, pattern=[[-1, P]], channel_multiplier=1))
            const(pool.memset(ones[:], 1.0))
            const(pool.affine_select(out=before[:], in_=ones[:], compare_op=ALU.is_gt, fill=0.0,
                                     base=0, pattern=[[1, P]], channel_multiplier=-1))
            const(pool.memset(mhalf[:], -0.5))
            const(pool.iota(iota_i[:, 0:E], [[1, E]], base=0, channel_multiplier=0))
            const(pool.iota(iota_i[:, 8:72], [[0, E], [P, E]], base=0, channel_multiplier=0))
            const(pool.iota(iota_i[:, 72:136], [[1, E], [-1, E]], base=0, channel_multiplier=0))
            const(pool.iota(iota_i[:, 136:136 + RESTBLK], [[1, RESTBLK]], base=0, channel_multiplier=0))
            const(pool.iota(iota_i[:, 192:192 + RESTBLK // 2], [[2, RESTBLK // 2]], base=0, channel_multiplier=0))
            const(pool.iota(tok_no[:], [[P, NT]], base=0, channel_multiplier=1))
            const(pool.memset(pad_row[:, 0:D + 1], 0.0))
            const(pool.iota(pad_row[:, D + 1:D + 2].bitcast(U32), [[0, 1]], base=PAD_TOK, channel_multiplier=0))
            assert const.n == CONST_ALL

            def layernorm1(n):
                q = n % 2
                pool.wait_ge(stats1, TB * (n + 1))
                pool.tensor_scalar(rs1[:, q, :], mv1[:, q, :, 1], EPS, None, ALU.add).then_inc(var1_ready, 1)
                pool.wait_ge(var1_ready, n + 1)
                pool.tensor_tensor(rs1[:, q, :], rs1[:, q, :], mhalf[:], ALU.pow).then_inc(rs1_ready, 1)

            def add_output_bias(n):
                pool.wait_ge(bias_ready, 1)
                pool.wait_ge(xn_ready, TB * (n + 1))
                xs = X[:, TB * n:TB * (n + 1), :]
                pool.tensor_tensor(xs, xs, bob[:].unsqueeze(1).broadcast_to([P, TB, D]), ALU.add).then_inc(xb_ready, 1)

            def layernorm2(n):
                q = n % 2
                pool.wait_ge(stats2, TB * (n + 1))
                pool.tensor_scalar(rs2[:, q, :], mv2[:, q, :, 1], EPS, None, ALU.add).then_inc(var2_ready, 1)
                pool.wait_ge(var2_ready, n + 1)
                pool.tensor_tensor(rs2[:, q, :], rs2[:, q, :], mhalf[:], ALU.pow).then_inc(rs2_ready, 1)

            def scatter(n):
                q = n % 2
                if n == 0:
                    pool.wait_ge(slots_padded, 16 * PADS)
                if n >= 2:
                    pool.wait_ge(scattered[q], 16 * TB * TOPK * (n // 2))
                pool.tensor_copy(R[:].bitcast(U32)[:, q, :, :, D + 1],
                                 tok_no[:, TB * n:TB * (n + 1)].unsqueeze(2).broadcast_to([P, TB, TOPK])).then_inc(numbers_ready, 1)
                pool.wait_ge(numbers_ready, n + 1)
                pool.wait_ge(gates_ready, n + 1)
                pool.wait_ge(rows_copied, n + 1)
                pool.wait_ge(slot_ready, n + 1)
                for t in range(TB):
                    for k in range(TOPK):
                        pool.indirect_dma_start(
                            slots, bass.IndirectOffsetOnAxis(ap=slot[:, q, t, k:k + 1], axis=0),
                            R[:, q, t, k, :], None, bounds_check=E * CAP - 1, oob_is_err=False).then_inc(scattered[q], 16)

            def ones_rows(slot_no):
                two = float(np.array([0x3F803F80], np.uint32).view(np.float32)[0])
                if slot_no == 0:
                    pool.wait_ge(rs1_ready, 1)
                elif slot_no == 1:
                    pool.wait_ge(xn_ready, 2 * TB)
                for dst, done in ((KS, ks_ones), (QS, qs_ones)):
                    pool.memset(dst[R_MASK:P, slot_no].rearrange("p h s -> p (h s)").bitcast(F32), two).then_inc(done, 1)
                    pool.wait_ge(done, slot_no + 1)

            layernorm1(0)
            ones_rows(0)
            for it in ITERATIONS[:-1]:
                if it == -2:
                    layernorm1(1)
                    normalize1(pool, 1)
                for n, _ in projected(it):
                    if n >= 2:
                        split(pool, n)
                    else:
                        ones_rows(n + 1)
                if it >= B - 2:
                    scatter(it - 2)
                if 0 <= it - 1:
                    layernorm2(it - 1)
                if 2 <= it < B - 2:
                    scatter(it - 2)
                if 2 <= it + 3 < B:
                    layernorm1(it + 3)
                    normalize1(pool, it + 3)
                if 0 <= it < B:
                    add_output_bias(it)
            scatter(B - 2)
            layernorm2(B - 1)

            no_row, last_row = pool.alloc_register("no_row"), pool.alloc_register("last_row")
            pool.reg_mov(no_row, 0)

            def add_block(t, u):
                if later(t, 1):
                    pool.wait_ge(added, t * 16)
                pool.wait_ge(ys_ready, t + 1)
                pool.reg_add(last_row, no_row, B * S - 1)
                pool.indirect_dma_start(out_rows, bass.IndirectOffsetOnAxis(ap=GI[u][:], axis=0), Y[:, u, :], None,
                                        bounds_check=last_row, oob_is_err=False,
                                        compute_op=ALU.add).then_inc(added, 16)

            pool.wait_ge(out_stored[0], 16 * KNOWN)
            add_block(0, 0)
            scatter(B - 1)
            for t in range(1, PEELED):
                add_block(t, t % 2)
            pool.wait_ge(out_stored[1], 16 * (B - KNOWN))
            pool.wait_ge(table_ready, 1)
            pairs = pool.value_load(npairs[0:1, 0:1], min_val=8, max_val=MAXPAIR)
            with pool.Fori(0, pairs - PEELED // 2) as i:
                for u in range(2):
                    add_block(2 * i + PEELED + u, u)
            pool.wait_ge(added, pairs * 32)

        @block.scalar
        def _(act):
            act.wait_ge(const_step, CONST_ALL)

            def evacuate(kind, n):
                wait_misc(act, kind, n)
                src = misc_bank(kind, n)
                q = n % 2
                if kind in ("CT", "XT"):
                    dst, ready = (CTt, ct_ready) if kind == "CT" else (XTt, xt_ready)
                    if n >= 2:
                        wait_misc(act, "V" if kind == "CT" else "Q", n - 2)
                    act.activation(dst[:, q].rearrange("p c s -> p (c s)"), src[:], ACT.Copy).then_inc(ready, 1)
                elif kind in ("K", "Q"):
                    dst, bias, scale, done, ready = ((KF, bkc, 1.0, kp_ready, kf_ready) if kind == "K" else
                                                     (QF, bq4, 0.25, qp_ready, qf_ready))
                    if n >= 2:
                        act.wait_ge(done, n - 1)
                    if n == 0 and kind == "K":
                        act.wait_ge(wkv_in, 48)
                    if n == 0 and kind == "Q":
                        act.wait_ge(dve_const, DVE_CONSTS)
                    for c in range(KC):
                        ins = act.activation(dst[:, q, c * S:(c + 1) * S], src[:, c * S:(c + 1) * S], ACT.Identity,
                                             bias=bias[:, c:c + 1], scale=scale)
                    ins.then_inc(ready, 1)
                    parts, copied, first_ready = (KP, kd_out, kp0_ready) if kind == "K" else (QP, qd_out, qp0_ready)
                    act.wait_ge(ready, n + 1)
                    if n >= 1:
                        act.wait_ge(copied[1 - q], 16 * ((n + 1) // 2))
                    act.activation(parts[:, :, 0, :], by_chunk(dst[:, q, :]), ACT.Copy).then_inc(first_ready, 1)
                elif kind in ("NM0", "NM1"):
                    half = int(kind[2])
                    if n >= 1:
                        act.wait_ge(nm_in[half], 48 * n)
                    act.activation(NMT[:, half, :], src[0:24, 0:S // 2].bitcast(BF16), ACT.Copy).then_inc(nmt_ready[half], 1)
                elif kind == "V":
                    if n >= 2:
                        act.wait_ge(av_done, UNITS * (n - 1))
                    act.activation(VA[:, n % 2, :, :, 0:DH], src[:].rearrange("p (t h d) -> p t h d", t=TB, d=DH),
                                   ACT.Copy).then_inc(v_ready, 1)
                elif kind == "X2":
                    if n >= 1:
                        wait_misc(act, "LG", n - 1)
                    act.activation(X2T[:].rearrange("p c s -> p (c s)"), src[:], ACT.Copy).then_inc(x2t_ready, 1)

            def max_rows(n, half):
                act.wait_ge(nmt_ready[half], n + 1)
                if n >= 3:
                    act.wait_ge(st_ready, UNITS * (n - 2))
                if n < 3:
                    act.wait_ge(qs_ones, n + 1)
                for j in range(3):
                    act.dma_start(QS[R_MAX + j:R_MAX + j + 1, n % 3, 8 * half:8 * half + 8, :],
                                  NMT[8 * j:8 * j + 8, half, :]).then_inc(nm_in[half], 16)

            def second_part(n, parts, rest, rest_ready, copied, done):
                act.wait_ge(rest_ready, n + 1)
                if n >= 1:
                    act.wait_ge(copied[(n - 1) % 2], 16 * ((n + 1) // 2))
                act.activation(parts[:, :, 1, :], by_chunk(rest[:]), ACT.Copy).then_inc(done, 1)

            def copy_rows(n):
                q = n % 2
                act.wait_ge(rows_ready, TB * (n + 1))
                if n >= 2:
                    act.wait_ge(scattered[q], 16 * TB * TOPK * (n // 2))
                act.activation(R[:, q, :, 1, 0:D], R[:, q, :, 0, 0:D], ACT.Copy).then_inc(rows_copied, 1)

            pad_rows = slots.rearrange("(n p) f -> p n f", p=P)

            def pad_slots(k):
                a, b = XROWS // P * k // PADS, XROWS // P * (k + 1) // PADS
                act.dma_start(pad_rows[:, a:b], pad_row[:].unsqueeze(1).broadcast_to([P, b - a, RW])).then_inc(slots_padded, 16)

            def exponentials(n, u):
                s = UNITS * n + u
                act.wait_ge(st_ready, s + 1)
                if s >= NPROB:
                    act.wait_ge(av_done, s - NPROB + 1)
                act.activation(PR[:, s % NPROB, :], STB[s % 2][:], ACT.Exp).then_inc(exp_done, 1)

            def router_exponentials(n):
                act.wait_ge(ls_ready, n + 1)
                if n >= 1:
                    act.wait_ge(gates_ready, n)
                act.activation(ex[:], ls[:], ACT.Exp).then_inc(ex_ready, 1)

            for it in ITERATIONS[:-1]:
                for u in range(UNITS):
                    for n in projected_at(it, u, AT["second Q"]):
                        second_part(n, QP, QREST, qrest_ready, qd_out, qp1_ready)
                    if 0 <= it < B:
                        exponentials(it, u)
                    for n in projected_at(it, u, AT["second K"]):
                        second_part(n, KP, KREST, krest_ready, kd_out, kp1_ready)
                    for kind, n in misc_at(it, u):
                        if kind in ("CT", "XT", "K", "Q", "V", "NM0", "NM1", "X2"):
                            evacuate(kind, n)
                    if u == AT["copy rows"] and 0 <= it - 1:
                        copy_rows(it - 1)
                    if u == AT["max rows 1"] and 0 <= it < B:
                        max_rows(it, 1)
                    if -1 <= it < 2 and u % 3 == 2:
                        pad_slots(5 * (it + 1) + u // 3)
                    if u == AT["max rows 0"] and 0 <= it + 1 < B:
                        max_rows(it + 1, 0)
                    if u == (AT["LG of the last"] + 1 if it == B - 1 else AT["gate exps"]) and 0 <= it - 1:
                        router_exponentials(it - 1)

            def silu(t, u):
                act.wait_ge(h_ready, t + 1)
                if later(t, 2):
                    act.wait_ge(hm_ready, t - 1)
                act.activation(SG[:, u, :], bank[2 + 2 * u][:, 0:FF], ACT.Silu).then_inc(sg_ready, 1)

            def hidden_copy(t, u):
                act.wait_ge(ht_ready, t + 1)
                if later(t, 2):
                    act.wait_ge(y_ready, t - 1)
                act.activation(HT[:, u].rearrange("p c t -> p (c t)"), bank[1][:, 0:FF], ACT.Copy).then_inc(hte_ready, 1)

            def step(t, u):
                hidden_copy(t - 1, 1 - u)
                silu(t, u)

            silu(0, 0)
            evacuate("X2", B - 1)
            copy_rows(B - 1)
            hidden_copy(0, 0)
            router_exponentials(B - 1)
            silu(1, 1)
            for t in range(2, PEELED):
                step(t, t % 2)
            act.wait_ge(table_ready, 1)
            pairs = act.value_load(npairs[0:1, 0:1], min_val=8, max_val=MAXPAIR)
            last = act.value_load(npairs[0:1, 1:2], min_val=14, max_val=2 * MAXPAIR - 2) + 1
            with act.Fori(0, pairs - PEELED // 2) as i:
                for u in range(2):
                    step(2 * i + PEELED + u, u)
            hidden_copy(last, 1)

        @block.tensor
        def _(pe):
            def take_bank(kind, n):
                k = MISC_NO[kind, n]
                if k >= 2:
                    before_kind, m = MISC_ORDER[k - 2]
                    count = {"LG": TB * (m + 1), "CNT": 1}.get(before_kind, m + 1)
                    pe.wait_ge(EVACUATED[before_kind], count)
                return MISC[k % 2]

            def transposes(src, kind, n):
                dst = take_bank(kind, n)
                for k in range(KC):
                    for t in range(TB):
                        ins = pe.transpose(dst[:, k * S + t * P:k * S + (t + 1) * P], src(t, k), ident[:])
                ins.then_inc(misc_ready, 1)

            def misc(kind, n):
                q = n % 2
                if kind == "CT":
                    pe.wait_ge(c_in[n], 16)
                    transposes(lambda t, k: C[:, TB * (n % 3) + t, k * P:(k + 1) * P], kind, n)
                elif kind == "XT":
                    pe.wait_ge(xn_ready, TB * (n + 1))
                    transposes(lambda t, k: XN[:, q, t, k * P:(k + 1) * P], kind, n)
                elif kind in ("K", "Q"):
                    w, src, ready = (wk, CTt, ct_ready) if kind == "K" else (wq, XTt, xt_ready)
                    pe.wait_ge(ready, n + 1)
                    if n == 0 and kind == "K":
                        pe.wait_ge(wkv_in, 48)
                    if n == 0 and kind == "Q":
                        pe.wait_ge(wq_in, 48)
                    dst = take_bank(kind, n)
                    for c in range(KC):
                        for k in range(KC):
                            ins = pe.matmul(dst[:, c * S:(c + 1) * S], w[:, k, c * P:(c + 1) * P], src[:, q, k, :],
                                            start=k == 0, stop=k == KC - 1)
                    ins.then_inc(misc_ready, 1)
                elif kind == "V":
                    dst = take_bank(kind, n)
                    for t in range(TB):
                        for k in range(KC):
                            ins = pe.matmul(dst[:, t * D:(t + 1) * D], CTt[:, q, k, t * P:(t + 1) * P], wv[:, k, :],
                                            start=k == 0, stop=k == KC - 1)
                    ins.then_inc(misc_ready, 1)
                elif kind in ("NM0", "NM1"):
                    half = int(kind[2])
                    pe.wait_ge(neg_split[half], n + 1)
                    if n == 0:
                        pe.wait_ge(dve_const, DVE_CONSTS)
                    dst = take_bank(kind, n)
                    for t in range(TB):
                        ins = pe.transpose(dst[0:24, t * P // 2:(t + 1) * P // 2].bitcast(BF16),
                                           NMS[:, half, t].rearrange("p j h -> p (j h)"), identb[:])
                    ins.then_inc(misc_ready, 1)
                elif kind == "BO":
                    pe.wait_ge(bvm_ready, 2)
                    pe.wait_ge(wrest_in, 272)
                    dst = take_bank(kind, n)
                    for g in range(2):
                        ins = pe.matmul(dst[:, 0:D], bvm[:, g, :], wo[:, g, :], start=g == 0, stop=g == 1)
                    ins.then_inc(misc_ready, 1)
                elif kind == "WO":
                    pe.wait_ge(norm_done, n + 1)
                    if n == 0:
                        pe.wait_ge(wrest_in, 272)
                    dst = take_bank(kind, n)
                    for t in range(TB):
                        for g in range(2):
                            ins = pe.matmul(dst[:, t * D:(t + 1) * D], ON[:, g * S + t * P:g * S + (t + 1) * P], wo[:, g, :],
                                            start=g == 0, stop=g == 1)
                    ins.then_inc(misc_ready, 1)
                elif kind == "X2":
                    pe.wait_ge(rows_ready, TB * (n + 1))
                    transposes(lambda t, k: R[:, q, t, 0, k * P:(k + 1) * P], kind, n)
                elif kind == "LG":
                    pe.wait_ge(x2t_ready, n + 1)
                    dst = take_bank(kind, n)
                    for t in range(TB):
                        for k in range(KC):
                            ins = pe.matmul(dst[:, t * E:(t + 1) * E], X2T[:, k, t * P:(t + 1) * P], wg[:, k, :],
                                            start=k == 0, stop=k == KC - 1)
                    ins.then_inc(misc_ready, 1)
                elif kind == "CNT":
                    pe.wait_ge(chosen_ready, 2 * n)
                    dst = take_bank(kind, n)
                    pe.matmul(dst[:, 0:E], onesb[:], chosen[:, n, 0, :], start=True, stop=True).then_inc(misc_ready, 1)
                elif kind == "PF":
                    pe.wait_ge(chosen_ready, 2 * n + 1)
                    dst = take_bank(kind, n)
                    pe.matmul(dst[:, 0:TB * E], beforeb[:], sel[:, q].rearrange("p t e -> p (t e)"), start=True, stop=False)
                    pe.matmul(dst[:, 0:TB * E], onesb[:], chosen[:, n].rearrange("p t e -> p (t e)"),
                              start=False, stop=True).then_inc(misc_ready, 1)

            def row_max_logits(n, u):
                m = UNITS * n + u
                hp, t = u // 2, u % 2
                if u == 0:
                    pe.wait_ge(kq_in[n % 3], KQ_LOADS * 16 * (n // 3 + 1))
                if m >= 2:
                    pe.wait_ge(mx_reduced, m - 1)
                for i in range(2):
                    h = 2 * hp + i
                    ins = pe.matmul(MXB[m % 2][:, i * S:(i + 1) * S], QS[0:R_MAX, n % 3, h, t * P:(t + 1) * P],
                                    KS[0:R_MAX, n % 3, h, :], start=True, stop=True)
                ins.then_inc(mx_ready, 1)

            def logits(n, u):
                s = UNITS * n + u
                hp, c = u // 2, u % 2
                if u % 8 == 0:
                    pe.wait_ge(nm_in[u // 8], 48 * (n + 1))
                if s >= 2:
                    pe.wait_ge(exp_done, s - 1)
                for i in range(2):
                    h = 2 * hp + i
                    ins = pe.matmul(STB[s % 2][:, i * S:(i + 1) * S], KS[0:R_END, n % 3, h, c * P:(c + 1) * P],
                                    QS[0:R_END, n % 3, h, :], start=True, stop=True)
                ins.then_inc(st_ready, 1)

            def values(n, u):
                s = UNITS * n + u
                hp, c = u // 2, u % 2
                pe.wait_ge(exp_done, s + 1)
                if u == 0:
                    pe.wait_ge(v_ready, n + 1)
                    pe.wait_ge(va_ones, 1)
                if u % 8 == 0 and n >= 1:
                    pe.wait_ge(av_taken, 2 * (n - 1) + u // 8 + 1)
                for i in range(2):
                    h = 2 * hp + i
                    g, j = h // 4, h % 4
                    ins = pe.matmul(AVB[g // 2][32 * j:32 * j + 32, (g % 2) * S:(g % 2 + 1) * S],
                                    VA[:, n % 2, c, h, :], PR[:, s % NPROB, i * S:(i + 1) * S],
                                    start=c == 0, stop=c == 1)
                ins.then_inc(av_done, 1)

            pe.wait_ge(const_step, CONST_IDENT)
            for it in ITERATIONS[:-1]:
                for u in range(UNITS):
                    if 0 <= it + 1 < B:
                        row_max_logits(it + 1, u)
                    if 0 <= it < B:
                        logits(it, u)
                    if u >= AT["values"] and 0 <= it < B:
                        values(it, u - AT["values"])
                    if u < AT["values"] and 0 <= it - 1:
                        values(it - 1, UNITS - AT["values"] + u)
                    for kind, n in misc_at(it, u):
                        misc(kind, n)

            def turn_rows(t, u):
                pe.wait_ge(xg_in[u], (t - u) * 8 + 16)
                if later(t, 1):
                    pe.wait_ge(txe_ready, t)
                for k in range(KC):
                    ins = pe.transpose(bank[0][:, k * P:(k + 1) * P], XG[:, u, k * P:(k + 1) * P], ident[:])
                ins.then_inc(tx_ready, 1)

            up_at = pe.alloc_register("up_at")
            down_at = [pe.alloc_register("down_at0"), pe.alloc_register("down_at1")]

            def at(register, largest):
                return pe.snap(register, min_val=0, max_val=largest)

            def load_up_at(t):
                pe.reg_load(up_at, table[0:1, 1, bass.ds(t, 1)])

            def load_down_at(t, u):
                pe.reg_load(down_at[u], table[0:1, 2, bass.ds(t, 1)])

            def hidden(t, u):
                off = at(up_at, (E - 1) * KC * 2 * FF)
                pe.wait_ge(txe_ready, t + 1)
                if later(t, 2):
                    pe.wait_ge(hm_ready, t - 1)
                for g in range(2):
                    if g == 1 and later(t, 2):
                        pe.wait_ge(ys_ready, t - 1)
                    for k in range(KC):
                        ins = pe.matmul(bank[2 + 2 * u + g][:, 0:FF], XTG[:, u, k, :],
                                        wf[:, bass.ds(off + (k * 2 + g) * FF, FF)],
                                        start=k == 0, stop=k == KC - 1)
                ins.then_inc(h_ready, 1)
                load_up_at(t + 1)
                load_down_at(t, u)

            def turn_hidden(t, u):
                pe.wait_ge(hm_ready, t + 1)
                if later(t, 1):
                    pe.wait_ge(hte_ready, t)
                for c in range(FC):
                    ins = pe.transpose(bank[1][:, c * P:(c + 1) * P], HM[:, u, c * P:(c + 1) * P], ident[:])
                ins.then_inc(ht_ready, 1)

            def down(t, u):
                off = at(down_at[u], (E - 1) * FC * D)
                pe.wait_ge(hte_ready, t + 1)
                for c in range(FC):
                    ins = pe.matmul(bank[3 + 2 * u][:, 0:D], HT[:, u, c, :], wp[:, bass.ds(off + c * D, D)],
                                    start=c == 0, stop=c == FC - 1)
                ins.then_inc(y_ready, 1)

            def step(t, u):
                turn_hidden(t - 1, 1 - u)
                hidden(t, u)
                turn_rows(t + 1, 1 - u)
                down(t - 1, 1 - u)

            pe.wait_ge(mx_reduced, UNITS * B)
            turn_rows(0, 0)
            for u in range(UNITS - AT["values"], UNITS):
                values(B - 1, u)
            misc("PF", B - 2)
            misc("WO", B - 1)
            pe.wait_ge(ahead_ready, 1)
            pe.wait_ge(we_in, 32 * E)
            pe.wait_ge(exp_done, UNITS * B)
            load_up_at(0)
            hidden(0, 0)
            pe.wait_ge(av_taken, 2 * B)
            turn_rows(1, 1)
            misc("X2", B - 1)
            turn_hidden(0, 0)
            misc("LG", B - 1)
            hidden(1, 1)
            turn_rows(2, 0)
            down(0, 0)
            turn_hidden(1, 1)
            misc("PF", B - 1)
            misc("CNT", B)
            hidden(2, 0)
            turn_rows(3, 1)
            down(1, 1)
            for t in range(3, PEELED):
                step(t, t % 2)
            pe.wait_ge(table_ready, 1)
            pairs = pe.value_load(npairs[0:1, 0:1], min_val=8, max_val=MAXPAIR)
            last = pe.value_load(npairs[0:1, 1:2], min_val=14, max_val=2 * MAXPAIR - 2) + 1
            with pe.Fori(0, pairs - PEELED // 2) as i:
                for u in range(2):
                    step(2 * i + PEELED + u, u)
            turn_hidden(last, 1)
            down(last, 1)

        @block.vector
        def _(dve):
            def link(ins):
                link.n += 1
                ins.then_inc(dve_step, 1)
                dve.wait_ge(dve_step, link.n)
            link.n = 0

            def stats(n, src, bn, mv, out_sem, read_sem):
                q = n % 2
                if n >= 2:
                    dve.wait_ge(read_sem, TB * (n - 1))
                if n >= 1:
                    dve.wait_ge(out_sem, TB * n)
                for t in range(TB):
                    link(dve.bn_stats(bn[:, t, :], src[:, TB * n + t, :]))
                for t in range(TB):
                    dve.bn_aggr(mv[:, q, t, :], bn[:, t, :]).then_inc(out_sem, 1)

            def stats1_of(n):
                dve.wait_ge(x_in[n], 16)
                stats(n, X, bn1, mv1, stats1, xn_ready)

            def bias_columns():
                dve.wait_ge(wrest_in, 272)
                for g in range(2):
                    dve.tensor_scalar(bvm[:, g, :], ones[:], bvc[:, g:g + 1], None, ALU.mult).then_inc(bvm_ready, 1)

            stats1_of(0)
            normalize1(dve, 0)
            dve.memset(VA[:, :, :, :, DH:32], 1.0).then_inc(va_ones, 1)
            dve.memset(chosen[:, 0, 0, :], 0.0).then_inc(dve_const, 1)
            dve.wait_ge(mask_in, 16)
            link(dve.tensor_scalar(mres[:], maskrow[:], MASK_BIG, None, ALU.mult))
            link(dve.tensor_copy(mparts[:, 0, :], mres[:]))
            link(dve.tensor_tensor(mres2[:], mres[:], mparts[:, 0, :], ALU.subtract))
            link(dve.tensor_copy(mparts[:, 1, :], mres2[:]))
            dve.tensor_tensor(mparts[:, 2, :], mres2[:], mparts[:, 1, :], ALU.subtract).then_inc(mask_split, 1)
            dve.wait_ge(wq_in, 48)
            dve.tensor_scalar(bq4[:], bqc[:], 0.25, None, ALU.mult).then_inc(dve_const, 1)
            dve.wait_ge(const_step, CONST_ALL)
            dve.tensor_copy(identb[:], ident[:]).then_inc(dve_const, 1)
            dve.tensor_copy(beforeb[:], before[:]).then_inc(dve_const, 1)
            dve.tensor_copy(onesb[:], ones[:]).then_inc(dve_const, 1)
            dve.tensor_copy(expert_no[:], iota_i[:, 0:E]).then_inc(dve_const, 1)
            dve.tensor_copy(blk_lim[:].rearrange("p a b -> p (a b)"), iota_i[:, 8:72]).then_inc(dve_const, 1)
            dve.tensor_scalar(tri[:].rearrange("p a b -> p (a b)"), iota_i[:, 72:136], 0.0, None, ALU.is_ge).then_inc(dve_const, 1)
            dve.tensor_copy(blk_no[:], iota_i[:, 136:136 + RESTBLK]).then_inc(dve_const, 1)
            dve.tensor_copy(pair_lim[:], iota_i[:, 192:192 + RESTBLK // 2]).then_inc(dve_const, 1)
            dve.wait_ge(dve_const, DVE_CONSTS)
            dve.wait_ge(mask_split, 1)

            def reduce_max(n, u):
                m = UNITS * n + u
                hp, t = u // 2, u % 2
                dve.wait_ge(mx_ready, m + 1)
                dve.tensor_reduce(NEG[:, n % 2, t, 2 * hp:2 * hp + 2],
                                  MXB[m % 2][:].rearrange("p (i s) -> p i s", i=2), AX.X, ALU.max,
                                  negate=True).then_inc(mx_reduced, 1)

            def split_max(n, half):
                neg = NEG[:, n % 2, :, 8 * half:8 * half + 8]
                dve.wait_ge(mx_reduced, UNITS * n + 8 * (half + 1))
                if n >= 1:
                    wait_misc(dve, f"NM{half}", n - 1)
                if n >= 1 or half == 1:
                    dve.wait_ge(neg_split[1 - half], n + half)
                link(dve.tensor_copy(NMS[:, half, :, 0, :], neg))
                link(dve.tensor_tensor(NR[:], neg, NMS[:, half, :, 0, :], ALU.subtract))
                link(dve.tensor_copy(NMS[:, half, :, 1, :], NR[:]))
                dve.tensor_tensor(NMS[:, half, :, 2, :], NR[:], NMS[:, half, :, 1, :], ALU.subtract).then_inc(neg_split[half], 1)

            def normalize_product(n, i):
                dve.wait_ge(av_done, UNITS * n + 8 * (i + 1))
                dve.transpose(AVT[:].rearrange("p b c -> p (b c)"), AVB[i][:]).then_inc(av_taken, 1)
                dve.wait_ge(av_taken, 2 * n + i + 1)
                link(dve.reciprocal(RSUM[:], AVT[:, :, DH]))
                link(dve.tensor_tensor(AVN[:, :, i, :], AVT[:, :, 0:DH],
                                       RSUM[:].unsqueeze(2).broadcast_to([P, 16, DH]), ALU.mult))
                if i == 1:
                    if n >= 1:
                        wait_misc(dve, "WO", n - 1)
                    dve.transpose(ON[:], AVN[:].rearrange("p b i d -> p (b i d)")).then_inc(norm_done, 1)
                    dve.wait_ge(norm_done, n + 1)

            def normalize2(n):
                q = n % 2
                dve.wait_ge(rs2_ready, n + 1)
                if n >= 2:
                    dve.wait_ge(scattered[q], 16 * TB * TOPK * (n // 2))
                for t in range(TB):
                    dve.tensor_scalar(R[:, q, t, 0, 0:D], X[:, TB * n + t, :], mv2[:, q, t, 0:1], rs2[:, q, t:t + 1],
                                      ALU.subtract, ALU.mult).then_inc(rows_ready, 1)

            def total_bias():
                wait_misc(dve, "BO", 0)
                dve.wait_ge(wq_in, 48)
                dve.tensor_tensor(bob[:], misc_bank("BO", 0)[:, 0:D], bob[:], ALU.add).then_inc(bias_ready, 1)

            def residual(n):
                wait_misc(dve, "WO", n)
                dve.wait_ge(xb_ready, n + 1)
                xs = X[:, TB * n:TB * (n + 1), :].rearrange("p t d -> p (t d)")
                dve.tensor_tensor(xs, misc_bank("WO", n)[:], xs, ALU.add).then_inc(xmid_ready, 1)
                dve.wait_ge(xmid_ready, n + 1)
                stats(n, X, bn2, mv2, stats2, rows_ready)

            def route_choice(n):
                q = n % 2
                wait_misc(dve, "LG", n)
                if n >= 1:
                    dve.wait_ge(ex_ready, n)
                    dve.wait_ge(pos_read, n)
                    dve.wait_ge(slot_ready, n)
                scores = misc_bank("LG", n)[:, 0:TB * E].rearrange("p (t e) -> p t e", e=E)
                for t in range(TB):
                    link(dve.max(top[:, t, :], scores[:, t, :]))
                dve.tensor_tensor(ls[:], top[:], top[:, :, 0:1].broadcast_to([P, TB, E]), ALU.subtract).then_inc(ls_ready, 1)
                for t in range(TB):
                    dve.max_index(topi[:, t, :], top[:, t, :], scores[:, t, :]).then_inc(lg_ready, 1)
                dve.wait_ge(lg_ready, TB * (n + 1))
                link(dve.tensor_copy(topf[:], topi[:, :, 0:TOPK]))
                link(dve.tensor_tensor(oh[:], topf[:].unsqueeze(3).broadcast_to([P, TB, TOPK, E]),
                                       expert_no[:].unsqueeze(1).unsqueeze(1).broadcast_to([P, TB, TOPK, E]), ALU.is_equal))
                if n >= 2:
                    wait_misc(dve, "PF", n - 2)
                dve.tensor_tensor(sel[:, q], oh[:, :, 0, :], oh[:, :, 1, :], ALU.add).then_inc(sel_ready, 1)
                dve.wait_ge(sel_ready, n + 1)
                dve.tensor_tensor(chosen[:, n, 1, :], chosen[:, n, 0, :], sel[:, q, 0, :], ALU.add).then_inc(chosen_ready, 1)
                dve.wait_ge(chosen_ready, 2 * n + 1)
                dve.tensor_tensor(chosen[:, n + 1, 0, :], chosen[:, n, 1, :], sel[:, q, 1, :], ALU.add).then_inc(chosen_ready, 1)

            def route_gates(n):
                q = n % 2
                dve.wait_ge(ex_ready, n + 1)
                if n >= 1:
                    dve.wait_ge(gates_ready, n)
                link(dve.tensor_reduce(sm[:], ex[:], AX.X, ALU.add))
                link(dve.reciprocal(rsm[:], sm[:]))
                if n >= 2:
                    dve.wait_ge(scattered[q], 16 * TB * TOPK * (n // 2))
                dve.tensor_tensor(R[:, q, :, :, D], ex[:, :, 0:TOPK], rsm[:].unsqueeze(2).broadcast_to([P, TB, TOPK]),
                                  ALU.mult).then_inc(gates_ready, 1)

            def route_slots(n):
                q = n % 2
                wait_misc(dve, "PF", n)
                earlier = misc_bank("PF", n)[:, 0:TB * E].rearrange("p (t e) -> p t e", e=E)
                dve.tensor_tensor(ohp[:], earlier.unsqueeze(2).broadcast_to([P, TB, TOPK, E]), oh[:], ALU.mult).then_inc(pos_read, 1)
                dve.wait_ge(pos_read, n + 1)
                link(dve.tensor_reduce(pos[:], ohp[:], AX.X, ALU.add))
                link(dve.tensor_scalar(lost[:], pos[:], float(CAP), float(SLOT_LOST), ALU.is_ge, ALU.mult))
                link(dve.scalar_tensor_tensor(out=slotf[:], in0=topf[:], scalar=float(CAP), in1=pos[:],
                                              op0=ALU.mult, op1=ALU.add))
                dve.tensor_tensor(slot[:, q], slotf[:], lost[:], ALU.add).then_inc(slot_ready, 1)

            def running(dst, counts):
                link(dve.tensor_tensor(cum8[:], tri[:], counts.unsqueeze(1).broadcast_to([P, E, E]), ALU.mult))
                link(dve.tensor_reduce(dst, cum8[:], AX.X, ALU.add))

            def blocks_table(incl, weight, first, n, extra, done):
                b = blk_no[:, 0:n]
                link(dve.tensor_tensor(le[:, 0:n], incl.unsqueeze(1).broadcast_to([P, n, E]),
                                       b.unsqueeze(2).broadcast_to([P, n, E]), ALU.is_le))
                link(dve.tensor_reduce(bexp[:, 0:n], le[:, 0:n], AX.X, ALU.add))
                link(dve.tensor_tensor(leb[:, 0:n], le[:, 0:n], weight.unsqueeze(1).broadcast_to([P, n, E]), ALU.mult))
                link(dve.tensor_reduce(bex[:, 0:n], leb[:, 0:n], AX.X, ALU.add))
                link(dve.scalar_tensor_tensor(out=btmp[:, 0:n], in0=bexp[:, 0:n], scalar=float(CAP // P), in1=b,
                                              op0=ALU.mult, op1=ALU.add))
                link(dve.tensor_tensor(btmp2[:, 0:n], btmp[:, 0:n], bex[:, 0:n], ALU.subtract))
                if extra is not None:
                    link(dve.tensor_scalar(btmp[:, 0:n], btmp2[:, 0:n], extra, None, ALU.add))
                at = (btmp2 if extra is None else btmp)[:, 0:n]
                link(dve.tensor_scalar(bcl[:, 0:n], bexp[:, 0:n], float(E - 1), None, ALU.min))
                link(dve.tensor_scalar(table[:, 0, first:first + n], at, float(P), None, ALU.mult))
                link(dve.tensor_scalar(table[:, 1, first:first + n], bcl[:, 0:n], float(KC * 2 * FF), None, ALU.mult))
                dve.tensor_scalar(table[:, 2, first:first + n], bcl[:, 0:n], float(FC * D), None, ALU.mult).then_inc(done, 1)

            def ahead_table():
                link(dve.memset(taken[:], 0.0))
                wait_misc(dve, "CNT", KNOWN)
                dve.tensor_scalar(cnt[:], misc_bank("CNT", KNOWN)[:, 0:E], float(CAP), float(1 - P), ALU.min, ALU.add).then_inc(cnt_read, 1)
                dve.wait_ge(cnt_read, 1)
                link(dve.tensor_tensor(cmp8[:], cnt[:].unsqueeze(2).broadcast_to([P, E, E]), blk_lim[:], ALU.is_gt))
                link(dve.tensor_reduce(full[:], cmp8[:], AX.X, ALU.add))
                running(incl[:], full[:])
                link(dve.tensor_tensor(before8[:], incl[:], full[:], ALU.subtract))
                link(dve.tensor_scalar(taken_incl[:], incl[:], float(AHEAD), None, ALU.min))
                link(dve.tensor_scalar(taken_excl[:], before8[:], float(AHEAD), None, ALU.min))
                link(dve.tensor_tensor(taken[:, 0:E], taken_incl[:], taken_excl[:], ALU.subtract))
                blocks_table(taken_incl[:], taken[:, 0:E], 0, AHEAD, None, ahead_ready)

            def rest_counts():
                wait_misc(dve, "CNT", B)
                link(dve.tensor_scalar(cnt[:], misc_bank("CNT", B)[:, 0:E], float(CAP), None, ALU.min))
                link(dve.tensor_tensor(cmp8[:], cnt[:].unsqueeze(2).broadcast_to([P, E, E]), blk_lim[:], ALU.is_gt))
                link(dve.tensor_reduce(nblk[:], cmp8[:], AX.X, ALU.add))
                link(dve.tensor_tensor(full[:], nblk[:], taken[:, 0:E], ALU.subtract))
                running(incl[:], full[:])
                link(dve.tensor_tensor(more[:], taken[:, 1:E + 1], taken[:, 0:E], ALU.subtract))
                link(dve.tensor_tensor(weight8[:], full[:], more[:], ALU.subtract))

            def rest_table():
                blocks_table(incl[:], weight8[:], AHEAD, RESTBLK, taken[:, 0:1], rest_ready)

            def rest_pairs():
                dve.wait_ge(rest_ready, 1)
                link(dve.tensor_scalar(pcmp[:], pair_lim[:], incl[:, E - 1:E], None, ALU.is_lt))
                link(dve.tensor_reduce(pcnt[:], pcmp[:], AX.X, ALU.add))
                link(dve.tensor_scalar(npairs[:, 0:1], pcnt[:], float(AHEAD // 2), None, ALU.add))
                dve.tensor_scalar(npairs[:, 1:2], pcnt[:], 2.0, float(AHEAD - 2), ALU.mult, ALU.add).then_inc(table_ready, 1)
                dve.wait_ge(table_ready, 1)

            for it in ITERATIONS[:-1]:
                if it == -1:
                    split(dve, 0)
                    split(dve, 1)
                for u in range(UNITS):
                    if 0 <= it + 1 < B:
                        reduce_max(it + 1, u)
                    if u == AT["split 1"] and 0 <= it < B:
                        split_max(it, 1)
                    if u == AT["slots"] and 0 <= it - 2:
                        route_slots(it - 2)
                    if u == AT["stats1"] and 1 <= it + 3 < B:
                        stats1_of(it + 3)
                    if u == AT["product 1"] and 0 <= it - 1:
                        normalize_product(it - 1, 1)
                    if u == AT["normalize2"] and 0 <= it - 1:
                        normalize2(it - 1)
                    if u == AT["residual"] and 0 <= it - 1:
                        residual(it - 1)
                    if u == 0 and it == 0:
                        bias_columns()
                    if u == AT["BO"] and it == 0:
                        total_bias()
                    if u == AT["split 0"] and 0 <= it + 1 < B:
                        split_max(it + 1, 0)
                    if u == AT["product 0"] and 0 <= it < B:
                        normalize_product(it, 0)
                    if u == AT["LG of the last" if it == B - 1 else "choice"] and 0 <= it - 1:
                        route_choice(it - 1)
                    if u == (AT["LG of the last"] + 1 if it == B - 1 else AT["gates"]) and 0 <= it - 1:
                        route_gates(it - 1)
                    if u == AT["table"] and it == B - 1:
                        ahead_table()

            def rows_copy(t, u):
                dve.wait_ge(tx_ready, t + 1)
                if later(t, 2):
                    dve.wait_ge(h_ready, t - 1)
                dve.tensor_copy(XTG[:, u].rearrange("p k t -> p (k t)"), bank[0][:, 0:D]).then_inc(txe_ready, 1)

            def gates_copy(t, u):
                dve.wait_ge(xg_in[u], (t - u) * 8 + 16)
                if later(t, 2):
                    dve.wait_ge(added, (t - 1) * 16)
                dve.tensor_copy(GW[:, u, :], XG[:, u, D:D + 1]).then_inc(gw_ready, 1)
                dve.tensor_copy(GI[u][:], XG[:, u, D + 1:D + 2].bitcast(U32)).then_inc(gi_ready, 1)

            def gated(t, u):
                dve.wait_ge(sg_ready, t + 1)
                if later(t, 2):
                    dve.wait_ge(ht_ready, t - 1)
                dve.tensor_tensor(HM[:, u, :], bank[3 + 2 * u][:, 0:FF], SG[:, u, :], ALU.mult).then_inc(hm_ready, 1)

            def weigh(t, u):
                dve.wait_ge(y_ready, t + 1)
                dve.wait_ge(gw_ready, t + 1)
                if later(t, 2):
                    dve.wait_ge(added, (t - 1) * 16)
                dve.tensor_scalar(Y[:, u, :], bank[3 + 2 * u][:, 0:D], GW[:, u, 0:1], None, ALU.mult).then_inc(ys_ready, 1)

            def step(t, u):
                gates_copy(t, u)
                gated(t, u)
                rows_copy(t + 1, 1 - u)
                weigh(t - 1, 1 - u)

            rows_copy(0, 0)
            gates_copy(0, 0)
            normalize_product(B - 1, 1)
            route_slots(B - 2)
            residual(B - 1)
            normalize2(B - 1)
            rows_copy(1, 1)
            gated(0, 0)
            route_choice(B - 1)
            route_gates(B - 1)
            step(1, 1)
            route_slots(B - 1)
            step(2, 0)
            rest_counts()
            step(3, 1)
            rest_table()
            step(4, 0)
            rest_pairs()
            for t in range(5, PEELED):
                step(t, t % 2)
            pairs = dve.value_load(npairs[0:1, 0:1], min_val=8, max_val=MAXPAIR)
            last = dve.value_load(npairs[0:1, 1:2], min_val=14, max_val=2 * MAXPAIR - 2) + 1
            with dve.Fori(0, pairs - PEELED // 2) as i:
                for u in range(2):
                    step(2 * i + PEELED + u, u)
            weigh(last, 1)


INPUTS = ["x", "ctx_1024", "mask_Bx1x1xS2_fk0", "L0_xattn_Wq", "L0_xattn_bq", "L0_xattn_Wk", "L0_xattn_bk",
          "L0_xattn_Wv", "L0_xattn_bv", "L0_xattn_Wo", "L0_xattn_bo", "L0_ffn_w_gate", "L0_ffn_c_fc", "L0_ffn_c_proj"]


def kernel(**inputs):
    import concourse.bacc as bacc
    from concourse.bass_utils import run_bass_kernel_spmd

    nc = bacc.Bacc("TRN2", target_bir_lowering=False, num_devices=1)
    arrays, args = {}, []
    for name in INPUTS:
        a = np.ascontiguousarray(inputs[name])
        arrays[f"in_{name}"] = a
        args.append(nc.dram_tensor(f"in_{name}", a.shape, mybir.dt.from_np(a.dtype), kind="ExternalInput").ap())
    out = nc.dram_tensor("out_0", (B, S, D), F32, kind="ExternalOutput").ap()
    program(nc, *args, out)
    r = run_bass_kernel_spmd(nc, [arrays], core_ids=[0])
    return r.results[0]["out_0"]
```
